# Optimizing a Trainium2 kernel written in Bass

```python
import numpy as np
import jax
import jax.numpy as jnp

def _softmax(x, axis=-1):
    return jax.nn.softmax(x, axis=axis)

def _gelu(x):
    return jax.nn.gelu(x, approximate=True)

def _silu(x):
    return jax.nn.silu(x)

def _sigmoid(x):
    return jax.nn.sigmoid(x)

def _layernorm(x, axis=-1, eps=1e-05):
    m = jnp.mean(x, axis=axis, keepdims=True)
    v = jnp.var(x, axis=axis, keepdims=True)
    return (x - m) / jnp.sqrt(v + eps)

def _scatter_add(tgt, idx, src, axis=0):
    return tgt.at[idx].add(src)

def _segment_sum(src, seg, n):
    return jax.ops.segment_sum(src, seg, n)
kernel_name = 'mk_gnn_resnorm_d4_gnn_r32_5a6bf7'

def setup_inputs(seed: int=0):
    np.random.seed(seed)
    _w = jnp.asarray

    def _rec_inputs():
        import jax
        import jax.numpy as jnp
        _gk = jax.random.key(seed)
        x = -8.776e-05 + 1 * jax.random.normal(jax.random.fold_in(_gk, 1), (3125, 128), jnp.float32)
        src = jax.random.randint(jax.random.fold_in(_gk, 2), (100000,), 0, 3125, jnp.int32)
        dst = jnp.minimum((3125 * jax.random.uniform(jax.random.fold_in(_gk, 3), (100000,)) ** 2.0).astype(jnp.int32), 99999)
        _o = jnp.argsort(dst, stable=True)
        src = src[_o]
        dst = dst[_o]
        edge_attr_64 = 0.000189758 + 1.00013 * jax.random.normal(jax.random.fold_in(_gk, 12), (100000, 64), jnp.float32)
        edge_type_32 = jax.random.randint(jax.random.fold_in(_gk, 14), (100000,), 0, 32, jnp.int32)
        edge_type_500 = jax.random.randint(jax.random.fold_in(_gk, 15), (100000,), 0, 500, jnp.int32)
        return (x, src, dst, edge_attr_64, edge_type_32, edge_type_500)
    x, src, dst, edge_attr_64, edge_type_32, edge_type_500 = _rec_inputs()

    def _L0_gnn_setup():
        import jax, jax.numpy as jnp
        import numpy as np
        ALPHA = 0.2
        key = jax.random.key(seed)
        k1, k2, k3, k4, k5, k6 = jax.random.split(key, 6)
        N, E, D, R = (1250, 20000, 128, 500)
        ent_embedding = jax.random.normal(k1, (N, D), dtype=jnp.float32)
        rel_embedding = jax.random.normal(k2, (R, D), dtype=jnp.float32)
        W_e1 = jax.random.normal(k3, (D, 3 * D), dtype=jnp.float32) * (1.414 / np.sqrt(2.0 * D))
        W_e2 = jax.random.normal(k4, (1, D), dtype=jnp.float32) * (1.414 / np.sqrt(D))
        edge = jax.random.randint(k5, (2, E), 0, N, dtype=jnp.int64)
        rel = jax.random.randint(k6, (E,), 0, R, dtype=jnp.int64)
        return {'ent_embedding': ent_embedding, 'rel_embedding': rel_embedding, 'W_e1': W_e1, 'W_e2': W_e2, 'edge': edge, 'rel': rel}
    _L0_gnn_all = _L0_gnn_setup()
    _L0_gnn_in = {k: v for k, v in _L0_gnn_all.items() if k in ('rel_embedding', 'W_e1', 'W_e2')}
    del _L0_gnn_all

    def _L1_gnn_setup():
        import jax, jax.numpy as jnp
        import numpy as np
        N, E, D, H, ED = (50000, 25000, 128, 8, 64)
        C = D // H

        def _ln(x, g, b, eps=1e-05):
            m = jnp.mean(x, axis=-1, keepdims=True)
            v = jnp.var(x, axis=-1, keepdims=True)
            return (x - m) * jax.lax.rsqrt(v + eps) * g + b
        key = jax.random.key(seed)
        ks = jax.random.split(key, 16)
        p = lambda k, shape: jax.random.normal(k, shape, dtype=jnp.float32) * 0.05
        return {'x': jax.random.normal(ks[0], (N, D), dtype=jnp.float32), 'edge_index': jax.random.randint(ks[1], (2, E), 0, N, dtype=jnp.int64), 'edge_attr': jax.random.normal(ks[2], (E, ED), dtype=jnp.float32), 'Wq': p(ks[3], (D, D)), 'bq': jnp.zeros((D,), jnp.float32), 'Wk': p(ks[4], (D, D)), 'bk': jnp.zeros((D,), jnp.float32), 'Wv': p(ks[5], (D, D)), 'bv': jnp.zeros((D,), jnp.float32), 'We': p(ks[6], (ED, D)), 'Wskip': p(ks[7], (D, D)), 'bskip': jnp.zeros((D,), jnp.float32), 'g1': jnp.ones((D,), jnp.float32), 'b1': jnp.zeros((D,), jnp.float32), 'g2': jnp.ones((D,), jnp.float32), 'b2': jnp.zeros((D,), jnp.float32), 'Wf1': p(ks[8], (D, 4 * D)), 'bf1': jnp.zeros((4 * D,), jnp.float32), 'Wf2': p(ks[9], (4 * D, D)), 'bf2': jnp.zeros((D,), jnp.float32)}
    _L1_gnn_all = _L1_gnn_setup()
    _L1_gnn_in = {k: v for k, v in _L1_gnn_all.items() if k in ('Wq', 'bq', 'Wk', 'bk', 'Wv', 'bv', 'We', 'Wskip', 'bskip', 'g1', 'b1', 'g2', 'b2', 'Wf1', 'bf1', 'Wf2', 'bf2')}
    del _L1_gnn_all

    def _L2_gnn_setup():
        import jax, jax.numpy as jnp
        import numpy as np
        N = 30000
        E = 30000
        DIN = 128
        DOUT = 128
        R = 32
        NUM_RULES = 100
        ACTIVE = 4
        EPS = 1e-05
        key = jax.random.key(seed)
        ks = jax.random.split(key, 10)
        x = jax.random.normal(ks[0], (N, DIN), jnp.float32)
        src = jax.random.randint(ks[1], (E,), 0, N)
        dst = jax.random.randint(ks[2], (E,), 0, N)
        edge_type = jax.random.randint(ks[3], (E,), 0, R)
        rule_ids = jax.random.randint(ks[4], (ACTIVE,), 0, NUM_RULES)
        W_r = jax.random.normal(ks[5], (R, DIN, DOUT), jnp.float32) * 0.05
        Wq_w = jax.random.normal(ks[6], (DIN, DOUT), jnp.float32) * 0.05
        Wq_b = jnp.zeros((DOUT,), jnp.float32)
        Wk_w = jax.random.normal(ks[7], (3 * DIN, DOUT), jnp.float32) * 0.05
        Wk_b = jnp.zeros((DOUT,), jnp.float32)
        rule_emb = jax.random.normal(ks[8], (NUM_RULES, DIN), jnp.float32) * 0.05
        bias = jnp.zeros((DOUT,), jnp.float32)
        ln_gamma = jnp.ones((DOUT,), jnp.float32)
        ln_beta = jnp.zeros((DOUT,), jnp.float32)
        return {'x': x, 'W_r': W_r, 'Wq_w': Wq_w, 'Wq_b': Wq_b, 'Wk_w': Wk_w, 'Wk_b': Wk_b, 'rule_emb': rule_emb, 'bias': bias, 'ln_gamma': ln_gamma, 'ln_beta': ln_beta, 'src': src, 'dst': dst, 'edge_type': edge_type, 'rule_ids': rule_ids}
    _L2_gnn_all = _L2_gnn_setup()
    _L2_gnn_in = {k: v for k, v in _L2_gnn_all.items() if k in ('W_r', 'Wq_w', 'Wq_b', 'Wk_w', 'Wk_b', 'rule_emb', 'bias', 'ln_gamma', 'ln_beta', 'rule_ids')}
    del _L2_gnn_all

    def _L3_gnn_setup():
        import jax, jax.numpy as jnp
        import numpy as np
        N_NODES = 50000
        N_EDGES = 50000
        D_FEAT = 128
        EMB = 32
        HEADS = 4
        SLOPE = 0.2

        def _gatv2_layer(x, src, dst, W_l, W_r, att, bias, n_nodes):
            H, C = att.shape
            xl = (x @ W_l).reshape(n_nodes, H, C)
            xr = (x @ W_r).reshape(n_nodes, H, C)
            msg = xl[src] + xr[dst]
            e = jnp.einsum('ehc,hc->eh', jax.nn.leaky_relu(msg, SLOPE), att)
            m = jax.ops.segment_max(e, dst, num_segments=n_nodes)
            ex = jnp.exp(e - m[dst])
            denom = jax.ops.segment_sum(ex, dst, num_segments=n_nodes)
            alpha = ex / (denom[dst] + 1e-16)
            out = jax.ops.segment_sum(alpha[:, :, None] * xl[src], dst, num_segments=n_nodes)
            return out.reshape(n_nodes, H * C) + bias
        key = jax.random.key(seed)
        ks = jax.random.split(key, 12)
        H, C = (HEADS, EMB)
        hid = H * C

        def glorot(k, shape):
            fan_in, fan_out = (shape[0], shape[-1] if len(shape) > 1 else shape[0])
            lim = jnp.sqrt(6.0 / (fan_in + fan_out)).astype(jnp.float32)
            return jax.random.uniform(k, shape, jnp.float32, -lim, lim)
        x = jax.random.normal(ks[0], (N_NODES, D_FEAT), jnp.float32)
        edge_index = jax.random.randint(ks[1], (2, N_EDGES), 0, N_NODES, jnp.int32).astype(jnp.int64)
        return {'x': x, 'edge_index': edge_index, 'W1_l': glorot(ks[2], (D_FEAT, hid)), 'W1_r': glorot(ks[3], (D_FEAT, hid)), 'att1': glorot(ks[4], (H, C)), 'b1': jnp.zeros((hid,), jnp.float32), 'W2_l': glorot(ks[5], (hid, hid)), 'W2_r': glorot(ks[6], (hid, hid)), 'att2': glorot(ks[7], (H, C)), 'b2': jnp.zeros((hid,), jnp.float32)}
    _L3_gnn_all = _L3_gnn_setup()
    _L3_gnn_in = {k: v for k, v in _L3_gnn_all.items() if k in ('W1_l', 'W1_r', 'att1', 'b1', 'W2_l', 'W2_r', 'att2', 'b2')}
    del _L3_gnn_all
    return {'x': x, 'src': src, 'dst': dst, 'edge_attr_64': edge_attr_64, 'edge_type_32': edge_type_32, 'edge_type_500': edge_type_500, 'L0_gnn_rel_embedding': _L0_gnn_in['rel_embedding'], 'L0_gnn_W_e1': _L0_gnn_in['W_e1'], 'L0_gnn_W_e2': _L0_gnn_in['W_e2'], 'L1_gnn_Wq': _L1_gnn_in['Wq'], 'L1_gnn_bq': _L1_gnn_in['bq'], 'L1_gnn_Wk': _L1_gnn_in['Wk'], 'L1_gnn_bk': _L1_gnn_in['bk'], 'L1_gnn_Wv': _L1_gnn_in['Wv'], 'L1_gnn_bv': _L1_gnn_in['bv'], 'L1_gnn_We': _L1_gnn_in['We'], 'L1_gnn_Wskip': _L1_gnn_in['Wskip'], 'L1_gnn_bskip': _L1_gnn_in['bskip'], 'L1_gnn_g1': _L1_gnn_in['g1'], 'L1_gnn_b1': _L1_gnn_in['b1'], 'L1_gnn_g2': _L1_gnn_in['g2'], 'L1_gnn_b2': _L1_gnn_in['b2'], 'L1_gnn_Wf1': _L1_gnn_in['Wf1'], 'L1_gnn_bf1': _L1_gnn_in['bf1'], 'L1_gnn_Wf2': _L1_gnn_in['Wf2'], 'L1_gnn_bf2': _L1_gnn_in['bf2'], 'L2_gnn_W_r': _L2_gnn_in['W_r'], 'L2_gnn_Wq_w': _L2_gnn_in['Wq_w'], 'L2_gnn_Wq_b': _L2_gnn_in['Wq_b'], 'L2_gnn_Wk_w': _L2_gnn_in['Wk_w'], 'L2_gnn_Wk_b': _L2_gnn_in['Wk_b'], 'L2_gnn_rule_emb': _L2_gnn_in['rule_emb'], 'L2_gnn_bias': _L2_gnn_in['bias'], 'L2_gnn_ln_gamma': _L2_gnn_in['ln_gamma'], 'L2_gnn_ln_beta': _L2_gnn_in['ln_beta'], 'L2_gnn_rule_ids': _L2_gnn_in['rule_ids'], 'L3_gnn_W1_l': _L3_gnn_in['W1_l'], 'L3_gnn_W1_r': _L3_gnn_in['W1_r'], 'L3_gnn_att1': _L3_gnn_in['att1'], 'L3_gnn_b1': _L3_gnn_in['b1'], 'L3_gnn_W2_l': _L3_gnn_in['W2_l'], 'L3_gnn_W2_r': _L3_gnn_in['W2_r'], 'L3_gnn_att2': _L3_gnn_in['att2'], 'L3_gnn_b2': _L3_gnn_in['b2']}

def reference(x, src, dst, edge_attr_64, edge_type_32, edge_type_500, L0_gnn_rel_embedding, L0_gnn_W_e1, L0_gnn_W_e2, L1_gnn_Wq, L1_gnn_bq, L1_gnn_Wk, L1_gnn_bk, L1_gnn_Wv, L1_gnn_bv, L1_gnn_We, L1_gnn_Wskip, L1_gnn_bskip, L1_gnn_g1, L1_gnn_b1, L1_gnn_g2, L1_gnn_b2, L1_gnn_Wf1, L1_gnn_bf1, L1_gnn_Wf2, L1_gnn_bf2, L2_gnn_W_r, L2_gnn_Wq_w, L2_gnn_Wq_b, L2_gnn_Wk_w, L2_gnn_Wk_b, L2_gnn_rule_emb, L2_gnn_bias, L2_gnn_ln_gamma, L2_gnn_ln_beta, L2_gnn_rule_ids, L3_gnn_W1_l, L3_gnn_W1_r, L3_gnn_att1, L3_gnn_b1, L3_gnn_W2_l, L3_gnn_W2_r, L3_gnn_att2, L3_gnn_b2):
    import jax
    import jax.numpy as jnp

    def _L0_gnn_ref(ent_embedding, rel_embedding, W_e1, W_e2, edge, rel):
        import jax, jax.numpy as jnp
        import numpy as np
        ALPHA = 0.2
        N = ent_embedding.shape[0]
        src, dst = (edge[0], edge[1])
        edge_h = jnp.concatenate([ent_embedding[src], rel_embedding[rel], ent_embedding[dst]], axis=1)
        edge_m = jnp.einsum('ef,df->ed', edge_h, W_e1)
        powers = -jax.nn.leaky_relu(edge_m @ W_e2[0], negative_slope=ALPHA)
        edge_e = jnp.exp(powers)
        e_rowsum = jax.ops.segment_sum(edge_e, src, num_segments=N)
        e_rowsum = jnp.where(e_rowsum == 0.0, 1e-12, e_rowsum)
        edge_w = edge_e[:, None] * edge_m
        h_prime = jax.ops.segment_sum(edge_w, src, num_segments=N)
        h_prime = h_prime / e_rowsum[:, None]
        return h_prime

    def _L1_gnn_ref(x, edge_index, edge_attr, Wq, bq, Wk, bk, Wv, bv, We, Wskip, bskip, g1, b1, g2, b2, Wf1, bf1, Wf2, bf2):
        import jax, jax.numpy as jnp
        import numpy as np
        N, E, D, H, ED = (50000, 25000, 128, 8, 64)
        C = D // H

        def _ln(x, g, b, eps=1e-05):
            m = jnp.mean(x, axis=-1, keepdims=True)
            v = jnp.var(x, axis=-1, keepdims=True)
            return (x - m) * jax.lax.rsqrt(v + eps) * g + b
        n = x.shape[0]
        src, dst = (edge_index[0], edge_index[1])
        q = (x @ Wq + bq).reshape(n, H, C)
        k = (x @ Wk + bk).reshape(n, H, C)
        v = (x @ Wv + bv).reshape(n, H, C)
        e = (edge_attr @ We).reshape(-1, H, C)
        k_j = k[src] + e
        v_j = v[src] + e
        logits = jnp.sum(q[dst] * k_j, axis=-1) / np.sqrt(C)
        m = jax.ops.segment_max(logits, dst, num_segments=n)
        ex = jnp.exp(logits - m[dst])
        denom = jax.ops.segment_sum(ex, dst, num_segments=n)
        alpha = ex / denom[dst]
        agg = jax.ops.segment_sum(alpha[..., None] * v_j, dst, num_segments=n)
        conv = agg.reshape(n, D) + x @ Wskip + bskip
        h = _ln(conv + x, g1, b1)
        ffn = jax.nn.gelu(h @ Wf1 + bf1, approximate=False) @ Wf2 + bf2
        return _ln(ffn + h, g2, b2)

    def _L2_gnn_ref(x, W_r, Wq_w, Wq_b, Wk_w, Wk_b, rule_emb, bias, ln_gamma, ln_beta, src, dst, edge_type, rule_ids):
        import jax, jax.numpy as jnp
        import numpy as np
        N = 30000
        E = 30000
        DIN = 128
        DOUT = 128
        R = 32
        NUM_RULES = 100
        ACTIVE = 4
        EPS = 1e-05
        n_nodes, _ = x.shape
        n_rel, _, dout = W_r.shape
        scale = 1.0 / jnp.sqrt(jnp.float32(dout))
        h_R = rule_emb[rule_ids]
        q = (x @ Wq_w + Wq_b)[dst]
        Wk1, Wk2, Wk3 = jnp.split(Wk_w, 3, axis=0)
        h_rel = W_r.mean(axis=-1)
        k_node = x @ Wk1
        k_rel = h_rel @ Wk2
        v_rule = h_R @ Wk3
        k_base = k_node[src] + k_rel[edge_type] + Wk_b
        score_base = jnp.sum(q * k_base, axis=-1)
        scores = (score_base[:, None] + q @ v_rule.T) * scale
        seg = edge_type * n_nodes + dst
        nseg = n_rel * n_nodes
        m = jax.ops.segment_max(scores, seg, num_segments=nseg)
        ex = jnp.exp(scores - m[seg])
        s = jax.ops.segment_sum(ex, seg, num_segments=nseg)
        attn = ex / s[seg]
        attn_mean = attn.mean(axis=-1)
        proj = jnp.einsum('nd,rdo->nro', x, W_r)
        msg = proj[src, edge_type] * attn_mean[:, None]
        out = jax.ops.segment_sum(msg, dst, num_segments=n_nodes) + bias
        mu = out.mean(axis=-1, keepdims=True)
        var = out.var(axis=-1, keepdims=True)
        out = (out - mu) * jax.lax.rsqrt(var + EPS) * ln_gamma + ln_beta
        return jax.nn.relu(out)

    def _L3_gnn_ref(x, edge_index, W1_l, W1_r, att1, b1, W2_l, W2_r, att2, b2):
        import jax, jax.numpy as jnp
        import numpy as np
        N_NODES = 50000
        N_EDGES = 50000
        D_FEAT = 128
        EMB = 32
        HEADS = 4
        SLOPE = 0.2

        def _gatv2_layer(x, src, dst, W_l, W_r, att, bias, n_nodes):
            H, C = att.shape
            xl = (x @ W_l).reshape(n_nodes, H, C)
            xr = (x @ W_r).reshape(n_nodes, H, C)
            msg = xl[src] + xr[dst]
            e = jnp.einsum('ehc,hc->eh', jax.nn.leaky_relu(msg, SLOPE), att)
            m = jax.ops.segment_max(e, dst, num_segments=n_nodes)
            ex = jnp.exp(e - m[dst])
            denom = jax.ops.segment_sum(ex, dst, num_segments=n_nodes)
            alpha = ex / (denom[dst] + 1e-16)
            out = jax.ops.segment_sum(alpha[:, :, None] * xl[src], dst, num_segments=n_nodes)
            return out.reshape(n_nodes, H * C) + bias
        n = x.shape[0]
        loop = jnp.arange(n, dtype=edge_index.dtype)
        src = jnp.concatenate([edge_index[0], loop])
        dst = jnp.concatenate([edge_index[1], loop])
        h = jax.nn.relu(_gatv2_layer(x, src, dst, W1_l, W1_r, att1, b1, n))
        h = jax.nn.relu(_gatv2_layer(h, src, dst, W2_l, W2_r, att2, b2, n))
        return h
    edge_index = jnp.stack([src, dst])
    x = _layernorm(x + _L0_gnn_ref(x, L0_gnn_rel_embedding, L0_gnn_W_e1, L0_gnn_W_e2, edge_index, edge_type_500), axis=-1)
    x = _layernorm(x + _L1_gnn_ref(x, edge_index, edge_attr_64, L1_gnn_Wq, L1_gnn_bq, L1_gnn_Wk, L1_gnn_bk, L1_gnn_Wv, L1_gnn_bv, L1_gnn_We, L1_gnn_Wskip, L1_gnn_bskip, L1_gnn_g1, L1_gnn_b1, L1_gnn_g2, L1_gnn_b2, L1_gnn_Wf1, L1_gnn_bf1, L1_gnn_Wf2, L1_gnn_bf2), axis=-1)
    x = _layernorm(x + _L2_gnn_ref(x, L2_gnn_W_r, L2_gnn_Wq_w, L2_gnn_Wq_b, L2_gnn_Wk_w, L2_gnn_Wk_b, L2_gnn_rule_emb, L2_gnn_bias, L2_gnn_ln_gamma, L2_gnn_ln_beta, src, dst, edge_type_32, L2_gnn_rule_ids), axis=-1)
    x = _layernorm(x + _L3_gnn_ref(x, edge_index, L3_gnn_W1_l, L3_gnn_W1_r, L3_gnn_att1, L3_gnn_b1, L3_gnn_W2_l, L3_gnn_W2_r, L3_gnn_att2, L3_gnn_b2), axis=-1)
    return x

_drawn_inputs = setup_inputs


def setup_inputs(seed=0):
    import zlib

    import numpy as np

    out = dict(_drawn_inputs(seed))
    spreads = {'L1_gnn_bq': (0.0, 0.8),
     'L1_gnn_bk': (0.0, 0.8),
     'L1_gnn_bv': (0.0, 0.1),
     'L1_gnn_bskip': (0.0, 0.1),
     'L1_gnn_g1': (1.0, 0.2),
     'L1_gnn_b1': (0.0, 0.1),
     'L1_gnn_g2': (1.0, 0.2),
     'L1_gnn_b2': (0.0, 0.1),
     'L1_gnn_bf1': (0.0, 0.1),
     'L1_gnn_bf2': (0.0, 0.1),
     'L2_gnn_Wq_b': (0.0, 0.775),
     'L2_gnn_Wk_b': (0.0, 0.8),
     'L2_gnn_bias': (0.0, 0.1),
     'L2_gnn_ln_gamma': (1.0, 0.2),
     'L2_gnn_ln_beta': (0.0, 0.1),
     'L3_gnn_b1': (0.0, 0.1),
     'L3_gnn_b2': (0.0, 0.1)}
    factors = {'L2_gnn_rule_emb': 8.0, 'L3_gnn_W1_r': 6.042, 'L3_gnn_W2_r': 8.0, 'L3_gnn_att2': 8.0}
    for name, (base, spread) in spreads.items():
        noise = np.random.default_rng([zlib.crc32(name.encode()), seed]).standard_normal(out[name].shape)
        drawn = base * np.exp(spread * noise) if base else spread * noise
        out[name] = jnp.asarray(drawn.astype(out[name].dtype))
    for name, factor in factors.items():
        out[name] = (out[name] * factor).astype(out[name].dtype)
    return out
```

```python
import concourse.bass as bass
from concourse import mybir
from contextlib import ExitStack, contextmanager

F32, BF16 = mybir.dt.float32, mybir.dt.bfloat16
I32, U32, U8 = mybir.dt.int32, mybir.dt.uint32, mybir.dt.uint8
ALU = mybir.AluOpType
ACT = mybir.ActivationFunctionType
AX = mybir.AxisListType
ENG = mybir.EngineType

P = 128
N, E, D = 3125, 100000, 128
NT = (N + P - 1) // P
NPAD = NT * P
NLAST = N - (NT - 1) * P
RELS, TYPES = 500, 32
ED = 64
ROWS = 125
ECOL, NCOL = E // ROWS, N // ROWS
ACOL = ECOL + NCOL
ALL = E + N
U = 4
C = 16
HD = 8
G = -(-(ALL // P + NT) // C)
SLOTS = G * C * P
SEQ = G * P
EG = -(-(E // P + NT) // C)
ESLOTS = EG * C * P
NIL = 4095
BIG = 1.0e30
NEG = 256.0
STEPS = C // U
W0 = 130
LQ = 164


class Count:

    def __init__(self, sem):
        self.sem, self.n = sem, 0

    def inc(self, ins, k=1):
        ins.then_inc(self.sem, k)
        self.n += k

    def wait(self, eng):
        eng.wait_ge(self.sem, self.n)

    def link(self, eng, ins):
        self.inc(ins)
        self.wait(eng)


class Marks:
    pass


class Step:

    def __init__(self, count, i, per):
        self.count, self.i, self.per, self.k = count, i, per, 0

    def inc(self, ins):
        ins.then_inc(self.count.sem, 1)
        self.k += 1

    def wait(self, eng):
        eng.wait_ge(self.count.sem, self.i * self.per + (self.count.n + self.k))

    def link(self, eng, ins):
        self.inc(ins)
        self.wait(eng)

    def end(self, turns):
        assert self.k == self.per, (self.k, self.per)
        self.count.n += turns * self.per


def bc(ap, axis, n):
    u = ap.unsqueeze(axis)
    shape = list(u.shape)
    shape[axis] = n
    return u.to_broadcast(shape)


def gnn_kernel(nc, A, out):
    ctx = ExitStack()
    with ctx:
        nc_dram = lambda name, shape, dt=F32: nc.dram_tensor("scr_" + name, shape, dt, kind="Internal")

        def sb(name, shape, dt=F32):
            return ctx.enter_context(nc.sbuf_tensor("sb_" + name, shape, dt))

        moved = [Count(ctx.enter_context(nc.semaphore(f"rows_moved{k}"))) for k in range(5)]

        class Phase:

            def __init__(self):
                self.stack, self.counts = ExitStack(), []

            def rows_moved(self, n):
                return moved[:n]

            def __call__(self, name):
                self.counts.append(Count(self.stack.enter_context(nc.semaphore(name))))
                return self.counts[-1]

            @contextmanager
            def block(self):
                with nc.Block() as block:
                    yield block
                with nc.Block() as block:
                    @block.sync
                    def _(sp):
                        for c in self.counts:
                            sp.sem_clear(c.sem)
                self.stack.close()

        d_pass = [nc_dram(f"pass{i}", [ALL, 4], I32) for i in range(2)]
        d_list = nc_dram("list", [SLOTS, 4], I32)
        d_slist = nc_dram("slist", [ESLOTS, 4], I32)
        d_dst = nc_dram("tab_dst", [NPAD, W0])
        d_rel = nc_dram("tab_rel", [RELS, W0])
        d_kv = nc_dram("tab_kv", [NPAD, 2 * D])
        d_kn = nc_dram("tab_kn", [NPAD, D])
        d_xl = nc_dram("tab_xl", [NPAD, D])
        d_proj = nc_dram("tab_proj", [NPAD * TYPES, D])
        d_spill = nc_dram("spill", [G, P, C, D])

        X = sb("x", [P, NT, D])
        ACC = sb("acc", [P, NT, W0])
        QT = sb("qt", [P, NT * LQ])
        ident = sb("ident", [P, P])
        iota = sb("iota", [P, P])
        iota16 = sb("iota16", [P, P], BF16)
        ones = sb("ones", [P, P])
        lower = sb("lower", [P, P])
        up8 = sb("up8", [P, P])
        down8 = sb("down8", [P, P])
        src_i = sb("src_i", [P, G * C], U32)
        eid_i = sb("eid_i", [P, G * C], U32)
        prj_i = sb("prj_i", [P, G * C], U32)
        dl = sb("dl", [P, G * C + U], BF16)
        dlm = sb("dlm", [P, G * C + U], BF16)
        typ = sb("typ", [P, G * C], BF16)
        bt = sb("bt", [1, G * C], I32)
        sbt = sb("sbt", [1, EG * C], I32)
        sdl = sb("sdl", [P, EG * C + U], BF16)
        cD = sb("cD", [P, SEQ + 1], U8)
        cK = sb("cK", [P, SEQ + 1], U8)
        LA = sb("la", [P, G, C, HD])
        XT = sb("xt", [P, SEQ])
        FW = sb("fw", [P, SEQ])
        TT = sb("tt", [P, SEQ])
        PS = ctx.enter_context(nc.psum_tensor("psum", [P, 8, 512], F32))

        def over(buf, at, shape, dt=F32, parts=P):
            n = 1
            for s in shape:
                n *= s
            if dt == BF16:
                v = buf[0:parts, at:at + (n + 1) // 2].bitcast(BF16)
            else:
                v = buf[0:parts, at:at + n]
                if dt != F32:
                    v = v.bitcast(dt)
            if len(shape) == 1:
                return v
            names = "abcd"[:len(shape)]
            sizes = {m: s for m, s in zip(names[1:], shape[1:])}
            return v.rearrange(f"p ({' '.join(names)}) -> p {' '.join(names)}", **sizes)

        def constants():
            sem = Phase()
            s_x, s_p, s_v = sem("c_x"), sem("c_pool"), sem("c_vec")
            with sem.block() as block:
                @block.vector
                def _(dve):
                    s_v.link(dve, dve.memset(X[:, NT - 1, :], 0.0))
                    s_v.inc(dve.memset(ones[:, :], 1.0))
                    s_v.inc(dve.memset(LA[:, :, :, :], 0.0))
                    dve.wait_ge(s_p.sem, 2)
                    s_v.inc(dve.tensor_copy(iota16[:, :], iota[:, :]))

                @block.gpsimd
                def _(pool):
                    s_p.inc(pool.memset(ident[:, :], 0.0))
                    s_p.inc(pool.iota(iota[:, :], [[1, P]], base=0, channel_multiplier=0,
                                      allow_small_or_imprecise_dtypes=True))
                    s_p.inc(pool.memset(lower[:, :], 1.0))
                    s_p.inc(pool.memset(up8[:, :], 0.0))
                    s_p.inc(pool.memset(down8[:, :], 0.0))
                    s_p.wait(pool)
                    for t, base in ((ident, 0), (up8, HD), (down8, -HD)):
                        s_p.inc(pool.affine_select(out=t[:, :], in_=t[:, :], compare_op=ALU.not_equal,
                                                   fill=1.0, base=base, pattern=[[-1, P]], channel_multiplier=1))
                    s_p.inc(pool.affine_select(out=lower[:, :], in_=lower[:, :], compare_op=ALU.is_ge,
                                               fill=0.0, base=-1, pattern=[[1, P]], channel_multiplier=-1))

                @block.sync
                def _(sp):
                    sp.wait_ge(s_v.sem, 1)
                    s_x.inc(sp.dma_start(X[:, 0:NT - 1, :],
                                         A["x"][0:(NT - 1) * P, :].rearrange("(t p) d -> p t d", p=P)), 16)
                    s_x.inc(sp.dma_start(X[0:NLAST, NT - 1, :], A["x"][(NT - 1) * P:N, :]), 16)
                    s_x.wait(sp)

        REC = lambda cols: over(XT, 0, [cols, 4], I32, ROWS)

        def records_by_dst():
            sem = Phase()
            s_l, s_v, s_p = sem("rd_l"), sem("rd_v"), sem("rd_p")
            rec = REC(ACOL)
            raw = [over(FW, i * ECOL, [ECOL], I32, ROWS) for i in range(3)]
            tmp = over(FW, 3 * ECOL, [ECOL], I32, ROWS)
            with sem.block() as block:
                @block.sync
                def _(sp):
                    for t, name in zip(raw, ("dst", "edge_type_32", "src")):
                        s_l.inc(sp.dma_start(t, A[name].rearrange("(p c) -> p c", p=ROWS)), 16)

                @block.gpsimd
                def _(pool):
                    s_p.inc(pool.iota(rec[:, 0:ECOL, 2], [[1, ECOL]], base=0, channel_multiplier=ECOL))
                    s_p.inc(pool.memset(rec[:, ECOL:ACOL, 2], 0))
                    s_p.inc(pool.iota(rec[:, ECOL:ACOL, 1], [[1, NCOL]], base=0, channel_multiplier=NCOL))
                    s_p.inc(pool.memset(rec[:, ECOL:ACOL, 3], 0))
                    s_p.inc(pool.iota(rec[:, ECOL:ACOL, 0], [[64, NCOL]], base=TYPES, channel_multiplier=64 * NCOL))

                @block.vector
                def _(dve):
                    dve.wait_ge(s_l.sem, 48)
                    s_v.inc(dve.tensor_scalar(tmp, raw[0], 64.0, None, ALU.mult))
                    s_v.inc(dve.tensor_copy(rec[:, 0:ECOL, 1], raw[2]))
                    s_v.wait(dve)
                    s_v.link(dve, dve.scalar_tensor_tensor(rec[:, 0:ECOL, 0], raw[0], 64.0, raw[1], ALU.mult, ALU.add))
                    s_v.inc(dve.scalar_tensor_tensor(rec[:, 0:ECOL, 3], raw[2], float(TYPES), raw[1], ALU.mult, ALU.add))

        def records_by_src():
            sem = Phase()
            s_l, s_v = sem("rs_l"), sem("rs_v")
            rec = REC(ECOL)
            raw = [over(FW, i * ECOL, [ECOL], I32, ROWS) for i in range(3)]
            with sem.block() as block:
                @block.sync
                def _(sp):
                    for t, name in zip(raw, ("src", "dst", "edge_type_500")):
                        s_l.inc(sp.dma_start(t, A[name].rearrange("(p c) -> p c", p=ROWS)), 16)

                @block.vector
                def _(dve):
                    dve.wait_ge(s_l.sem, 48)
                    for w in range(3):
                        s_v.inc(dve.tensor_copy(rec[:, 0:ECOL, w], raw[w]))
                    s_v.inc(dve.memset(rec[:, 0:ECOL, 3], 0))

        def sort_pass(tag, cols, shift, bits, bins, target, into, bucket):
            sem = Phase()
            s_v, s_pe, s_pool, s_init = sem(tag + "_v"), sem(tag + "_pe"), sem(tag + "_pool"), sem(tag + "_init")
            s_slot = sem.rows_moved(5)
            s_gate, s_gate2 = sem(tag + "_gate"), sem(tag + "_gate2")
            rec = REC(cols)
            o = 0
            views = []
            for dt in (I32, F32, I32, F32, F32):
                views.append(over(FW, o, [cols], dt, ROWS))
                o += ACOL
            key, dig, mask, run, pos = views
            unit = over(TT, 0, [cols], F32, ROWS)
            small = [over(TT, ACOL + 64 * i, [64], F32, ROWS) for i in range(4)]
            cnt, off, tot, beg = small
            pair = over(TT, ACOL + 256, [64], F32, ROWS)
            pair_i = over(TT, ACOL + 320, [64], I32, ROWS)
            pos_i = over(TT, 2 * ACOL, [cols], I32, ROWS)
            ring_pos = over(TT, 3 * ACOL, [5, 5], I32, ROWS)
            ring_rec = over(TT, 3 * ACOL + 32, [5, 5, 4], I32, ROWS)
            tile_no = over(TT, 4 * ACOL, [G * C], F32, 1)
            tiles = over(TT, 4 * ACOL + G * C, [G * C], F32, 1)
            nil = over(LA[:, :, :, :].rearrange("p a b c -> p (a b c)"), 0, [G * C, 4], I32)
            slots = 0 if not bucket else target.shape[0]
            at = Marks()

            with sem.block() as block:
                if bucket:
                    @block.sync
                    def _(sp):
                        sp.wait_ge(s_v.sem, 2)
                        s_init.inc(sp.dma_start(target[:, :].rearrange("(p c) w -> p c w", p=P),
                                                nil[:, 0:slots // P, :]), 16)
                        s_init.wait(sp)

                @block.vector
                def _(dve):
                    if bucket:
                        s_v.link(dve, dve.memset(nil[:, :, :], 0))
                        s_v.link(dve, dve.memset(nil[:, :, 0], NIL << shift if bucket == 1 else NIL << 6))
                    s_v.link(dve, dve.tensor_scalar(key, rec[:, :, 0], shift, (1 << bits) - 1,
                                                    ALU.logical_shift_right, ALU.bitwise_and))
                    s_v.inc(dve.tensor_copy(dig, key))
                    s_v.inc(dve.memset(unit, 1.0))
                    s_v.inc(dve.memset(cnt, 0.0))
                    s_v.inc(dve.memset(pos, 0.0))
                    s_v.wait(dve)
                    with dve.Fori(0, bins) as b:
                        t = Step(s_v, b, 1)
                        t.link(dve, dve.tensor_scalar(mask, dig, iota[0:ROWS, bass.ds(b, 1)], None,
                                                      ALU.is_equal, ALU.add, accum_out=cnt[:, bass.ds(b, 1)]))
                    t.end(bins)
                    at.counted = s_v.n
                    dve.wait_ge(s_pe.sem, 2)
                    s_v.link(dve, dve.tensor_copy(tot, PS[0:ROWS, 1, 0:64]))
                    if bucket:
                        nb = bins // bucket
                        if bucket == 2:
                            even, odd = (tot.rearrange("p (a b) -> p b a", b=2)[:, i, 0:nb] for i in range(2))
                            s_v.link(dve, dve.tensor_tensor(pair[:, 0:nb], even, odd, ALU.add))
                        else:
                            s_v.link(dve, dve.tensor_copy(pair[:, 0:nb], tot[:, 0:nb]))
                        s_v.link(dve, dve.tensor_scalar(pair[:, 0:nb], pair[:, 0:nb], float(P - 1), None, ALU.add))
                        s_v.link(dve, dve.tensor_copy(pair_i[:, 0:nb], pair[:, 0:nb]))
                        s_v.link(dve, dve.tensor_scalar(pair_i[:, 0:nb], pair_i[:, 0:nb], 7, 7,
                                                        ALU.logical_shift_right, ALU.logical_shift_left))
                        s_v.link(dve, dve.tensor_copy(pair[:, 0:nb], pair_i[:, 0:nb]))
                        s_v.link(dve, dve.tensor_tensor_scan(off[:, 0:nb], unit[:, 0:nb], pair[:, 0:nb], 0.0,
                                                             ALU.mult, ALU.add))
                        s_v.link(dve, dve.tensor_tensor(off[:, 0:nb], off[:, 0:nb], pair[:, 0:nb], ALU.subtract))
                        if bucket == 2:
                            b_even, b_odd = (beg.rearrange("p (a b) -> p b a", b=2)[:, i, 0:nb] for i in range(2))
                            s_v.inc(dve.tensor_copy(b_even, off[:, 0:nb]))
                            s_v.inc(dve.tensor_tensor(b_odd, off[:, 0:nb], even, ALU.add))
                            s_v.wait(dve)
                        else:
                            s_v.link(dve, dve.tensor_copy(beg[:, 0:nb], off[:, 0:nb]))
                        s_v.link(dve, dve.tensor_scalar(pair[:, 0:nb], off[:, 0:nb], 1.0 / P, None, ALU.mult))
                        s_v.link(dve, dve.memset(tiles, -1.0))
                        nt = into.shape[1]
                        dve.wait_ge(s_pool.sem, 1)
                        for b in range(nb):
                            s_v.link(dve, dve.scalar_tensor_tensor(tiles[:, 0:nt], tile_no[:, 0:nt], pair[0:1, b:b + 1],
                                                                   tiles[:, 0:nt], ALU.is_ge, ALU.add))
                        s_v.link(dve, dve.tensor_copy(into[:, :], tiles[:, 0:nt]))
                    else:
                        s_v.link(dve, dve.tensor_tensor_scan(beg[:, 0:bins], unit[:, 0:bins], tot[:, 0:bins], 0.0,
                                                             ALU.mult, ALU.add))
                        s_v.link(dve, dve.tensor_tensor(beg[:, 0:bins], beg[:, 0:bins], tot[:, 0:bins], ALU.subtract))
                    s_v.link(dve, dve.scalar_tensor_tensor(off[:, 0:bins], beg[:, 0:bins], -1.0, PS[0:ROWS, 0, 0:bins],
                                                           ALU.add, ALU.add))
                    with dve.Fori(0, bins) as b:
                        t = Step(s_v, b, 3)
                        t.link(dve, dve.tensor_scalar(mask, dig, iota[0:ROWS, bass.ds(b, 1)], None, ALU.is_equal))
                        t.link(dve, dve.tensor_tensor_scan(run, unit, mask, off[:, bass.ds(b, 1)], ALU.mult, ALU.add))
                        dve.sem_inc(s_gate.sem, 1)
                        t.inc(dve.copy_predicated(pos, mask, run))
                        t.wait(dve)
                    t.end(bins)
                    s_v.link(dve, dve.tensor_copy(pos_i, pos))
                    s_v.inc(dve.memset(mask[:, 0:1], 0))
                    at.placed = s_v.n

                @block.tensor
                def _(pe):
                    pe.wait_ge(s_v.sem, at.counted)
                    s_pe.inc(pe.matmul(PS[0:ROWS, 0, 0:64], lower[0:ROWS, 0:ROWS], cnt, start=True, stop=True))
                    s_pe.inc(pe.matmul(PS[0:ROWS, 1, 0:64], ones[0:ROWS, 0:ROWS], cnt, start=True, stop=True))

                @block.gpsimd
                def _(pool):
                    if bucket:
                        if into is bt:
                            s_pool.inc(pool.iota(tile_no[:, 0:G * C], [[1, G], [G, C]], base=0, channel_multiplier=0,
                                                 allow_small_or_imprecise_dtypes=True))
                        else:
                            s_pool.inc(pool.iota(tile_no[:, 0:EG * C], [[1, EG * C]], base=0, channel_multiplier=0,
                                                 allow_small_or_imprecise_dtypes=True))
                        pool.wait_ge(s_init.sem, 16)
                    pool.wait_ge(s_v.sem, at.placed)
                    base = s_pool.n

                    def scatter_turn(i, peeled):
                        for k in range(5):
                            if not peeled:
                                pool.wait_ge(s_slot[k].sem, i * 80 + s_slot[k].n)
                            pool.tensor_copy(ring_pos[:, k, :], pos_i[:, bass.ds(i * 25 + k * 5, 5)])\
                                .then_inc(s_pool.sem, 1)
                            pool.tensor_copy(ring_rec[:, k, :, :], rec[:, bass.ds(i * 25 + k * 5, 5), :])\
                                .then_inc(s_pool.sem, 1)
                            pool.wait_ge(s_pool.sem, i * 10 + (base + 2 * k + 2))
                            pool.sem_inc(s_gate2.sem, 1)
                            for j in range(5):
                                pool.indirect_dma_start(
                                    out=target[:, :], out_offset=bass.IndirectOffsetOnAxis(
                                        ap=ring_pos[:, k, j:j + 1].bitcast(U32), axis=0),
                                    in_=ring_rec[:, k, j, :], in_offset=None).then_inc(s_slot[k].sem, 16)

                    scatter_turn(0, True)
                    with pool.Fori(1, cols // 25) as i:
                        scatter_turn(i, False)
                    for k in range(5):
                        s_slot[k].n += 80 * (cols // 25)
                        s_slot[k].wait(pool)

        def load_records(tag, source):
            sem = Phase()
            s_l = sem(tag + "_l")
            with sem.block() as block:
                @block.sync
                def _(sp):
                    s_l.inc(sp.dma_start(REC(ACOL), source[:, :].rearrange("(p c) w -> p c w", p=ROWS)), 16)
                    s_l.wait(sp)

        LAF = LA[:, :, :, :].rearrange("p g c h -> p (g c h)")

        PLACE = sb("place", [P, 2, 2 * P])

        def turn(tag, src, dst):
            sem = Phase()
            s_turned = [sem(f"{tag}_turned{h}") for h in range(2)]
            s_copied = [sem(f"{tag}_copied{h}") for h in range(2)]
            s_here = [sem(f"{tag}_here{h}") for h in range(2)]
            with sem.block() as block:
                @block.gpsimd
                def _(pool):
                    for h in range(2):
                        pool.sem_inc(s_here[h].sem, 1)
                    with pool.Fori(0, G // 4) as i:
                        for h in range(2):
                            pool.wait_ge(s_turned[h].sem, i + 1)
                            pool.tensor_copy(PLACE[:, h, :], src[:, bass.ds((i * 4 + 2 * h) * P, 2 * P)])\
                                .then_inc(s_here[h].sem, 1)

                @block.tensor
                def _(pe):
                    for h in range(2):
                        pe.sem_inc(s_turned[h].sem, 1)
                    with pe.Fori(0, G // 4) as i:
                        for h in range(2):
                            pe.wait_ge(s_copied[h].sem, i + 1)
                            pe.wait_ge(s_here[h].sem, i + 2)
                            for j in range(2):
                                m = pe.transpose(PS[:, h, j * P:(j + 1) * P], PLACE[:, h, j * P:(j + 1) * P], ident[:, :])
                            m.then_inc(s_turned[h].sem, 1)

                @block.scalar
                def _(act):
                    act.sem_inc(s_copied[0].sem, 1)
                    with act.Fori(0, G // 4) as i:
                        act.wait_ge(s_turned[0].sem, i + 2)
                        act.activation(dst[:, bass.ds(i * 4 * P, 2 * P)], PS[:, 0, 0:2 * P], ACT.Copy)\
                           .then_inc(s_copied[0].sem, 1)

                @block.vector
                def _(dve):
                    dve.sem_inc(s_copied[1].sem, 1)
                    with dve.Fori(0, G // 4) as i:
                        dve.wait_ge(s_turned[1].sem, i + 2)
                        dve.tensor_copy(dst[:, bass.ds(i * 4 * P + 2 * P, 2 * P)], PS[:, 1, 0:2 * P])\
                           .then_inc(s_copied[1].sem, 1)

        def keys(tag, rec, shift, first):
            sem = Phase()
            s_l, s_v = sem(tag + "_l"), sem(tag + "_v")
            keyf, tmp = over(FW, 0, [G, C]), over(FW, 2 * G * C, [G, C])
            keyi = over(FW, G * C, [G, C], I32)
            rep = over(TT, 0, [G, C, HD])
            by_group = rec.rearrange("p c g w -> p w g c")
            gc = lambda t: t[:, 0:G * C].rearrange("p (g c) -> p g c", c=C)
            with sem.block() as block:
                if first:
                    @block.sync
                    def _(sp):
                        for c in range(C):
                            s_l.inc(sp.dma_start(rec[:, c, :, :], d_list[c * SEQ:(c + 1) * SEQ, :]
                                                 .rearrange("(g p) w -> p g w", p=P)), 16)

                @block.vector
                def _(dve):
                    if first:
                        dve.wait_ge(s_l.sem, 16 * C)
                        for index, w in ((src_i, 1), (eid_i, 2), (prj_i, 3)):
                            s_v.inc(dve.tensor_copy(gc(index), by_group[:, w]))
                        s_v.inc(dve.memset(dl[:, G * C:], NEG))
                        s_v.inc(dve.memset(dlm[:, G * C:], NEG))
                        s_v.inc(dve.tensor_copy(keyf, by_group[:, 0]))
                        s_v.link(dve, dve.tensor_copy(keyi, by_group[:, 0]))
                        s_v.link(dve, dve.tensor_scalar(keyi, keyi, 63, None, ALU.bitwise_and))
                        s_v.link(dve, dve.tensor_copy(gc(typ), keyi))
                        s_v.link(dve, dve.tensor_copy(keyi, by_group[:, 0]))
                        s_v.link(dve, dve.tensor_scalar(keyi, keyi, 6, P - 1, ALU.logical_shift_right, ALU.bitwise_and))
                        s_v.link(dve, dve.tensor_copy(tmp, keyi))
                        s_v.link(dve, dve.tensor_scalar(keyf, keyf, float(NIL * 64), NEG, ALU.is_ge, ALU.mult))
                        s_v.link(dve, dve.tensor_tensor(gc(dl), tmp, keyf, ALU.add))
                        s_v.link(dve, dve.tensor_scalar(tmp, gc(typ), float(TYPES), NEG, ALU.is_equal, ALU.mult))
                        s_v.link(dve, dve.tensor_tensor(gc(dlm), gc(dl), tmp, ALU.add))
                    s_v.link(dve, dve.tensor_copy(keyi, by_group[:, 0]))
                    if shift:
                        s_v.link(dve, dve.tensor_scalar(keyi, keyi, shift, None, ALU.logical_shift_right))
                    s_v.inc(dve.tensor_copy(rep, bc(keyi, 3, HD)))

        def flags(tag, flag, whole):
            sem = Phase()
            s_v, s_pe = sem(tag + "_v"), sem(tag + "_pe")
            with sem.block() as block:
                @block.tensor
                def _(pe):
                    pe.matmul(PS[:, 2, 0:1], up8[:, :], LAF[:, SEQ - 1:SEQ], start=True, stop=True)
                    pe.matmul(PS[:, 2, 1:2], down8[:, :], LAF[:, 0:1], start=True, stop=True).then_inc(s_pe.sem, 1)

                @block.vector
                def _(dve):
                    s_v.inc(dve.tensor_tensor(flag[:, 1:SEQ], LAF[:, 1:SEQ], LAF[:, 0:SEQ - 1], ALU.is_equal))
                    dve.wait_ge(s_pe.sem, 1)
                    s_v.inc(dve.tensor_tensor(flag[:, 0:1], LAF[:, 0:1], PS[:, 2, 0:1], ALU.is_equal))
                    s_v.inc(dve.tensor_tensor(flag[:, SEQ:SEQ + 1], LAF[:, SEQ - 1:SEQ], PS[:, 2, 1:2], ALU.is_equal))
                    s_v.wait(dve)
                    s_v.inc(dve.tensor_reduce(whole[:, 0:1], flag[:, 0:SEQ], AX.X, ALU.min))
                    s_v.inc(dve.tensor_reduce(whole[:, 1:2], flag[:, 1:SEQ + 1], AX.X, ALU.min))

        def source_tables():
            sem = Phase()
            s_l, s_v = sem("st_l"), sem("st_v")
            rec = over(XT, 0, [EG * C, 4], I32)
            keyf, tmp = over(FW, 0, [EG * C]), over(FW, 2 * EG * C, [EG * C])
            keyi = over(FW, EG * C, [EG * C], I32)
            with sem.block() as block:
                @block.sync
                def _(sp):
                    s_l.inc(sp.dma_start(rec, d_slist[:, :].rearrange("(t p) w -> p t w", p=P)), 16)

                @block.vector
                def _(dve):
                    dve.wait_ge(s_l.sem, 16)
                    s_v.inc(dve.tensor_copy(SDST, rec[:, :, 1]))
                    s_v.inc(dve.tensor_copy(SREL, rec[:, :, 2]))
                    s_v.inc(dve.tensor_copy(keyf, rec[:, :, 0]))
                    s_v.link(dve, dve.tensor_copy(keyi, rec[:, :, 0]))
                    s_v.link(dve, dve.tensor_scalar(keyi, keyi, P - 1, None, ALU.bitwise_and))
                    s_v.link(dve, dve.tensor_copy(tmp, keyi))
                    s_v.link(dve, dve.tensor_scalar(keyf, keyf, float(NIL), NEG, ALU.is_ge, ALU.mult))
                    s_v.inc(dve.tensor_tensor(sdl[:, 0:EG * C], tmp, keyf, ALU.add))

        SDST = src_i[:, 0:EG * C]
        SREL = eid_i[:, 0:EG * C]

        WCAT = over(TT, 0, [512])
        BIAS = over(TT, 512, [512], F32, 1)
        XT5 = over(TT, 1024, [5, P])
        FIVE = over(TT, 1664, [5, P])
        STAGE = over(FW, 0, [5, 512])
        HID = over(LAF, 0, [NT, D])

        def project(tag, src, width, keep, adds, sends):
            sem = Phase()
            s_t, s_pe, s_a, s_v = sem(tag + "_t"), sem(tag + "_pe"), sem(tag + "_a"), sem(tag + "_v")
            s_st, s_here, s_stored = sem(tag + "_st"), sem(tag + "_here"), sem(tag + "_stored")
            turns, whole = NT // 5, 16 * len(sends)
            qt = QT[:, 0:NT * keep].rearrange("p (t q) -> p t q", q=keep)
            pairs = PS[:, 0:2, :].rearrange("p b d -> p (b d)")
            with sem.block() as block:
                @block.gpsimd
                def _(pool):
                    with pool.Fori(0, turns) as i:
                        pool.wait_ge(s_t.sem, i + 1)
                        pool.tensor_copy(FIVE, src[:, bass.ds(i * 5, 5), :]).then_inc(s_here.sem, 1)

                @block.tensor
                def _(pe):
                    pe.sem_inc(s_t.sem, 1)
                    with pe.Fori(0, turns) as i:
                        pe.wait_ge(s_here.sem, i + 1)
                        for j in range(5):
                            m = pe.transpose(pairs[:, j * P:(j + 1) * P], FIVE[:, j, :], ident[:, :])
                        m.then_inc(s_t.sem, 1)
                        pe.wait_ge(s_a.sem, i + 1)
                        for j in range(5):
                            pe.wait_ge(s_v.sem, i * 5 + 1)
                            pe.matmul(PS[:, 2 + j, 0:width], XT5[:, j, :], WCAT[:, 0:width], start=True, stop=False)
                            pe.matmul(PS[:, 2 + j, 0:width], ones[0:1, :], BIAS[:, 0:width], start=False, stop=True)\
                              .then_inc(s_pe.sem, 1)

                @block.scalar
                def _(act):
                    with act.Fori(0, turns) as i:
                        act.wait_ge(s_t.sem, i + 2)
                        act.activation(XT5.rearrange("p j d -> p (j d)"), pairs[:, 0:5 * P], ACT.Copy)\
                           .then_inc(s_a.sem, 1)

                @block.vector
                def _(dve):
                    dve.sem_inc(s_v.sem, 1)
                    dve.sem_inc(s_stored.sem, 1)
                    with dve.Fori(0, turns) as i:
                        dve.wait_ge(s_stored.sem, i + 1)
                        for j in range(5):
                            dve.wait_ge(s_pe.sem, i * 5 + j + 1)
                            at = bass.ds(i * 5 + j, 1)
                            dve.tensor_copy(qt[:, at, :], PS[:, 2 + j:3 + j, 0:keep])
                            if adds:
                                dve.tensor_tensor(ACC[:, at, 0:D], PS[:, 2 + j:3 + j, adds[0]:adds[1]],
                                                  src[:, at, :], ALU.add)
                            a, b = sends[0][0], sends[-1][1]
                            dve.tensor_copy(STAGE[:, j:j + 1, 0:b - a], PS[:, 2 + j:3 + j, a:b]).then_inc(s_v.sem, 1)

                @block.sync
                def _(sp):
                    base = sends[0][0]
                    with sp.Fori(0, turns) as i:
                        sp.wait_ge(s_v.sem, i * 5 + 6)
                        for a, b, table in sends:
                            sp.dma_start(table[:, :].rearrange("(t p) d -> p t d", p=P)[:, bass.ds(i * 5, 5), :],
                                         STAGE[:, :, a - base:b - base]).then_inc(s_st.sem, 16)
                        sp.wait_ge(s_st.sem, i * whole + whole)
                        sp.sem_inc(s_stored.sem, 1)

        class Norms:

            def __init__(self, s_v, s_a):
                self.s_v, self.s_a, self.asked = s_v, s_a, []
                self.mean, self.var = over(TT, 4096, [NT]), over(TT, 4096 + NT, [NT])

            def norm(self, dve, x, scratch, gamma=None, beta=None):
                v, mean, var = self.s_v, self.mean, self.var
                v.link(dve, dve.tensor_reduce(mean, x, AX.X, ALU.add))
                v.link(dve, dve.tensor_scalar(mean, mean, 1.0 / D, None, ALU.mult))
                v.link(dve, dve.tensor_tensor(x, x, bc(mean, 2, D), ALU.subtract))
                v.link(dve, dve.tensor_tensor(scratch, x, x, ALU.mult))
                v.link(dve, dve.tensor_reduce(var, scratch, AX.X, ALU.add))
                v.link(dve, dve.tensor_scalar(var, var, 1.0 / D, 1e-5, ALU.mult, ALU.add))
                self.asked.append(v.n)
                dve.wait_ge(self.s_a.sem, len(self.asked))
                v.link(dve, dve.reciprocal(var, var))
                v.link(dve, dve.tensor_tensor(x, x, bc(var, 2, D), ALU.mult))
                if gamma is not None:
                    v.link(dve, dve.tensor_tensor(x, x, bc(gamma, 1, NT), ALU.mult))
                    v.link(dve, dve.tensor_tensor(x, x, bc(beta, 1, NT), ALU.add))

            def roots(self, act):
                for n in self.asked:
                    act.wait_ge(self.s_v.sem, n)
                    act.activation(self.var, self.var, ACT.Sqrt).then_inc(self.s_a.sem, 1)

        row_of = lambda name: A[name].rearrange("(a n) -> a n", a=1)
        rows_of = lambda name: row_of(name).to_broadcast([P, D])

        T = STEPS
        RING = over(XT, 0, [T, U, 2 * D])
        RING2 = over(XT, T * U * 2 * D, [T, U, ED])
        IDX = over(XT, T * U * (2 * D + ED), [T, U], U32)
        IDX2 = over(XT, T * U * (2 * D + ED + 1), [T, U], U32)
        OH = over(FW, 0, [2, U, P])
        OHT = over(FW, 1024, [2, U, P])
        ATT = over(FW, 2048, [2, U, P], F32, ED)
        SUM = over(FW, 3072, [2, U, D])
        PROD = over(FW, 4096, [2, U, D])
        VOUT = over(TT, 0, [T, U, D])
        WE = over(TT, 2048, [D], F32, ED)
        ATTW = over(TT, 2176, [D])
        TOH = over(TT, 2304, [2, U, TYPES])
        SMALL = over(TT, 2560, [6, U])

        def one_hot(dve, to, labels, at):
            return dve.tensor_tensor(to, bc(iota16[:, :], 1, U), bc(labels[:, bass.ds(at, U)], 2, P), ALU.is_equal)

        def gather(pool, idx, at, rows, table, ring, s_idx, copies, s_land, s_gate):
            pool.tensor_copy(idx, rows[:, bass.ds(at, U)]).then_inc(s_idx.sem, 1)
            pool.wait_ge(s_idx.sem, copies)
            pool.sem_inc(s_gate.sem, 1)
            for j in range(U):
                pool.indirect_dma_start(out=ring[:, j, :], out_offset=None, in_=table,
                                        in_offset=bass.IndirectOffsetOnAxis(ap=idx[:, j:j + 1], axis=0))\
                    .then_inc(s_land.sem, 16)

        def tiles_of(eng, which, table, i):
            _, tiles = nc.values_load_multi_w_load_instructions(
                table[0:1, bass.ds(i * C, C)], engines=(which,), min_val=0, max_val=NT - 1,
                skip_runtime_bounds_check_because="the sort writes tile numbers below NT")
            return tiles

        def scores(tag, kind, table, width, qw):
            mha, rules, gat = kind == "mha", kind == "rules", kind == "gatv2"
            sem = Phase()
            s_idx, s_done = sem(tag + "_idx"), sem(tag + "_done")
            s_gate, s_gate2 = sem(tag + "_gate"), sem(tag + "_gate2")
            s_land = sem.rows_moved(T)
            s_spill, s_stored = [sem(f"{tag}_spill{k}") for k in range(T)], sem(tag + "_stored")
            s_oh, s_ohT, s_ohc, s_q = (sem(tag + x) for x in ("_oh", "_ohT", "_ohc", "_q"))
            s_v, s_at, s_atc = sem(tag + "_v"), sem(tag + "_at"), sem(tag + "_atc")
            qt = QT[:, 0:NT * qw].rearrange("p (t q) -> p t q", q=qw)
            gathers = 2 if mha else 1
            landed = 16 * U * gathers
            ops = {"mha": 3, "rules": 6, "gatv2": 3}[kind]

            def qps(b):
                if rules:
                    return PS[:, 2 + 2 * b:4 + 2 * b, :].rearrange("p b (a d) -> p (b a) d", d=256)
                return PS[:, 2 + b, :].rearrange("p (a d) -> p a d", d=D)

            with sem.block() as block:
                @block.gpsimd
                def _(pool):
                    with pool.Fori(0, G) as i:
                        for k in range(T):
                            pool.wait_ge(s_done.sem, i * T + k + 1)
                            if gat:
                                pool.wait_ge(s_stored.sem, i * T + k + 1)
                            at, n = i * C + k * U, i * (T * gathers) + k * gathers
                            gather(pool, IDX[:, k, :], at, src_i, table[:, :], RING[:, k, :, 0:width], s_idx, n + 1, s_land[k], s_gate)
                            if mha:
                                gather(pool, IDX2[:, k, :], at, eid_i, A["edge_attr_64"][:, :], RING2[:, k, :, :], s_idx,
                                       n + 2, s_land[k], s_gate)

                @block.vector
                def _(dve):
                    dve.sem_inc(s_done.sem, T)
                    one_hot(dve, OH[:, 0, :, :], dl, 0).then_inc(s_oh.sem, 1)
                    with dve.Fori(0, G) as i:
                        t = Step(s_v, i, T * ops)
                        for k in range(T):
                            b = k % 2
                            dve.wait_ge(s_ohT.sem, i * T + k + 1)
                            one_hot(dve, OH[:, 1 - b, :, :], dl, i * C + (k + 1) * U).then_inc(s_oh.sem, 1)
                            dve.wait_ge(s_land[k].sem, i * landed + (s_land[k].n + landed))
                            dve.wait_ge(s_q.sem, i * T + k + 2)
                            q = qps(b)
                            la = LA[:, bass.ds(i, 1), k * U:(k + 1) * U, :].rearrange("p g u h -> p (g u) h")
                            x = RING[:, k, :, 0:D]
                            if mha:
                                edge = PS[:, 4 + b, :].rearrange("p (a d) -> p a d", d=D)
                                dve.wait_ge(s_stored.sem, i * T + k + 1)
                                t.inc(dve.tensor_tensor(VOUT[:, k, :, :], RING[:, k, :, D:2 * D], edge, ALU.add))
                                t.link(dve, dve.tensor_tensor(SUM[:, b, :, :], x, edge, ALU.add))
                                t.link(dve, dve.tensor_tensor(PROD[:, b, :, :], SUM[:, b, :, :], q, ALU.mult))
                                last = dve.tensor_reduce(la, PROD[:, b, :, :].rearrange("p a (h c) -> p a h c", h=HD),
                                                         AX.X, ALU.add)
                            elif gat:
                                t.link(dve, dve.tensor_tensor(SUM[:, b, :, :], x, q, ALU.add))
                                t.link(dve, dve.scalar_tensor_tensor(PROD[:, b, :, :], SUM[:, b, :, :], 0.2,
                                                                     SUM[:, b, :, :], ALU.mult, ALU.max))
                                t.link(dve, dve.tensor_tensor(SUM[:, b, :, :], PROD[:, b, :, :], bc(ATTW, 1, U), ALU.mult))
                                last = dve.tensor_reduce(la[:, :, 0:4], SUM[:, b, :, :].rearrange("p a (h c) -> p a h c", h=4),
                                                         AX.X, ALU.add)
                            else:
                                base, rel, both = (SMALL[:, 3 * b + n, :] for n in range(3))
                                kinds = bc(typ[:, bass.ds(i * C + k * U, U)], 2, TYPES)
                                t.inc(dve.tensor_tensor(PROD[:, b, :, :], x, q[:, :, 0:D], ALU.mult))
                                t.link(dve, dve.tensor_tensor(TOH[:, b, :, :], bc(iota16[:, 0:TYPES], 1, U), kinds, ALU.is_equal))
                                t.inc(dve.tensor_reduce(base, PROD[:, b, :, :], AX.X, ALU.add))
                                t.link(dve, dve.tensor_tensor(TOH[:, b, :, :], TOH[:, b, :, :], q[:, :, D:D + TYPES], ALU.mult))
                                t.link(dve, dve.tensor_reduce(rel, TOH[:, b, :, :], AX.X, ALU.add))
                                t.link(dve, dve.tensor_tensor(both, base, rel, ALU.add))
                                last = dve.tensor_tensor(la[:, :, 0:4], bc(both, 2, 4), q[:, :, D + TYPES:LQ], ALU.add)
                            last.then_inc(s_done.sem, 1)
                    t.end(G)

                @block.tensor
                def _(pe):
                    def turn_one_hots(b):
                        for j in range(U):
                            m = pe.transpose(PS[:, b, j * P:(j + 1) * P], OH[:, b, j, :], ident[:, :])
                        m.then_inc(s_ohT.sem, 1)

                    pe.sem_inc(s_q.sem, 1)
                    pe.wait_ge(s_oh.sem, 1)
                    turn_one_hots(0)
                    with pe.Fori(0, G) as i:
                        tiles = tiles_of(pe, ENG.PE, bt, i)
                        for k in range(T):
                            b = k % 2
                            pe.wait_ge(s_ohc.sem, i * T + k + 1)
                            pe.wait_ge(s_oh.sem, i * T + k + 2)
                            turn_one_hots(1 - b)
                            if mha:
                                pe.wait_ge(s_land[k].sem, i * landed + (s_land[k].n + landed))
                                pe.sem_inc(s_gate2.sem, 1)
                                for j in range(U):
                                    m = pe.transpose(PS[0:ED, 6 + b, j * P:(j + 1) * P], RING2[:, k, j, :], ident[:, :])
                                m.then_inc(s_at.sem, 1)
                            pe.wait_ge(s_done.sem, i * T + k + 3)
                            q = qps(b)
                            for j in range(U):
                                m = pe.matmul(q[:, j, 0:qw], OHT[:, b, j, :],
                                              qt[:, bass.ds(tiles[k * U + j], 1), :].rearrange("p a q -> p (a q)"),
                                              start=True, stop=True)
                            if mha:
                                pe.wait_ge(s_atc.sem, i * T + k + 1)
                                for j in range(U):
                                    m = pe.matmul(PS[:, 4 + b, j * P:(j + 1) * P], ATT[:, b, j, :], WE,
                                                  start=True, stop=True)
                            m.then_inc(s_q.sem, 1)

                @block.scalar
                def _(act):
                    def copy_one_hots(b):
                        act.activation(OHT[:, b, :, :].rearrange("p a d -> p (a d)"), PS[:, b, :], ACT.Copy)\
                           .then_inc(s_ohc.sem, 1)

                    act.wait_ge(s_ohT.sem, 1)
                    copy_one_hots(0)
                    with act.Fori(0, G) as i:
                        for k in range(T):
                            b = k % 2
                            if mha:
                                act.wait_ge(s_at.sem, i * T + k + 1)
                                act.activation(ATT[:, b, :, :].rearrange("p a d -> p (a d)"), PS[0:ED, 6 + b, :], ACT.Copy)\
                                   .then_inc(s_atc.sem, 1)
                            act.wait_ge(s_ohT.sem, i * T + k + 2)
                            act.wait_ge(s_q.sem, i * T + k + 1)
                            copy_one_hots(1 - b)

                @block.sync
                def _(sp):
                    if not rules:
                        def stored(i, k):
                            sp.wait_ge(s_spill[k].sem, i * 16 + 16)
                            sp.sem_inc(s_stored.sem, 1)

                        sp.sem_inc(s_stored.sem, T)
                        with sp.Fori(0, G) as i:
                            for k in range(T):
                                if mha:
                                    sp.wait_ge(s_v.sem, i * (T * ops) + k * ops + 1)
                                else:
                                    sp.wait_ge(s_land[k].sem, i * landed + (s_land[k].n + landed))
                                rows = VOUT[:, k, :, :] if mha else RING[:, k, :, 0:D]
                                sp.dma_start(d_spill[bass.ds(i, 1), :, k * U:(k + 1) * U, :]
                                             .rearrange("g p c d -> (g p) c d"), rows).then_inc(s_spill[k].sem, 16)
                                if k:
                                    stored(i, k - 1)
                            stored(i, T - 1)

            for k in range(T):
                s_land[k].n += landed * G

        carry = sb("carry", [P, 4])
        row = sb("row", [1, P + 2 * HD])
        rowf = sb("rowf", [1, P])
        whole_d = sb("whole_d", [P, 2])
        whole_k = sb("whole_k", [P, 2])
        ALPHA = QT[:, 0:G * C]

        def softmax(tag, flag, whole, eps, scale):
            sem = Phase()
            s_v, s_pe, s_a = sem(tag + "_v"), sem(tag + "_pe"), sem(tag + "_a")
            stages = []
            heads = [lambda t, o, h=h: t[0:1, o:o + P].rearrange("p (c h) -> p h c", h=HD)[:, h, :] for h in range(HD)]
            back = lambda ap: ap[:, ::-1]
            with sem.block() as block:
                @block.vector
                def _(dve):
                    v = s_v

                    def ask(what):
                        stages.append((v.n, what))
                        dve.wait_ge(s_pe.sem, len(stages))

                    def carried(last, kind):
                        v.link(dve, dve.tensor_copy(carry[:, 0:1], last))
                        v.link(dve, dve.tensor_copy(carry[:, 1:2], whole[:, 1:2] if kind == "back" else whole[:, 0:1]))
                        ask("row")
                        neutral = -BIG if kind == "max" else 0.0
                        v.link(dve, dve.memset(row[:, :], neutral))
                        if kind == "max":
                            v.link(dve, dve.tensor_scalar(rowf[:, :], PS[0:1, 1, 0:P], BIG, -BIG, ALU.mult, ALU.add))
                        else:
                            v.link(dve, dve.tensor_copy(rowf[:, :], PS[0:1, 1, 0:P]))
                        for h in range(HD):
                            f, x = heads[h](rowf, 0), PS[0:1, 0, 0:P].rearrange("p (c h) -> p h c", h=HD)[:, h, :]
                            if kind == "back":
                                v.inc(dve.tensor_tensor_scan(back(heads[h](row, 0)), back(f), back(x), 0.0, ALU.mult, ALU.add))
                            elif kind == "max":
                                v.inc(dve.tensor_tensor_scan(heads[h](row, 2 * HD), f, x, neutral, ALU.add, ALU.max))
                            else:
                                v.inc(dve.tensor_tensor_scan(heads[h](row, 2 * HD), f, x, 0.0, ALU.mult, ALU.add))
                        v.wait(dve)
                        ask("column")
                        v.link(dve, dve.tensor_copy(carry[:, 2:3], PS[:, 2, 0:1]))

                    def last_value_back():
                        v.link(dve, dve.scalar_tensor_tensor(LAF, flag[:, 1:SEQ + 1], 1.0, FW[:, :], ALU.not_equal, ALU.mult))
                        run = lambda init: dve.tensor_tensor_scan(back(TT), back(flag[:, 1:SEQ + 1]), back(LAF), init,
                                                                  ALU.mult, ALU.add)
                        v.link(dve, run(0.0))
                        carried(TT[:, 0:1], "back")
                        v.link(dve, run(carry[:, 2:3]))

                    v.link(dve, dve.tensor_scalar(TT[:, :], flag[:, 0:SEQ], BIG, -BIG, ALU.mult, ALU.add))
                    v.link(dve, dve.tensor_tensor_scan(FW[:, :], TT[:, :], XT[:, :], -BIG, ALU.add, ALU.max))
                    carried(FW[:, SEQ - 1:SEQ], "max")
                    v.link(dve, dve.tensor_tensor_scan(FW[:, :], TT[:, :], XT[:, :], carry[:, 2:3], ALU.add, ALU.max))
                    last_value_back()
                    v.link(dve, dve.tensor_tensor(XT[:, :], XT[:, :], TT[:, :], ALU.subtract))
                    at.shifted = v.n
                    dve.wait_ge(s_a.sem, 1)
                    sums = lambda init: dve.tensor_tensor_scan(FW[:, :], flag[:, 0:SEQ], XT[:, :], init, ALU.mult, ALU.add)
                    v.link(dve, sums(0.0))
                    carried(FW[:, SEQ - 1:SEQ], "sum")
                    v.link(dve, sums(carry[:, 2:3]))
                    last_value_back()
                    if eps:
                        v.link(dve, dve.tensor_scalar(TT[:, :], TT[:, :], eps, None, ALU.add))
                    v.link(dve, dve.reciprocal(TT[:, :], TT[:, :]))
                    v.link(dve, dve.tensor_tensor(XT[:, :], XT[:, :], TT[:, :], ALU.mult))

                @block.tensor
                def _(pe):
                    for n, what in stages:
                        pe.wait_ge(s_v.sem, n)
                        if what == "row":
                            pe.matmul(PS[0:1, 0, 0:P], carry[:, 0:1], ident[:, :], start=True, stop=True)
                            pe.matmul(PS[0:1, 1, 0:P], carry[:, 1:2], ident[:, :], start=True, stop=True)\
                              .then_inc(s_pe.sem, 1)
                        else:
                            pe.matmul(PS[:, 2, 0:1], row[0:1, HD:HD + P], ones[0:1, 0:1], start=True, stop=True)\
                              .then_inc(s_pe.sem, 1)

                @block.scalar
                def _(act):
                    act.wait_ge(s_v.sem, at.shifted)
                    act.activation(XT[:, :], XT[:, :], ACT.Exp, scale=scale).then_inc(s_a.sem, 1)

        at = Marks()

        VIN = over(XT, 0, [T, U, D])
        MSG = over(XT, 2048, [2, U, W0])
        IDX3 = over(XT, 3200, [T, U], U32)

        def aggregate(tag, labels, heads, table):
            sem = Phase()
            s_idx, s_v, s_sum, s_gate = sem(tag + "_idx"), sem(tag + "_v"), sem(tag + "_sum"), sem(tag + "_gate")
            s_land = [sem(f"{tag}_land{k}") for k in range(T)] if table is None else sem.rows_moved(T)
            landed = 16 if table is None else 16 * U
            order = [("build", 0), ("build", 1), ("add", 0), ("build", 2), ("add", 1), ("build", 3), ("add", 2), ("add", 3)]
            built, n = {}, 0
            for what, k in order:
                n += 2 if what == "build" else U
                if what == "build":
                    built[k] = n
            per = n
            sums = lambda b: PS[:, 2 * b:2 * b + 2, :].rearrange("p b (a d) -> p (b a) d", d=256)

            with sem.block() as block:
                @block.vector
                def _(dve):
                    dve.sem_inc(s_v.sem, per)
                    s_v.n = per
                    with dve.Fori(0, G) as i:
                        tiles = tiles_of(dve, ENG.DVE, bt, i)
                        t = Step(s_v, i, per)
                        for what, k in order:
                            b = k % 2
                            if what == "build":
                                t.inc(one_hot(dve, OH[:, b, :, :], labels, i * C + k * U))
                                dve.wait_ge(s_land[k].sem, i * landed + (s_land[k].n + landed))
                                if heads:
                                    w = D // heads
                                    la = LA[:, bass.ds(i, 1), k * U:(k + 1) * U, 0:heads].rearrange("p g u h -> p (g u) h")
                                    t.inc(dve.tensor_tensor(MSG[:, b, :, 0:D].rearrange("p a (h c) -> p a h c", h=heads),
                                                            VIN[:, k, :, :].rearrange("p a (h c) -> p a h c", h=heads),
                                                            bc(la, 3, w), ALU.mult))
                                else:
                                    t.inc(dve.tensor_tensor(MSG[:, b, :, 0:D], VIN[:, k, :, :],
                                                            bc(ALPHA[:, bass.ds(i * C + k * U, U)], 2, D), ALU.mult))
                            else:
                                dve.wait_ge(s_sum.sem, i * T + k + 1)
                                for j in range(U):
                                    acc = ACC[:, bass.ds(tiles[k * U + j], 1), 0:D]
                                    t.link(dve, dve.tensor_tensor(acc, acc, sums(b)[:, j:j + 1, 0:D], ALU.add))
                    t.end(G)

                @block.tensor
                def _(pe):
                    with pe.Fori(0, G) as i:
                        for k in range(T):
                            b = k % 2
                            pe.wait_ge(s_v.sem, i * per + (per + built[k]))
                            for j in range(U):
                                m = pe.matmul(sums(b)[:, j, 0:D], OH[:, b, j, :], MSG[:, b, j, 0:D], start=True, stop=True)
                            m.then_inc(s_sum.sem, 1)

                if table is None:
                    @block.sync
                    def _(sp):
                        with sp.Fori(0, G) as i:
                            for k in range(T):
                                sp.wait_ge(s_v.sem, i * per + built[k])
                                sp.dma_start(VIN[:, k, :, :], d_spill[bass.ds(i, 1), :, k * U:(k + 1) * U, :]
                                             .rearrange("g p c d -> (g p) c d")).then_inc(s_land[k].sem, 16)
                else:
                    @block.gpsimd
                    def _(pool):
                        with pool.Fori(0, G) as i:
                            for k in range(T):
                                pool.wait_ge(s_v.sem, i * per + built[k])
                                gather(pool, IDX3[:, k, :], i * C + k * U, prj_i, table[:, :], VIN[:, k, :, :], s_idx,
                                       i * T + k + 1, s_land[k], s_gate)

            for k in range(T):
                s_land[k].n += landed * G

        def layer0():
            W1 = over(FW, 0, [3, D])
            W1T = over(XT, 0, [3, D])
            w2 = over(FW, 400, [1])
            REL = over(FW, 512, [4, D], F32, ROWS)
            RELT = over(FW, 1024, [4, ROWS])
            WREL = over(FW, 2048, [W0])
            BX = over(FW, 2304, [4, W0], F32, ROWS)
            sem = Phase()
            s_l, s_v, s_pe = sem("l0w_l"), sem("l0w_v"), sem("l0w_pe")
            with sem.block() as block:
                @block.sync
                def _(sp):
                    s_l.inc(sp.dma_start(W1, A["L0_gnn_W_e1"].rearrange("d (a f) -> d a f", a=3)), 16)
                    s_l.inc(sp.dma_start(w2, A["L0_gnn_W_e2"].rearrange("a d -> d a")), 16)
                    s_l.inc(sp.dma_start(REL, A["L0_gnn_rel_embedding"].rearrange("(t p) d -> p t d", p=ROWS)), 16)
                    sp.wait_ge(s_v.sem, 8)
                    s_l.inc(sp.dma_start(d_rel[0:RELS, :].rearrange("(t p) d -> p t d", p=ROWS), BX), 16)
                    s_l.wait(sp)

                @block.tensor
                def _(pe):
                    pe.wait_ge(s_l.sem, 48)
                    for a in range(3):
                        pe.transpose(PS[:, 0, a * P:(a + 1) * P], W1[:, a, :], ident[:, :])
                        pe.matmul(PS[:, 1, a:a + 1], W1[:, a, :], w2, start=True, stop=True)
                    for r in range(4):
                        m = pe.transpose(PS[:, 2, r * P:r * P + ROWS], REL[:, r, :], ident[0:ROWS, 0:ROWS])
                    m.then_inc(s_pe.sem, 1)
                    pe.wait_ge(s_v.sem, 7)
                    for r in range(4):
                        m = pe.matmul(PS[0:ROWS, 3 + r, 0:D + 1], RELT[:, r, :], WREL[:, 0:D + 1], start=True, stop=True)
                    m.then_inc(s_pe.sem, 1)

                @block.vector
                def _(dve):
                    s_v.inc(dve.memset(BIAS, 0.0))
                    s_v.inc(dve.memset(WCAT, 0.0))
                    s_v.inc(dve.memset(BX, 0.0))
                    s_v.wait(dve)
                    dve.wait_ge(s_pe.sem, 1)
                    dve.tensor_copy(WCAT[:, 0:D], PS[:, 0, 0:D])
                    dve.tensor_copy(WCAT[:, D:D + 1], PS[:, 1, 0:1])
                    dve.tensor_copy(WCAT[:, D + 1:2 * D + 1], PS[:, 0, 2 * D:3 * D])
                    s_v.inc(dve.tensor_copy(WCAT[:, 2 * D + 1:2 * D + 2], PS[:, 1, 2:3]))
                    s_v.inc(dve.memset(BIAS[:, 2 * D + 2:2 * D + 3], 1.0))
                    dve.tensor_copy(WREL[:, 0:D], PS[:, 0, D:2 * D])
                    s_v.inc(dve.tensor_copy(WREL[:, D:D + 1], PS[:, 1, 1:2]))
                    s_v.inc(dve.tensor_copy(RELT, PS[:, 2, :].rearrange("p (r n) -> p r n", r=4)[:, :, 0:ROWS]))
                    dve.wait_ge(s_pe.sem, 2)
                    s_v.inc(dve.tensor_copy(BX[:, :, 0:D + 1], PS[0:ROWS, 3:7, 0:D + 1]))

            project("l0p", X, 2 * D + 3, D + 1, None, [(D + 1, 2 * D + 3, d_dst)])

            RA = over(XT, 0, [T, U, W0])
            RB = over(XT, 2304, [T, U, W0])
            I1, I2 = over(XT, 4608, [T, U], U32), over(XT, 4624, [T, U], U32)
            SC = over(XT, 4640, [T, 3, U])
            ONE = over(FW, 0, [T, U, P])
            ONET = over(FW, 2048, [T, U, P])
            qt = QT[:, 0:NT * (D + 1)].rearrange("p (t q) -> p t q", q=D + 1)
            sem = Phase()
            s_idx, s_v, s_oh, s_t, s_sc, s_w, s_sum = (sem("l0e" + x) for x in
                                                     ("_idx", "_v", "_oh", "_t", "_sc", "_w", "_sum"))
            s_tc, s_gate = sem("l0e_tc"), sem("l0e_gate")
            s_land = sem.rows_moved(T)
            ops = 5 + U
            landed = 32 * U
            sums = lambda b: PS[:, 2 * b:2 * b + 2, :].rearrange("p b (a d) -> p (b a) d", d=256)
            with sem.block() as block:
                @block.gpsimd
                def _(pool):
                    with pool.Fori(0, EG) as i:
                        for k in range(T):
                            pool.wait_ge(s_v.sem, i * (T * ops) + k * ops + 6)
                            at, n = i * C + k * U, i * (2 * T) + 2 * k
                            gather(pool, I1[:, k, :], at, SDST, d_dst[:, :], RA[:, k, :, :], s_idx, n + 1, s_land[k], s_gate)
                            gather(pool, I2[:, k, :], at, SREL, d_rel[:, :], RB[:, k, :, :], s_idx, n + 2, s_land[k], s_gate)

                @block.vector
                def _(dve):
                    s_v.n = T * ops
                    dve.sem_inc(s_v.sem, T * ops)
                    dve.memset(ACC[:, :, :], 0.0).then_inc(s_oh.sem, 1)
                    dve.wait_ge(s_oh.sem, 1)
                    with dve.Fori(0, EG) as i:
                        tiles = tiles_of(dve, ENG.DVE, sbt, i)
                        t = Step(s_v, i, T * ops)
                        for k in range(T):
                            total, leaky, weight = (SC[:, k, n, :] for n in range(3))
                            t.inc(one_hot(dve, ONE[:, k, :, :], sdl, i * C + k * U))
                            dve.wait_ge(s_land[k].sem, i * landed + (s_land[k].n + landed))
                            t.link(dve, dve.tensor_tensor(RA[:, k, :, :], RA[:, k, :, :], RB[:, k, :, :], ALU.add))
                            dve.wait_ge(s_sc.sem, i * T + k + 1)
                            t.link(dve, dve.tensor_tensor(total, RA[:, k, :, D], PS[:, 6, k * U:(k + 1) * U], ALU.add))
                            t.inc(dve.scalar_tensor_tensor(leaky, total, 0.2, total, ALU.mult, ALU.max))
                            dve.wait_ge(s_w.sem, i * T + k + 1)
                            t.inc(dve.tensor_tensor(RA[:, k, :, :], RA[:, k, :, :], bc(weight, 2, W0), ALU.mult))
                            dve.wait_ge(s_sum.sem, i * T + k + 1)
                            for j in range(U):
                                acc = ACC[:, bass.ds(tiles[k * U + j], 1), :]
                                t.link(dve, dve.tensor_tensor(acc, acc, sums(k % 2)[:, j:j + 1, 0:W0], ALU.add))
                    t.end(EG)

                @block.tensor
                def _(pe):
                    with pe.Fori(0, EG) as i:
                        tiles = tiles_of(pe, ENG.PE, sbt, i)
                        for k in range(T):
                            n = i * (T * ops) + (T * ops + k * ops)
                            pe.wait_ge(s_v.sem, n + 1)
                            for j in range(U):
                                m = pe.transpose(PS[:, 4, j * P:(j + 1) * P], ONE[:, k, j, :], ident[:, :])
                            m.then_inc(s_t.sem, 1)
                            pe.wait_ge(s_tc.sem, i * T + k + 1)
                            for j in range(U):
                                m = pe.matmul(PS[:, 6, k * U + j:k * U + j + 1], ONET[:, k, j, :],
                                              qt[:, bass.ds(tiles[k * U + j], 1), D:D + 1].rearrange("p a q -> p (a q)"),
                                              start=True, stop=True)
                            m.then_inc(s_sc.sem, 1)
                            pe.wait_ge(s_v.sem, n + 5)
                            for j in range(U):
                                m = pe.matmul(sums(k % 2)[:, j, 0:W0], ONE[:, k, j, :], RA[:, k, j, :], start=True, stop=True)
                            m.then_inc(s_sum.sem, 1)

                @block.scalar
                def _(act):
                    with act.Fori(0, EG) as i:
                        for k in range(T):
                            act.wait_ge(s_t.sem, i * T + k + 1)
                            act.activation(ONET[:, k, :, :].rearrange("p a d -> p (a d)"), PS[:, 4, :], ACT.Copy)\
                               .then_inc(s_tc.sem, 1)
                            act.wait_ge(s_v.sem, i * (T * ops) + (T * ops + k * ops + 4))
                            act.activation(SC[:, k, 2, :], SC[:, k, 1, :], ACT.Exp, scale=-1.0).then_inc(s_w.sem, 1)

            for k in range(T):
                s_land[k].n += landed * EG

            sem = Phase()
            s_v, s_a = sem("l0f_v"), sem("l0f_a")
            norms = Norms(s_v, s_a)
            S, Z = over(TT, 4200, [NT]), over(TT, 4232, [NT])
            own = over(FW, 0, [NT, D])
            with sem.block() as block:
                @block.vector
                def _(dve):
                    v = s_v
                    v.link(dve, dve.tensor_copy(S, ACC[:, :, D + 1]))
                    v.inc(dve.tensor_tensor(own, qt[:, :, 0:D], bc(S, 2, D), ALU.mult))
                    v.inc(dve.tensor_scalar(Z, S, 0.0, 1e-12, ALU.is_equal, ALU.mult))
                    v.wait(dve)
                    v.link(dve, dve.tensor_tensor(Z, Z, S, ALU.add))
                    v.link(dve, dve.reciprocal(Z, Z))
                    v.link(dve, dve.tensor_tensor(own, own, ACC[:, :, 0:D], ALU.add))
                    v.link(dve, dve.tensor_tensor(own, own, bc(Z, 2, D), ALU.mult))
                    v.link(dve, dve.tensor_tensor(X[:, :, :], X[:, :, :], own, ALU.add))
                    norms.norm(dve, X[:, :, :], own)

                @block.scalar
                def _(act):
                    norms.roots(act)

        def layer1():
            sem = Phase()
            s_l, s_v = sem("l1w_l"), sem("l1w_v")
            names = ("q", "k", "v", "skip")
            with sem.block() as block:
                @block.sync
                def _(sp):
                    for n, w in enumerate(names):
                        s_l.inc(sp.dma_start(WCAT[:, n * D:(n + 1) * D], A["L1_gnn_W" + w][:, :]), 16)
                        s_l.inc(sp.dma_start(BIAS[:, n * D:(n + 1) * D], row_of("L1_gnn_b" + w)), 16)
                    s_l.wait(sp)

                @block.vector
                def _(dve):
                    dve.wait_ge(s_l.sem, 128)
                    s_v.inc(dve.tensor_scalar(WCAT[:, 0:D], WCAT[:, 0:D], 0.25, None, ALU.mult))
                    s_v.inc(dve.tensor_scalar(BIAS[:, 0:D], BIAS[:, 0:D], 0.25, None, ALU.mult))

            project("l1p", X, 4 * D, D, (3 * D, 4 * D), [(D, 3 * D, d_kv)])

            sem = Phase()
            s_l = sem("l1e_l")
            with sem.block() as block:
                @block.sync
                def _(sp):
                    s_l.inc(sp.dma_start(WE, A["L1_gnn_We"][:, :]), 16)
                    s_l.wait(sp)

            scores("l1s", "mha", d_kv, 2 * D, D)

            sem = Phase()
            s_v = sem("l1m_v")
            off = over(FW, 0, [G, C])
            with sem.block() as block:
                @block.vector
                def _(dve):
                    s_v.link(dve, dve.tensor_scalar(off, dlm[:, 0:G * C].rearrange("p (g c) -> p g c", c=C),
                                                    NEG, -BIG, ALU.is_ge, ALU.mult))
                    s_v.inc(dve.tensor_tensor(LA[:, :, :, :], LA[:, :, :, :], bc(off, 3, HD), ALU.add))

            turn("l1ta", LAF, XT)
            softmax("l1x", cD, whole_d, 0.0, 1.0)
            turn("l1tb", XT, LAF)
            aggregate("l1g", dlm, HD, None)

            RWS = over(FW, 3200, [4, D])
            WF1 = over(FW, 3712, [4 * D])
            WF2 = over(FW, 4224, [4, D])
            BF1 = over(FW, 4736, [4])
            BF2 = over(TT, 4300, [D], F32, 1)
            H = ACC[:, :, 0:D]
            sem = Phase()
            s_l, s_v, s_a = sem("l1f_l"), sem("l1f_v"), sem("l1f_a")
            norms = Norms(s_v, s_a)
            with sem.block() as block:
                @block.sync
                def _(sp):
                    for n, w in enumerate(("g1", "b1", "g2", "b2")):
                        s_l.inc(sp.dma_start(RWS[:, n, :], rows_of("L1_gnn_" + w)), 16)
                    s_l.inc(sp.dma_start(WF1, A["L1_gnn_Wf1"][:, :]), 16)
                    s_l.inc(sp.dma_start(WF2, A["L1_gnn_Wf2"].rearrange("(c p) d -> p c d", p=P)), 16)
                    s_l.inc(sp.dma_start(BF1, A["L1_gnn_bf1"].rearrange("(c p) -> p c", p=P),
                                         allow_slow_non_contiguous=True), 16)
                    s_l.inc(sp.dma_start(BF2, row_of("L1_gnn_bf2")), 16)
                    s_l.wait(sp)

                @block.vector
                def _(dve):
                    dve.wait_ge(s_l.sem, 128)
                    norms.norm(dve, H, over(FW, 0, [NT, D]), RWS[:, 0, :], RWS[:, 1, :])

                @block.scalar
                def _(act):
                    norms.roots(act)

            hT = over(TT, 0, [P])
            gT = over(TT, 128, [4, P])
            hin = over(TT, 640, [1, P])
            sem = Phase()
            s_t, s_tc, s_up, s_g, s_dn, s_add = (sem("ffn" + x) for x in ("_t", "_tc", "_up", "_g", "_dn", "_add"))
            s_here = sem("ffn_here")
            with sem.block() as block:
                @block.gpsimd
                def _(pool):
                    with pool.Fori(0, NT) as i:
                        pool.wait_ge(s_t.sem, i + 1)
                        pool.tensor_copy(hin, H[:, bass.ds(i, 1), :]).then_inc(s_here.sem, 1)

                @block.tensor
                def _(pe):
                    pe.sem_inc(s_t.sem, 1)
                    with pe.Fori(0, NT) as i:
                        pe.wait_ge(s_here.sem, i + 1)
                        pe.transpose(PS[:, 0, 0:P], hin.rearrange("p a d -> p (a d)"), ident[:, :]).then_inc(s_t.sem, 1)
                        pe.wait_ge(s_tc.sem, i + 1)
                        for c in range(4):
                            m = pe.matmul(PS[:, 1, c * P:(c + 1) * P], WF1[:, c * P:(c + 1) * P], hT, start=True, stop=True)
                        m.then_inc(s_up.sem, 1)
                        pe.wait_ge(s_g.sem, i * 4 + 4)
                        pe.wait_ge(s_add.sem, i + 1)
                        for c in range(4):
                            pe.matmul(PS[:, 2, 0:D], gT[:, c, :], WF2[:, c, :], start=c == 0, stop=False)
                        pe.matmul(PS[:, 2, 0:D], ones[0:1, :], BF2, start=False, stop=True).then_inc(s_dn.sem, 1)

                @block.scalar
                def _(act):
                    with act.Fori(0, NT) as i:
                        act.wait_ge(s_up.sem, i + 1)
                        for c in range(4):
                            act.activation(gT[:, c, :], PS[:, 1, c * P:(c + 1) * P], ACT.Gelu, bias=BF1[:, c:c + 1])\
                               .then_inc(s_g.sem, 1)

                @block.vector
                def _(dve):
                    dve.sem_inc(s_add.sem, 1)
                    with dve.Fori(0, NT) as i:
                        dve.wait_ge(s_t.sem, i + 2)
                        dve.tensor_copy(hT, PS[:, 0, 0:P]).then_inc(s_tc.sem, 1)
                        dve.wait_ge(s_dn.sem, i + 1)
                        dve.tensor_tensor(HID[:, bass.ds(i, 1), :], H[:, bass.ds(i, 1), :], PS[:, 2:3, 0:D], ALU.add)\
                           .then_inc(s_add.sem, 1)

            sem = Phase()
            s_v, s_a = sem("l1n_v"), sem("l1n_a")
            norms = Norms(s_v, s_a)
            with sem.block() as block:
                @block.vector
                def _(dve):
                    norms.norm(dve, HID, over(FW, 0, [NT, D]), RWS[:, 2, :], RWS[:, 3, :])
                    s_v.link(dve, dve.tensor_tensor(X[:, :, :], X[:, :, :], HID, ALU.add))
                    norms.norm(dve, X[:, :, :], over(FW, 0, [NT, D]))

                @block.scalar
                def _(act):
                    norms.roots(act)

        def layer2():
            WR = over(XT, 0, [TYPES, D])
            WK2, WK3 = over(FW, 0, [D]), over(FW, 128, [D])
            WQ = over(FW, 256, [D])
            WQT = over(FW, 384, [D])
            KM = over(FW, 512, [TYPES + 4])
            HREL = over(FW, 576, [TYPES])
            HRUL = over(FW, 640, [4])
            BQ = over(FW, 656, [1])
            RID = over(FW, 660, [1], U32, 4)
            RULE = over(FW, 700, [D], F32, 4)
            M = TYPES + 4
            sem = Phase()
            s_l, s_v, s_pe, s_id = sem("l2w_l"), sem("l2w_v"), sem("l2w_pe"), sem("l2w_id")
            s_r, = sem.rows_moved(1)
            with sem.block() as block:
                @block.sync
                def _(sp):
                    s_id.inc(sp.dma_start(RID.bitcast(I32), A["L2_gnn_rule_ids"].rearrange("(p a) -> p a", a=1)), 16)
                    wk = A["L2_gnn_Wk_w"].rearrange("(a f) d -> a f d", a=3)
                    for t, src in ((WR, A["L2_gnn_W_r"].rearrange("r f o -> f r o")), (WQ, A["L2_gnn_Wq_w"][:, :]),
                                   (WCAT[:, 0:D], A["L2_gnn_Wq_w"][:, :]), (WCAT[:, LQ:LQ + D], wk[0]), (WK2, wk[1]), (WK3, wk[2]),
                                   (BIAS[:, 0:D], row_of("L2_gnn_Wq_b")), (BIAS[:, LQ:LQ + D], row_of("L2_gnn_Wk_b")),
                                   (BQ, A["L2_gnn_Wq_b"].rearrange("(p a) -> p a", a=1))):
                        s_l.inc(sp.dma_start(t, src), 16)
                    s_l.wait(sp)

                @block.gpsimd
                def _(pool):
                    pool.wait_ge(s_id.sem, 16)
                    pool.indirect_dma_start(out=RULE, out_offset=None, in_=A["L2_gnn_rule_emb"][:, :],
                                            in_offset=bass.IndirectOffsetOnAxis(ap=RID, axis=0)).then_inc(s_r.sem, 16)
                    s_r.n += 16
                    s_r.wait(pool)

                @block.vector
                def _(dve):
                    v = s_v
                    dve.wait_ge(s_l.sem, 9 * 16)
                    v.link(dve, dve.tensor_reduce(HREL, WR, AX.X, ALU.add))
                    v.link(dve, dve.tensor_scalar(HREL, HREL, 1.0 / D, None, ALU.mult))
                    dve.wait_ge(s_pe.sem, 1)
                    v.inc(dve.tensor_copy(HRUL, PS[:, 0, 0:4]))
                    v.inc(dve.tensor_copy(WQT, PS[:, 1, 0:D]))
                    dve.wait_ge(s_pe.sem, 2)
                    v.inc(dve.tensor_copy(KM[:, 0:TYPES], PS[:, 2, 0:TYPES]))
                    v.inc(dve.tensor_copy(KM[:, TYPES:M], PS[:, 2, TYPES:M]))
                    dve.wait_ge(s_pe.sem, 3)
                    v.inc(dve.tensor_copy(WCAT[:, D:LQ], PS[:, 3, 0:M]))
                    v.inc(dve.tensor_copy(BIAS[:, D:LQ], PS[0:1, 4, 0:M]))

                @block.tensor
                def _(pe):
                    pe.wait_ge(s_l.sem, 9 * 16)
                    s_r.wait(pe)
                    pe.transpose(PS[:, 0, 0:4], RULE, ident[0:4, 0:4])
                    pe.transpose(PS[:, 1, 0:D], WQ, ident[:, :]).then_inc(s_pe.sem, 1)
                    pe.wait_ge(s_v.sem, 4)
                    pe.matmul(PS[:, 2, 0:TYPES], WK2, HREL, start=True, stop=True)
                    pe.matmul(PS[:, 2, TYPES:M], WK3, HRUL, start=True, stop=True).then_inc(s_pe.sem, 1)
                    pe.wait_ge(s_v.sem, 6)
                    pe.matmul(PS[:, 3, 0:M], WQT, KM, start=True, stop=True)
                    pe.matmul(PS[0:1, 4, 0:M], BQ, KM, start=True, stop=True).then_inc(s_pe.sem, 1)

            stages = [over(FW, 1024, [4, 512]), over(FW, 1024 + 2048, [4, 512])]
            xT = over(FW, 5200, [P])
            sem = Phase()
            s_here, s_stored = sem("pr_here"), sem("pr_stored")
            xin = over(FW, 5330, [1, P])
            s_t, s_tc, s_pe, s_c = sem("pr_t"), sem("pr_tc"), sem("pr_pe"), [sem(f"pr_c{h}") for h in range(2)]
            s_st = [sem(f"pr_st{h}") for h in range(2)]
            WRF = WR.rearrange("p r o -> p (r o)")
            target = d_proj[:, :].rearrange("(t p r) o -> t p (r o)", p=P, r=TYPES)
            with sem.block() as block:
                @block.gpsimd
                def _(pool):
                    with pool.Fori(0, NT) as i:
                        pool.wait_ge(s_t.sem, i + 1)
                        pool.tensor_copy(xin, X[:, bass.ds(i, 1), :]).then_inc(s_here.sem, 1)

                @block.tensor
                def _(pe):
                    pe.sem_inc(s_t.sem, 1)
                    with pe.Fori(0, NT) as i:
                        pe.wait_ge(s_here.sem, i + 1)
                        pe.transpose(PS[:, 4, 0:P], xin.rearrange("p a d -> p (a d)"), ident[:, :]).then_inc(s_t.sem, 1)
                        pe.wait_ge(s_tc.sem, i + 1)
                        for n in range(8):
                            pe.wait_ge(s_c[n % 2].sem, i * 4 + n // 2 + 1)
                            pe.matmul(PS[:, n % 2 + 2 * (n // 2 % 2), :], xT, WRF[:, n * 512:(n + 1) * 512],
                                      start=True, stop=True).then_inc(s_pe.sem, 1)

                def copies(eng, copy, h):
                    eng.sem_inc(s_c[h].sem, 2)
                    with eng.Fori(0, NT) as i:
                        if h == 1:
                            eng.wait_ge(s_t.sem, i + 2)
                            copy(xT, PS[:, 4, 0:P]).then_inc(s_tc.sem, 1)
                        for n in range(h, 8, 2):
                            m = n // 4
                            eng.wait_ge(s_stored.sem, i * 2 + m + 1)
                            eng.wait_ge(s_pe.sem, i * 8 + n + 1)
                            copy(stages[m][:, n % 4, :], PS[:, n % 2 + 2 * (n // 2 % 2), :]).then_inc(s_c[h].sem, 1)

                @block.vector
                def _(dve):
                    copies(dve, dve.tensor_copy, 0)

                @block.scalar
                def _(act):
                    copies(act, lambda o, i: act.activation(o, i, ACT.Copy), 1)

                @block.sync
                def _(sp):
                    sp.sem_inc(s_stored.sem, 2)
                    with sp.Fori(0, NT) as i:
                        for m in range(2):
                            for h in range(2):
                                sp.wait_ge(s_c[h].sem, i * 4 + (2 * m + 4))
                            sp.dma_start(target[bass.ds(i, 1), :, m * 2048:(m + 1) * 2048].rearrange("t p o -> (t p) o"),
                                         stages[m].rearrange("p a o -> p (a o)")).then_inc(s_st[m].sem, 16)
                        for m in range(2):
                            sp.wait_ge(s_st[m].sem, i * 16 + 16)
                            sp.sem_inc(s_stored.sem, 1)

            project("l2p", X, LQ + D, LQ, None, [(LQ, LQ + D, d_kn)])
            scores("l2s", "rules", d_kn, D, LQ)
            turn("l2ta", LAF, XT)
            softmax("l2x", cK, whole_k, 0.0, float(D) ** -0.5)
            turn("l2tb", XT, LAF)

            ROW2 = over(FW, 3200, [3, D])
            sem = Phase()
            s_l, s_v = sem("l2m_l"), sem("l2m_v")
            with sem.block() as block:
                @block.vector
                def _(dve):
                    al = ALPHA.rearrange("p (g c) -> p g c", c=C)
                    s_v.link(dve, dve.tensor_reduce(al, LA[:, :, :, 0:4], AX.X, ALU.add))
                    s_v.inc(dve.tensor_scalar(al, al, 0.25, None, ALU.mult))
                    s_v.inc(dve.memset(ACC[:, :, :], 0.0))

            aggregate("l2g", dlm, 0, d_proj)

            sem = Phase()
            s_l, s_v, s_a = sem("l2f_l"), sem("l2f_v"), sem("l2f_a")
            norms = Norms(s_v, s_a)
            H = ACC[:, :, 0:D]
            with sem.block() as block:
                @block.sync
                def _(sp):
                    for n, w in enumerate(("bias", "ln_gamma", "ln_beta")):
                        s_l.inc(sp.dma_start(ROW2[:, n, :], rows_of("L2_gnn_" + w)), 16)

                @block.vector
                def _(dve):
                    dve.wait_ge(s_l.sem, 48)
                    s_v.link(dve, dve.tensor_tensor(H, H, bc(ROW2[:, 0, :], 1, NT), ALU.add))
                    norms.norm(dve, H, over(FW, 0, [NT, D]), ROW2[:, 1, :], ROW2[:, 2, :])
                    s_v.link(dve, dve.tensor_scalar(H, H, 0.0, None, ALU.max))
                    s_v.link(dve, dve.tensor_tensor(X[:, :, :], X[:, :, :], H, ALU.add))
                    norms.norm(dve, X[:, :, :], over(FW, 0, [NT, D]))

                @block.scalar
                def _(act):
                    norms.roots(act)

        def gatv2(n, src, final):
            tag = f"l3{n}"
            sem = Phase()
            s_l, s_v = sem(tag + "w_l"), sem(tag + "w_v")
            with sem.block() as block:
                @block.sync
                def _(sp):
                    s_l.inc(sp.dma_start(WCAT[:, 0:D], A[f"L3_gnn_W{n}_r"][:, :]), 16)
                    s_l.inc(sp.dma_start(WCAT[:, D:2 * D], A[f"L3_gnn_W{n}_l"][:, :]), 16)
                    s_l.wait(sp)

                @block.vector
                def _(dve):
                    s_v.inc(dve.memset(BIAS, 0.0))

            project(tag + "p", src, 2 * D, D, None, [(D, 2 * D, d_xl)])

            sem = Phase()
            s_l = sem(tag + "a_l")
            with sem.block() as block:
                @block.sync
                def _(sp):
                    s_l.inc(sp.dma_start(ATTW, A[f"L3_gnn_att{n}"].rearrange("h c -> (h c)").rearrange("(a m) -> a m", a=1)
                                         .to_broadcast([P, D])), 16)
                    s_l.wait(sp)

            scores(tag + "s", "gatv2", d_xl, D, D)
            turn(tag + "ta", LAF, XT)
            softmax(tag + "x", cD, whole_d, 1e-16, 1.0)
            turn(tag + "tb", XT, LAF)

            sem = Phase()
            s_v = sem(tag + "z_v")
            with sem.block() as block:
                @block.vector
                def _(dve):
                    s_v.inc(dve.memset(ACC[:, :, :], 0.0))

            aggregate(tag + "g", dl, 4, None)

            ROW1 = over(FW, 3200, [D])
            sem = Phase()
            s_l, s_v, s_a = sem(tag + "f_l"), sem(tag + "f_v"), sem(tag + "f_a")
            norms = Norms(s_v, s_a)
            H = ACC[:, :, 0:D]
            with sem.block() as block:
                @block.sync
                def _(sp):
                    s_l.inc(sp.dma_start(ROW1, rows_of(f"L3_gnn_b{n}")), 16)
                    s_l.wait(sp)
                    if final:
                        sp.wait_ge(s_v.sem, at.final)
                        s_l.inc(sp.dma_start(out[0:(NT - 1) * P, :].rearrange("(t p) d -> p t d", p=P), X[:, 0:NT - 1, :]), 16)
                        s_l.inc(sp.dma_start(out[(NT - 1) * P:N, :], X[0:NLAST, NT - 1, :]), 16)
                        s_l.wait(sp)

                at.final = 11

                @block.vector
                def _(dve):
                    dve.wait_ge(s_l.sem, 16)
                    s_v.link(dve, dve.tensor_tensor(H, H, bc(ROW1, 1, NT), ALU.add))
                    if final:
                        s_v.link(dve, dve.tensor_scalar(H, H, 0.0, None, ALU.max))
                        s_v.link(dve, dve.tensor_tensor(X[:, :, :], X[:, :, :], H, ALU.add))
                        norms.norm(dve, X[:, :, :], over(FW, 0, [NT, D]))
                        assert s_v.n == at.final
                    else:
                        s_v.inc(dve.tensor_scalar(HID, H, 0.0, None, ALU.max))

                @block.scalar
                def _(act):
                    norms.roots(act)

        constants()
        records_by_src()
        sort_pass("ss", ECOL, 7, 5, NT, d_slist, sbt, 1)
        source_tables()
        layer0()
        records_by_dst()
        sort_pass("s0", ACOL, 0, 6, TYPES + 1, d_pass[0], None, 0)
        load_records("r0", d_pass[0])
        sort_pass("s1", ACOL, 6, 6, 64, d_pass[1], None, 0)
        load_records("r1", d_pass[1])
        sort_pass("s2", ACOL, 12, 6, 2 * NT, d_list, bt, 2)
        LIST = over(XT, 0, [C, G, 4], I32)
        keys("kk", LIST, 0, True)
        turn("kt", TT, LAF)
        flags("kf", cK, whole_k)
        keys("dk", LIST, 6, False)
        turn("dt", TT, LAF)
        flags("df", cD, whole_d)
        layer1()
        layer2()
        gatv2(1, X, False)
        gatv2(2, HID, True)


_OUTS = [((N, D), "float32")]


def kernel(**inputs):
    import numpy as np
    import concourse.bacc as bacc
    from concourse.bass_utils import run_bass_kernel_spmd

    nc = bacc.Bacc("TRN2", target_bir_lowering=False, num_devices=1)
    arrays, aps = {}, {}
    for name, a in inputs.items():
        a = np.ascontiguousarray(a)
        arrays[f"in_{name}"] = a
        aps[name] = nc.dram_tensor(f"in_{name}", a.shape, mybir.dt.from_np(a.dtype), kind="ExternalInput").ap()
    out = nc.dram_tensor("out_x", (N, D), F32, kind="ExternalOutput").ap()
    gnn_kernel(nc, aps, out)
    r = run_bass_kernel_spmd(nc, [arrays], core_ids=[0])
    return r.results[0]["out_x"]
```

```python
import concourse.bass as bass
from concourse import mybir
from contextlib import ExitStack, contextmanager

F32, BF16 = mybir.dt.float32, mybir.dt.bfloat16
I32, U32, U16, U8 = mybir.dt.int32, mybir.dt.uint32, mybir.dt.uint16, mybir.dt.uint8
ALU = mybir.AluOpType
ACT = mybir.ActivationFunctionType
AX = mybir.AxisListType
ENG = mybir.EngineType

P = 128
N, E, D = 3125, 100000, 128
NT = (N + P - 1) // P
NPAD = NT * P
NLAST = N - (NT - 1) * P
RELS, TYPES = 500, 32
ED = 64
ROWS = 125
ECOL, NCOL = E // ROWS, N // ROWS
ACOL = ECOL + NCOL
ALL = E + N
U = 4
C = 16
HD = 8
G = -(-(ALL // P + NT) // C)
SLOTS = G * C * P
SEQ = G * P
EG = -(-(E // P + NT) // C)
ESLOTS = EG * C * P
NIL = 4095
BIG = 1.0e30
NEG = 256.0
STEPS = C // U
W0 = 130
LQ = 164


class Count:

    def __init__(self, sem):
        self.sem, self.n = sem, 0

    def inc(self, ins, k=1):
        ins.then_inc(self.sem, k)
        self.n += k

    def wait(self, eng):
        eng.wait_ge(self.sem, self.n)

    def link(self, eng, ins):
        self.inc(ins)
        self.wait(eng)


class Marks:
    pass


class Step:

    def __init__(self, count, i, per):
        self.count, self.i, self.per, self.k = count, i, per, 0

    def inc(self, ins):
        ins.then_inc(self.count.sem, 1)
        self.k += 1

    def wait(self, eng):
        eng.wait_ge(self.count.sem, self.i * self.per + (self.count.n + self.k))

    def link(self, eng, ins):
        self.inc(ins)
        self.wait(eng)

    def wait_for(self, eng, k):
        eng.wait_ge(self.count.sem, self.i * self.per + (self.count.n + k))

    def end(self, turns):
        assert self.k == self.per, (self.k, self.per)
        self.count.n += turns * self.per


def bc(ap, axis, n):
    u = ap.unsqueeze(axis)
    shape = list(u.shape)
    shape[axis] = n
    return u.to_broadcast(shape)


def gnn_kernel(nc, A, out):
    ctx = ExitStack()
    with ctx:
        nc_dram = lambda name, shape, dt=F32: nc.dram_tensor("scr_" + name, shape, dt, kind="Internal")

        def sb(name, shape, dt=F32):
            return ctx.enter_context(nc.sbuf_tensor("sb_" + name, shape, dt))

        moved = [Count(ctx.enter_context(nc.semaphore(f"rows_moved{k}"))) for k in range(5)]

        class Phase:

            def __init__(self):
                self.stack, self.counts = ExitStack(), []

            def rows_moved(self, n):
                return moved[:n]

            def __call__(self, name):
                self.counts.append(Count(self.stack.enter_context(nc.semaphore(name))))
                return self.counts[-1]

            @contextmanager
            def block(self):
                with nc.Block() as block:
                    yield block
                with nc.Block() as block:
                    @block.sync
                    def _(sp):
                        for c in self.counts:
                            sp.sem_clear(c.sem)
                self.stack.close()

        d_pass = [nc_dram(f"pass{i}", [ALL, 4], I32) for i in range(2)]
        d_list = nc_dram("list", [SLOTS, 4], I32)
        d_slist = nc_dram("slist", [ESLOTS, 4], I32)
        d_dst = nc_dram("tab_dst", [NPAD, W0])
        d_rel = nc_dram("tab_rel", [RELS, W0])
        d_kv = nc_dram("tab_kv", [NPAD, 2 * D])
        d_kn = nc_dram("tab_kn", [NPAD, D])
        d_xl = nc_dram("tab_xl", [NPAD, D])
        d_proj = nc_dram("tab_proj", [NPAD * TYPES, D])
        d_spill = nc_dram("spill", [G, P, C, D])

        X = sb("x", [P, NT, D])
        ACC = sb("acc", [P, NT, W0])
        QT = sb("qt", [P, NT * LQ])
        ident = sb("ident", [P, P])
        ident16 = sb("ident16", [P, P], BF16)
        iota = sb("iota", [P, P])
        iota16 = sb("iota16", [P, P], BF16)
        ones = sb("ones", [P, P])
        lower = sb("lower", [P, P])
        up8 = sb("up8", [P, P])
        down8 = sb("down8", [P, P])
        src_i = sb("src_i", [P, G * C + C], U32)
        eid_i = sb("eid_i", [P, G * C + C], U32)
        prj_i = sb("prj_i", [P, G * C + C], U32)
        dl = sb("dl", [P, G * C + 2 * U], BF16)
        dlm = sb("dlm", [P, G * C + U], BF16)
        typ = sb("typ", [P, G * C], BF16)
        bt = sb("bt", [1, G * C + U], I32)
        sbt = sb("sbt", [1, EG * C + U], I32)
        sdl = sb("sdl", [P, EG * C + 2 * U], BF16)
        cD = sb("cD", [P, SEQ + 1], U8)
        cK = sb("cK", [P, SEQ + 1], U8)
        LA = sb("la", [P, G, C, HD])
        XT = sb("xt", [P, SEQ])
        FW = sb("fw", [P, SEQ])
        TT = sb("tt", [P, SEQ])
        PS = ctx.enter_context(nc.psum_tensor("psum", [P, 8, 512], F32))

        def over(buf, at, shape, dt=F32, parts=P):
            n = 1
            for s in shape:
                n *= s
            if dt in (BF16, U16):
                v = buf[0:parts, at:at + (n + 1) // 2].bitcast(dt)[:, 0:n]
            else:
                v = buf[0:parts, at:at + n]
                if dt != F32:
                    v = v.bitcast(dt)
            if len(shape) == 1:
                return v
            names = "abcd"[:len(shape)]
            sizes = {m: s for m, s in zip(names[1:], shape[1:])}
            return v.rearrange(f"p ({' '.join(names)}) -> p {' '.join(names)}", **sizes)

        def constants():
            sem = Phase()
            s_x, s_p, s_v = sem("c_x"), sem("c_pool"), sem("c_vec")
            with sem.block() as block:
                @block.vector
                def _(dve):
                    s_v.link(dve, dve.memset(X[:, NT - 1, :], 0.0))
                    s_v.inc(dve.memset(ones[:, :], 1.0))
                    s_v.inc(dve.memset(LA[:, :, :, :], 0.0))
                    for index in (src_i, eid_i, prj_i):
                        s_v.inc(dve.memset(index[:, :], 0))
                    dve.wait_ge(s_p.sem, 9)
                    s_v.inc(dve.tensor_copy(ident16[:, :], ident[:, :]))
                    s_v.inc(dve.tensor_copy(iota16[:, :], iota[:, :]))

                @block.gpsimd
                def _(pool):
                    s_p.inc(pool.memset(ident[:, :], 0.0))
                    s_p.inc(pool.iota(iota[:, :], [[1, P]], base=0, channel_multiplier=0,
                                      allow_small_or_imprecise_dtypes=True))
                    s_p.inc(pool.memset(lower[:, :], 1.0))
                    s_p.inc(pool.memset(up8[:, :], 0.0))
                    s_p.inc(pool.memset(down8[:, :], 0.0))
                    s_p.wait(pool)
                    for t, base in ((ident, 0), (up8, HD), (down8, -HD)):
                        s_p.inc(pool.affine_select(out=t[:, :], in_=t[:, :], compare_op=ALU.not_equal,
                                                   fill=1.0, base=base, pattern=[[-1, P]], channel_multiplier=1))
                    s_p.inc(pool.affine_select(out=lower[:, :], in_=lower[:, :], compare_op=ALU.is_ge,
                                               fill=0.0, base=-1, pattern=[[1, P]], channel_multiplier=-1))

                @block.sync
                def _(sp):
                    sp.wait_ge(s_v.sem, 1)
                    s_x.inc(sp.dma_start(X[:, 0:NT - 1, :],
                                         A["x"][0:(NT - 1) * P, :].rearrange("(t p) d -> p t d", p=P)), 16)
                    s_x.inc(sp.dma_start(X[0:NLAST, NT - 1, :], A["x"][(NT - 1) * P:N, :]), 16)
                    s_x.wait(sp)

        REC = lambda cols: over(XT, 0, [cols, 4], I32, ROWS)

        def records_by_dst():
            sem = Phase()
            s_l, s_v, s_p = sem("rd_l"), sem("rd_v"), sem("rd_p")
            rec = REC(ACOL)
            raw = [over(FW, i * ECOL, [ECOL], I32, ROWS) for i in range(3)]
            tmp = over(FW, 3 * ECOL, [ECOL], I32, ROWS)
            with sem.block() as block:
                @block.sync
                def _(sp):
                    for t, name in zip(raw, ("dst", "edge_type_32", "src")):
                        s_l.inc(sp.dma_start(t, A[name].rearrange("(p c) -> p c", p=ROWS)), 16)

                @block.gpsimd
                def _(pool):
                    s_p.inc(pool.iota(rec[:, 0:ECOL, 2], [[1, ECOL]], base=0, channel_multiplier=ECOL))
                    s_p.inc(pool.memset(rec[:, ECOL:ACOL, 2], 0))
                    s_p.inc(pool.iota(rec[:, ECOL:ACOL, 1], [[1, NCOL]], base=0, channel_multiplier=NCOL))
                    s_p.inc(pool.memset(rec[:, ECOL:ACOL, 3], 0))
                    s_p.inc(pool.iota(rec[:, ECOL:ACOL, 0], [[64, NCOL]], base=TYPES, channel_multiplier=64 * NCOL))

                @block.vector
                def _(dve):
                    dve.wait_ge(s_l.sem, 48)
                    s_v.inc(dve.tensor_scalar(tmp, raw[0], 64.0, None, ALU.mult))
                    s_v.inc(dve.tensor_copy(rec[:, 0:ECOL, 1], raw[2]))
                    s_v.wait(dve)
                    s_v.link(dve, dve.scalar_tensor_tensor(rec[:, 0:ECOL, 0], raw[0], 64.0, raw[1], ALU.mult, ALU.add))
                    s_v.inc(dve.scalar_tensor_tensor(rec[:, 0:ECOL, 3], raw[2], float(TYPES), raw[1], ALU.mult, ALU.add))

        def records_by_src():
            sem = Phase()
            s_l, s_v = sem("rs_l"), sem("rs_v")
            rec = REC(ECOL)
            raw = [over(FW, i * ECOL, [ECOL], I32, ROWS) for i in range(3)]
            with sem.block() as block:
                @block.sync
                def _(sp):
                    for t, name in zip(raw, ("src", "dst", "edge_type_500")):
                        s_l.inc(sp.dma_start(t, A[name].rearrange("(p c) -> p c", p=ROWS)), 16)

                @block.vector
                def _(dve):
                    dve.wait_ge(s_l.sem, 48)
                    for w in range(3):
                        s_v.inc(dve.tensor_copy(rec[:, 0:ECOL, w], raw[w]))
                    s_v.inc(dve.memset(rec[:, 0:ECOL, 3], 0))

        def sort_pass(tag, cols, shift, bits, bins, target, into, bucket):
            sem = Phase()
            s_v, s_pe, s_pool, s_init = sem(tag + "_v"), sem(tag + "_pe"), sem(tag + "_pool"), sem(tag + "_init")
            s_slot = sem.rows_moved(5)
            s_gate, s_gate2, s_ring = sem(tag + "_gate"), sem(tag + "_gate2"), sem(tag + "_ring")
            rec = REC(cols)
            key, pos = over(FW, 0, [cols], I32, ROWS), over(FW, ACOL, [cols], F32, ROWS)
            run = [over(FW, (2 + h) * ACOL, [cols], F32, ROWS) for h in range(2)]
            dig = over(FW, 4 * ACOL, [cols], BF16, ROWS)
            mask = [over(FW, (5 + h) * ACOL, [cols], U16, ROWS) for h in range(2)]
            unit = over(TT, 0, [cols], F32, ROWS)
            small = [over(TT, ACOL + 64 * i, [64], F32, ROWS) for i in range(4)]
            cnt, off, tot, beg = small
            pair = over(TT, ACOL + 256, [64], F32, ROWS)
            pair_i = over(TT, ACOL + 320, [64], I32, ROWS)
            pos_i = over(TT, 2 * ACOL, [cols], I32, ROWS)
            ring_pos = over(TT, 3 * ACOL, [5, 5], I32, ROWS)
            ring_rec = over(TT, 3 * ACOL + 32, [5, 5, 4], I32, ROWS)
            tile_no = over(TT, 4 * ACOL, [G * C], F32, 1)
            tiles = over(TT, 4 * ACOL + G * C, [G * C], F32, 1)
            nil = over(LA[:, :, :, :].rearrange("p a b c -> p (a b c)"), 0, [G * C, 4], I32)
            slots = 0 if not bucket else target.shape[0]
            pairs = (bins + 1) // 2
            at = Marks()

            with sem.block() as block:
                if bucket:
                    @block.sync
                    def _(sp):
                        sp.wait_ge(s_v.sem, 2)
                        s_init.inc(sp.dma_start(target[:, :].rearrange("(p c) w -> p c w", p=P),
                                                nil[:, 0:slots // P, :]), 16)
                        s_init.wait(sp)

                @block.vector
                def _(dve):
                    if bucket:
                        s_v.link(dve, dve.memset(nil[:, :, :], 0))
                        s_v.link(dve, dve.memset(nil[:, :, 0], NIL << shift if bucket == 1 else NIL << 6))
                    s_v.link(dve, dve.tensor_scalar(key, rec[:, :, 0], shift, (1 << bits) - 1,
                                                    ALU.logical_shift_right, ALU.bitwise_and))
                    s_v.inc(dve.tensor_copy(dig, key))
                    s_v.inc(dve.memset(unit, 1.0))
                    s_v.inc(dve.memset(cnt, 0.0))
                    s_v.inc(dve.memset(pos, 0.0))
                    s_v.wait(dve)
                    with dve.Fori(0, pairs) as i:
                        t = Step(s_v, i, 2)
                        for h in range(2):
                            b = i * 2 + h
                            t.wait_for(dve, h - 1)
                            t.inc(dve.tensor_scalar(mask[h], dig, iota[0:ROWS, bass.ds(b, 1)], None,
                                                    ALU.is_equal, ALU.add, accum_out=cnt[:, bass.ds(b, 1)]))
                    t.end(pairs)
                    s_v.wait(dve)
                    at.counted = s_v.n
                    dve.wait_ge(s_pe.sem, 2)
                    s_v.link(dve, dve.tensor_copy(tot, PS[0:ROWS, 1, 0:64]))
                    if bucket:
                        nb = bins // bucket
                        if bucket == 2:
                            even, odd = (tot.rearrange("p (a b) -> p b a", b=2)[:, i, 0:nb] for i in range(2))
                            s_v.link(dve, dve.tensor_tensor(pair[:, 0:nb], even, odd, ALU.add))
                        else:
                            s_v.link(dve, dve.tensor_copy(pair[:, 0:nb], tot[:, 0:nb]))
                        s_v.link(dve, dve.tensor_scalar(pair[:, 0:nb], pair[:, 0:nb], float(P - 1), None, ALU.add))
                        s_v.link(dve, dve.tensor_copy(pair_i[:, 0:nb], pair[:, 0:nb]))
                        s_v.link(dve, dve.tensor_scalar(pair_i[:, 0:nb], pair_i[:, 0:nb], 7, 7,
                                                        ALU.logical_shift_right, ALU.logical_shift_left))
                        s_v.link(dve, dve.tensor_copy(pair[:, 0:nb], pair_i[:, 0:nb]))
                        s_v.link(dve, dve.tensor_tensor_scan(off[:, 0:nb], unit[:, 0:nb], pair[:, 0:nb], 0.0,
                                                             ALU.mult, ALU.add))
                        s_v.link(dve, dve.tensor_tensor(off[:, 0:nb], off[:, 0:nb], pair[:, 0:nb], ALU.subtract))
                        if bucket == 2:
                            b_even, b_odd = (beg.rearrange("p (a b) -> p b a", b=2)[:, i, 0:nb] for i in range(2))
                            s_v.inc(dve.tensor_copy(b_even, off[:, 0:nb]))
                            s_v.inc(dve.tensor_tensor(b_odd, off[:, 0:nb], even, ALU.add))
                            s_v.wait(dve)
                        else:
                            s_v.link(dve, dve.tensor_copy(beg[:, 0:nb], off[:, 0:nb]))
                        s_v.link(dve, dve.tensor_scalar(pair[:, 0:nb], off[:, 0:nb], 1.0 / P, None, ALU.mult))
                        s_v.link(dve, dve.memset(tiles, -1.0))
                        nt = (G if into is bt else EG) * C
                        dve.wait_ge(s_pool.sem, 1)
                        for b in range(nb):
                            s_v.link(dve, dve.scalar_tensor_tensor(tiles[:, 0:nt], tile_no[:, 0:nt], pair[0:1, b:b + 1],
                                                                   tiles[:, 0:nt], ALU.is_ge, ALU.add))
                        s_v.inc(dve.memset(into[:, :], 0))
                        s_v.wait(dve)
                        s_v.link(dve, dve.tensor_copy(into[:, 0:nt], tiles[:, 0:nt]))
                    else:
                        s_v.link(dve, dve.tensor_tensor_scan(beg[:, 0:bins], unit[:, 0:bins], tot[:, 0:bins], 0.0,
                                                             ALU.mult, ALU.add))
                        s_v.link(dve, dve.tensor_tensor(beg[:, 0:bins], beg[:, 0:bins], tot[:, 0:bins], ALU.subtract))
                    if bins % 2:
                        s_v.link(dve, dve.memset(beg[:, bins:bins + 1], 0.0))
                    s_v.link(dve, dve.scalar_tensor_tensor(off[:, 0:2 * pairs], beg[:, 0:2 * pairs], -1.0,
                                                           PS[0:ROWS, 0, 0:2 * pairs],
                                                           ALU.add, ALU.add))
                    with dve.Fori(0, pairs) as i:
                        t = Step(s_v, i, 6)
                        for h in range(2):
                            t.wait_for(dve, h - 1)
                            t.inc(dve.tensor_scalar(mask[h], dig, iota[0:ROWS, bass.ds(i * 2 + h, 1)], None, ALU.is_equal))
                        for h in range(2):
                            t.wait_for(dve, 1 + h)
                            t.inc(dve.tensor_tensor_scan(run[h], unit, mask[h], off[:, bass.ds(i * 2 + h, 1)],
                                                         ALU.mult, ALU.add))
                        for h in range(2):
                            t.wait_for(dve, 3 + 2 * h)
                            dve.sem_inc(s_gate.sem, 1)
                            t.inc(dve.copy_predicated(pos, mask[h], run[h]))
                    t.end(pairs)
                    s_v.wait(dve)
                    s_v.link(dve, dve.tensor_copy(pos_i, pos))
                    s_v.wait(dve)

                    def fill(i, k):
                        dve.tensor_copy(ring_pos[:, k, :], pos_i[:, bass.ds(i * 25 + k * 5, 5)])
                        dve.tensor_copy(ring_rec[:, k, :, :], rec[:, bass.ds(i * 25 + k * 5, 5), :]).then_inc(s_ring.sem, 1)

                    for k in range(5):
                        fill(0, k)
                    with dve.Fori(1, cols // 25) as i:
                        for k in range(5):
                            dve.wait_ge(s_slot[k].sem, i * 80 + s_slot[k].n)
                            fill(i, k)

                @block.tensor
                def _(pe):
                    pe.wait_ge(s_v.sem, at.counted)
                    s_pe.inc(pe.matmul(PS[0:ROWS, 0, 0:64], lower[0:ROWS, 0:ROWS], cnt, start=True, stop=True))
                    s_pe.inc(pe.matmul(PS[0:ROWS, 1, 0:64], ones[0:ROWS, 0:ROWS], cnt, start=True, stop=True))

                @block.gpsimd
                def _(pool):
                    if bucket:
                        if into is bt:
                            s_pool.inc(pool.iota(tile_no[:, 0:G * C], [[1, G], [G, C]], base=0, channel_multiplier=0,
                                                 allow_small_or_imprecise_dtypes=True))
                        else:
                            s_pool.inc(pool.iota(tile_no[:, 0:EG * C], [[1, EG * C]], base=0, channel_multiplier=0,
                                                 allow_small_or_imprecise_dtypes=True))
                        pool.wait_ge(s_init.sem, 16)
                    with pool.Fori(0, cols // 25) as i:
                        for k in range(5):
                            pool.wait_ge(s_ring.sem, i * 5 + k + 1)
                            pool.sem_inc(s_gate2.sem, 1)
                            for j in range(5):
                                pool.indirect_dma_start(
                                    out=target[:, :], out_offset=bass.IndirectOffsetOnAxis(
                                        ap=ring_pos[:, k, j:j + 1].bitcast(U32), axis=0),
                                    in_=ring_rec[:, k, j, :], in_offset=None).then_inc(s_slot[k].sem, 16)
                    for k in range(5):
                        s_slot[k].n += 80 * (cols // 25)
                        s_slot[k].wait(pool)

        def load_records(tag, source):
            sem = Phase()
            s_l = sem(tag + "_l")
            with sem.block() as block:
                @block.sync
                def _(sp):
                    s_l.inc(sp.dma_start(REC(ACOL), source[:, :].rearrange("(p c) w -> p c w", p=ROWS)), 16)
                    s_l.wait(sp)

        LAF = LA[:, :, :, :].rearrange("p g c h -> p (g c h)")

        PLACE = sb("place", [P, 2, 2 * P])

        def turn(tag, src, dst):
            sem = Phase()
            s_turned = [sem(f"{tag}_turned{h}") for h in range(2)]
            s_copied = [sem(f"{tag}_copied{h}") for h in range(2)]
            s_here = [sem(f"{tag}_here{h}") for h in range(2)]
            with sem.block() as block:
                @block.gpsimd
                def _(pool):
                    for h in range(2):
                        pool.sem_inc(s_here[h].sem, 1)
                    with pool.Fori(0, G // 4) as i:
                        for h in range(2):
                            pool.wait_ge(s_turned[h].sem, i + 1)
                            pool.tensor_copy(PLACE[:, h, :], src[:, bass.ds((i * 4 + 2 * h) * P, 2 * P)])\
                                .then_inc(s_here[h].sem, 1)

                @block.tensor
                def _(pe):
                    for h in range(2):
                        pe.sem_inc(s_turned[h].sem, 1)
                    with pe.Fori(0, G // 4) as i:
                        for h in range(2):
                            pe.wait_ge(s_copied[h].sem, i + 1)
                            pe.wait_ge(s_here[h].sem, i + 2)
                            for j in range(2):
                                m = pe.transpose(PS[:, h, j * P:(j + 1) * P], PLACE[:, h, j * P:(j + 1) * P], ident[:, :])
                            m.then_inc(s_turned[h].sem, 1)

                @block.scalar
                def _(act):
                    act.sem_inc(s_copied[0].sem, 1)
                    with act.Fori(0, G // 4) as i:
                        act.wait_ge(s_turned[0].sem, i + 2)
                        act.activation(dst[:, bass.ds(i * 4 * P, 2 * P)], PS[:, 0, 0:2 * P], ACT.Copy)\
                           .then_inc(s_copied[0].sem, 1)

                @block.vector
                def _(dve):
                    dve.sem_inc(s_copied[1].sem, 1)
                    with dve.Fori(0, G // 4) as i:
                        dve.wait_ge(s_turned[1].sem, i + 2)
                        dve.tensor_copy(dst[:, bass.ds(i * 4 * P + 2 * P, 2 * P)], PS[:, 1, 0:2 * P])\
                           .then_inc(s_copied[1].sem, 1)

        def keys(tag, rec, shift, first):
            sem = Phase()
            s_l, s_v = sem(tag + "_l"), sem(tag + "_v")
            keyf, tmp = over(FW, 0, [G, C]), over(FW, 2 * G * C, [G, C])
            keyi = over(FW, G * C, [G, C], I32)
            rep = over(TT, 0, [G, C, HD])
            by_group = rec.rearrange("p c g w -> p w g c")
            gc = lambda t: t[:, 0:G * C].rearrange("p (g c) -> p g c", c=C)
            with sem.block() as block:
                if first:
                    @block.sync
                    def _(sp):
                        for c in range(C):
                            s_l.inc(sp.dma_start(rec[:, c, :, :], d_list[c * SEQ:(c + 1) * SEQ, :]
                                                 .rearrange("(g p) w -> p g w", p=P)), 16)

                @block.vector
                def _(dve):
                    if first:
                        dve.wait_ge(s_l.sem, 16 * C)
                        for index, w in ((src_i, 1), (eid_i, 2), (prj_i, 3)):
                            s_v.inc(dve.tensor_copy(gc(index), by_group[:, w]))
                        s_v.inc(dve.memset(dl[:, G * C:], NEG))
                        s_v.inc(dve.memset(dlm[:, G * C:], NEG))
                        s_v.inc(dve.tensor_copy(keyf, by_group[:, 0]))
                        s_v.link(dve, dve.tensor_copy(keyi, by_group[:, 0]))
                        s_v.link(dve, dve.tensor_scalar(keyi, keyi, 63, None, ALU.bitwise_and))
                        s_v.link(dve, dve.tensor_copy(gc(typ), keyi))
                        s_v.link(dve, dve.tensor_copy(keyi, by_group[:, 0]))
                        s_v.link(dve, dve.tensor_scalar(keyi, keyi, 6, P - 1, ALU.logical_shift_right, ALU.bitwise_and))
                        s_v.link(dve, dve.tensor_copy(tmp, keyi))
                        s_v.link(dve, dve.tensor_scalar(keyf, keyf, float(NIL * 64), NEG, ALU.is_ge, ALU.mult))
                        s_v.link(dve, dve.tensor_tensor(gc(dl), tmp, keyf, ALU.add))
                        s_v.link(dve, dve.tensor_scalar(tmp, gc(typ), float(TYPES), NEG, ALU.is_equal, ALU.mult))
                        s_v.link(dve, dve.tensor_tensor(gc(dlm), gc(dl), tmp, ALU.add))
                    s_v.link(dve, dve.tensor_copy(keyi, by_group[:, 0]))
                    if shift:
                        s_v.link(dve, dve.tensor_scalar(keyi, keyi, shift, None, ALU.logical_shift_right))
                    s_v.inc(dve.tensor_copy(rep, bc(keyi, 3, HD)))

        def flags(tag, flag, whole):
            sem = Phase()
            s_v, s_pe = sem(tag + "_v"), sem(tag + "_pe")
            with sem.block() as block:
                @block.tensor
                def _(pe):
                    pe.matmul(PS[:, 2, 0:1], up8[:, :], LAF[:, SEQ - 1:SEQ], start=True, stop=True)
                    pe.matmul(PS[:, 2, 1:2], down8[:, :], LAF[:, 0:1], start=True, stop=True).then_inc(s_pe.sem, 1)

                @block.vector
                def _(dve):
                    s_v.inc(dve.tensor_tensor(flag[:, 1:SEQ], LAF[:, 1:SEQ], LAF[:, 0:SEQ - 1], ALU.is_equal))
                    dve.wait_ge(s_pe.sem, 1)
                    s_v.inc(dve.tensor_tensor(flag[:, 0:1], LAF[:, 0:1], PS[:, 2, 0:1], ALU.is_equal))
                    s_v.inc(dve.tensor_tensor(flag[:, SEQ:SEQ + 1], LAF[:, SEQ - 1:SEQ], PS[:, 2, 1:2], ALU.is_equal))
                    s_v.wait(dve)
                    s_v.inc(dve.tensor_reduce(whole[:, 0:1], flag[:, 0:SEQ], AX.X, ALU.min))
                    s_v.inc(dve.tensor_reduce(whole[:, 1:2], flag[:, 1:SEQ + 1], AX.X, ALU.min))

        def source_tables():
            sem = Phase()
            s_l, s_v = sem("st_l"), sem("st_v")
            rec = over(XT, 0, [EG * C, 4], I32)
            keyf, tmp = over(FW, 0, [EG * C]), over(FW, 2 * EG * C, [EG * C])
            keyi = over(FW, EG * C, [EG * C], I32)
            with sem.block() as block:
                @block.sync
                def _(sp):
                    s_l.inc(sp.dma_start(rec, d_slist[:, :].rearrange("(t p) w -> p t w", p=P)), 16)

                @block.vector
                def _(dve):
                    s_v.inc(dve.memset(sdl[:, EG * C:], NEG))
                    dve.wait_ge(s_l.sem, 16)
                    s_v.inc(dve.tensor_copy(SDST[:, 0:EG * C], rec[:, :, 1]))
                    s_v.inc(dve.tensor_copy(SREL[:, 0:EG * C], rec[:, :, 2]))
                    s_v.inc(dve.tensor_copy(keyf, rec[:, :, 0]))
                    s_v.link(dve, dve.tensor_copy(keyi, rec[:, :, 0]))
                    s_v.link(dve, dve.tensor_scalar(keyi, keyi, P - 1, None, ALU.bitwise_and))
                    s_v.link(dve, dve.tensor_copy(tmp, keyi))
                    s_v.link(dve, dve.tensor_scalar(keyf, keyf, float(NIL), NEG, ALU.is_ge, ALU.mult))
                    s_v.inc(dve.tensor_tensor(sdl[:, 0:EG * C], tmp, keyf, ALU.add))

        SDST, SREL = src_i, eid_i

        WCAT = over(TT, 0, [512])
        BIAS = over(TT, 512, [512], F32, 1)
        XT5 = over(TT, 1024, [5, P])
        FIVE = over(TT, 1664, [5, P])
        STAGE = over(FW, 0, [5, 512])
        HID = over(LAF, 0, [NT, D])

        def project(tag, src, width, keep, adds, sends):
            sem = Phase()
            s_t, s_pe, s_a, s_v = sem(tag + "_t"), sem(tag + "_pe"), sem(tag + "_a"), sem(tag + "_v")
            s_st, s_here, s_stored = sem(tag + "_st"), sem(tag + "_here"), sem(tag + "_stored")
            turns, whole = NT // 5, 16 * len(sends)
            qt = QT[:, 0:NT * keep].rearrange("p (t q) -> p t q", q=keep)
            pairs = PS[:, 0:2, :].rearrange("p b d -> p (b d)")
            with sem.block() as block:
                @block.gpsimd
                def _(pool):
                    with pool.Fori(0, turns) as i:
                        pool.wait_ge(s_t.sem, i + 1)
                        pool.tensor_copy(FIVE, src[:, bass.ds(i * 5, 5), :]).then_inc(s_here.sem, 1)

                @block.tensor
                def _(pe):
                    pe.sem_inc(s_t.sem, 1)
                    with pe.Fori(0, turns) as i:
                        pe.wait_ge(s_here.sem, i + 1)
                        for j in range(5):
                            m = pe.transpose(pairs[:, j * P:(j + 1) * P], FIVE[:, j, :], ident[:, :])
                        m.then_inc(s_t.sem, 1)
                        pe.wait_ge(s_a.sem, i + 1)
                        for j in range(5):
                            pe.wait_ge(s_v.sem, i * 5 + 1)
                            pe.matmul(PS[:, 2 + j, 0:width], XT5[:, j, :], WCAT[:, 0:width], start=True, stop=False)
                            pe.matmul(PS[:, 2 + j, 0:width], ones[0:1, :], BIAS[:, 0:width], start=False, stop=True)\
                              .then_inc(s_pe.sem, 1)

                @block.scalar
                def _(act):
                    with act.Fori(0, turns) as i:
                        act.wait_ge(s_t.sem, i + 2)
                        act.activation(XT5.rearrange("p j d -> p (j d)"), pairs[:, 0:5 * P], ACT.Copy)\
                           .then_inc(s_a.sem, 1)

                @block.vector
                def _(dve):
                    dve.sem_inc(s_v.sem, 1)
                    dve.sem_inc(s_stored.sem, 1)
                    with dve.Fori(0, turns) as i:
                        dve.wait_ge(s_stored.sem, i + 1)
                        for j in range(5):
                            dve.wait_ge(s_pe.sem, i * 5 + j + 1)
                            at = bass.ds(i * 5 + j, 1)
                            dve.tensor_copy(qt[:, at, :], PS[:, 2 + j:3 + j, 0:keep])
                            if adds:
                                dve.tensor_tensor(ACC[:, at, 0:D], PS[:, 2 + j:3 + j, adds[0]:adds[1]],
                                                  src[:, at, :], ALU.add)
                            a, b = sends[0][0], sends[-1][1]
                            dve.tensor_copy(STAGE[:, j:j + 1, 0:b - a], PS[:, 2 + j:3 + j, a:b]).then_inc(s_v.sem, 1)

                @block.sync
                def _(sp):
                    base = sends[0][0]
                    with sp.Fori(0, turns) as i:
                        sp.wait_ge(s_v.sem, i * 5 + 6)
                        for a, b, table in sends:
                            sp.dma_start(table[:, :].rearrange("(t p) d -> p t d", p=P)[:, bass.ds(i * 5, 5), :],
                                         STAGE[:, :, a - base:b - base]).then_inc(s_st.sem, 16)
                        sp.wait_ge(s_st.sem, i * whole + whole)
                        sp.sem_inc(s_stored.sem, 1)

        class Norms:

            def __init__(self, s_v, s_a):
                self.s_v, self.s_a, self.asked = s_v, s_a, []
                self.mean, self.var = over(TT, 4096, [NT]), over(TT, 4096 + NT, [NT])

            def norm(self, dve, x, scratch, gamma=None, beta=None):
                v, mean, var = self.s_v, self.mean, self.var
                v.link(dve, dve.tensor_reduce(mean, x, AX.X, ALU.add))
                v.link(dve, dve.tensor_scalar(mean, mean, 1.0 / D, None, ALU.mult))
                v.link(dve, dve.tensor_tensor(x, x, bc(mean, 2, D), ALU.subtract))
                v.link(dve, dve.tensor_tensor(scratch, x, x, ALU.mult))
                v.link(dve, dve.tensor_reduce(var, scratch, AX.X, ALU.add))
                v.link(dve, dve.tensor_scalar(var, var, 1.0 / D, 1e-5, ALU.mult, ALU.add))
                self.asked.append(v.n)
                dve.wait_ge(self.s_a.sem, len(self.asked))
                v.link(dve, dve.reciprocal(var, var))
                v.link(dve, dve.tensor_tensor(x, x, bc(var, 2, D), ALU.mult))
                if gamma is not None:
                    v.link(dve, dve.tensor_tensor(x, x, bc(gamma, 1, NT), ALU.mult))
                    v.link(dve, dve.tensor_tensor(x, x, bc(beta, 1, NT), ALU.add))

            def roots(self, act):
                for n in self.asked:
                    act.wait_ge(self.s_v.sem, n)
                    act.activation(self.var, self.var, ACT.Sqrt).then_inc(self.s_a.sem, 1)

        row_of = lambda name: A[name].rearrange("(a n) -> a n", a=1)
        rows_of = lambda name: row_of(name).to_broadcast([P, D])

        T = STEPS
        RING = over(XT, 0, [T, U, 2 * D])
        RING2 = over(XT, T * U * 2 * D, [T, U, ED])
        IDX = over(XT, T * U * (2 * D + ED), [T, U], U32)
        IDX2 = over(XT, T * U * (2 * D + ED + 1), [T, U], U32)
        OH = over(FW, 0, [2, U, P])
        OH16 = over(FW, 0, [2, U, P], BF16)
        OHT = over(FW, 1024, [2, U, P])
        ATT = over(FW, 2048, [2, U, P], F32, ED)
        SUM = over(FW, 3072, [2, U, D])
        PROD = over(FW, 4096, [2, U, D])
        VOUT = over(TT, 0, [T, U, D])
        WE = over(TT, 2048, [D], F32, ED)
        ATTW = over(TT, 2176, [D])
        TOH = over(TT, 2304, [2, U, TYPES])
        SMALL = over(TT, 2560, [6, U])

        def one_hot(eng, to, labels, at):
            return eng.tensor_tensor(to, bc(iota16[:, :], 1, U), bc(labels[:, bass.ds(at, U)], 2, P), ALU.is_equal)

        def distance(eng, to, labels, at):
            return eng.tensor_tensor(to, bc(iota16[:, :], 1, U), bc(labels[:, bass.ds(at, U)], 2, P), ALU.subtract)

        def ask(dve, idx, rows, at):
            return dve.tensor_copy(idx, rows[:, bass.ds(at, U)])

        def gather(pool, idx, table, ring, s_land):
            for j in range(U):
                pool.indirect_dma_start(out=ring[:, j, :], out_offset=None, in_=table,
                                        in_offset=bass.IndirectOffsetOnAxis(ap=idx[:, j:j + 1], axis=0))\
                    .then_inc(s_land.sem, 16)

        def tiles_of(eng, which, table, at):
            _, tiles = nc.values_load_multi_w_load_instructions(
                table[0:1, bass.ds(at, C)], engines=(which,), min_val=0, max_val=NT - 1,
                skip_runtime_bounds_check_because="the sort writes tile numbers below NT")
            return tiles

        def scores(tag, kind, table, width, qw):
            mha, rules, gat = kind == "mha", kind == "rules", kind == "gatv2"
            sem = Phase()
            s_done = sem(tag + "_done")
            s_gate, s_gate2 = sem(tag + "_gate"), sem(tag + "_gate2")
            s_land = sem.rows_moved(T)
            s_spill, s_stored = [sem(f"{tag}_spill{k}") for k in range(T)], sem(tag + "_stored")
            s_oh, s_ohT, s_ohc, s_q = (sem(tag + x) for x in ("_oh", "_ohT", "_ohc", "_q"))
            s_v, s_at, s_atc, s_e = sem(tag + "_v"), sem(tag + "_at"), sem(tag + "_atc"), sem(tag + "_e")
            qt = QT[:, 0:NT * qw].rearrange("p (t q) -> p t q", q=qw)
            gathers = 2 if mha else 1
            landed = 16 * U * gathers
            ops = {"mha": 3, "rules": 6, "gatv2": 3}[kind]

            def turned(b):
                return PS[:, b, 0:U * P // 2].bitcast(BF16).rearrange("p (a d) -> p a d", d=P)

            def qps(b):
                if rules:
                    return PS[:, 2 + 2 * b:4 + 2 * b, :].rearrange("p b (a d) -> p (b a) d", d=256)
                return PS[:, 2 + b, :].rearrange("p (a d) -> p a d", d=D)

            with sem.block() as block:
                @block.gpsimd
                def _(pool):
                    with pool.Fori(0, G) as i:
                        for k in range(T):
                            if gat:
                                pool.wait_ge(s_stored.sem, i * T + k + 1)
                            pool.wait_ge(s_done.sem, i * T + k + 1)
                            pool.sem_inc(s_gate.sem, 1)
                            gather(pool, IDX[:, k, :], table[:, :], RING[:, k, :, 0:width], s_land[k])
                            if mha:
                                gather(pool, IDX2[:, k, :], A["edge_attr_64"][:, :], RING2[:, k, :, :], s_land[k])

                @block.vector
                def _(dve):
                    def ask_step(k, at):
                        if mha:
                            ask(dve, IDX2[:, k, :], eid_i, at)
                        ask(dve, IDX[:, k, :], src_i, at).then_inc(s_done.sem, 1)

                    for k in range(T):
                        ask_step(k, k * U)
                    for b in range(2):
                        one_hot(dve, OH16[:, b, :, :], dl, b * U).then_inc(s_oh.sem, 1)
                    with dve.Fori(0, G) as i:
                        t = Step(s_v, i, T * ops)
                        for k in range(T):
                            b = k % 2
                            dve.wait_ge(s_ohT.sem, i * T + k + 1)
                            one_hot(dve, OH16[:, b, :, :], dl, i * C + (k + 2) * U).then_inc(s_oh.sem, 1)
                            dve.wait_ge(s_land[k].sem, i * landed + (s_land[k].n + landed))
                            dve.wait_ge(s_q.sem, i * T + k + 1)
                            q = qps(b)
                            la = LA[:, bass.ds(i, 1), k * U:(k + 1) * U, :].rearrange("p g u h -> p (g u) h")
                            x = RING[:, k, :, 0:D]
                            if mha:
                                dve.wait_ge(s_e.sem, i * T + k + 1)
                                edge = PS[:, 4 + b, :].rearrange("p (a d) -> p a d", d=D)
                                dve.wait_ge(s_stored.sem, i * T + k + 1)
                                t.inc(dve.tensor_tensor(VOUT[:, k, :, :], RING[:, k, :, D:2 * D], edge, ALU.add))
                                t.link(dve, dve.tensor_tensor(SUM[:, b, :, :], x, edge, ALU.add))
                                t.link(dve, dve.tensor_tensor(PROD[:, b, :, :], SUM[:, b, :, :], q, ALU.mult))
                                dve.tensor_reduce(la, PROD[:, b, :, :].rearrange("p a (h c) -> p a h c", h=HD),
                                                         AX.X, ALU.add)
                            elif gat:
                                t.link(dve, dve.tensor_tensor(SUM[:, b, :, :], x, q, ALU.add))
                                t.link(dve, dve.scalar_tensor_tensor(PROD[:, b, :, :], SUM[:, b, :, :], 0.2,
                                                                     SUM[:, b, :, :], ALU.mult, ALU.max))
                                t.link(dve, dve.tensor_tensor(SUM[:, b, :, :], PROD[:, b, :, :], bc(ATTW, 1, U), ALU.mult))
                                dve.tensor_reduce(la[:, :, 0:4], SUM[:, b, :, :].rearrange("p a (h c) -> p a h c", h=4),
                                                         AX.X, ALU.add)
                            else:
                                base, rel, both = (SMALL[:, 3 * b + n, :] for n in range(3))
                                kinds = bc(typ[:, bass.ds(i * C + k * U, U)], 2, TYPES)
                                t.inc(dve.tensor_tensor(PROD[:, b, :, :], x, q[:, :, 0:D], ALU.mult))
                                t.link(dve, dve.tensor_tensor(TOH[:, b, :, :], bc(iota16[:, 0:TYPES], 1, U), kinds, ALU.is_equal))
                                t.inc(dve.tensor_reduce(base, PROD[:, b, :, :], AX.X, ALU.add))
                                t.link(dve, dve.tensor_tensor(TOH[:, b, :, :], TOH[:, b, :, :], q[:, :, D:D + TYPES], ALU.mult))
                                t.link(dve, dve.tensor_reduce(rel, TOH[:, b, :, :], AX.X, ALU.add))
                                t.link(dve, dve.tensor_tensor(both, base, rel, ALU.add))
                                dve.tensor_tensor(la[:, :, 0:4], bc(both, 2, 4), q[:, :, D + TYPES:LQ], ALU.add)
                            ask_step(k, i * C + (C + k * U))
                    t.end(G)

                @block.tensor
                def _(pe):
                    def turn_one_hots(b):
                        for j in range(U):
                            m = pe.transpose(turned(b)[:, j, :], OH16[:, b, j, :], ident16[:, :])
                        m.then_inc(s_ohT.sem, 1)

                    def products(b, tiles):
                        for j in range(U):
                            m = pe.matmul(qps(b)[:, j, 0:qw], OHT[:, b, j, :],
                                          qt[:, bass.ds(tiles[j], 1), :].rearrange("p a q -> p (a q)"),
                                          start=True, stop=True)
                        m.then_inc(s_q.sem, 1)

                    for b in range(2):
                        pe.wait_ge(s_oh.sem, b + 1)
                        turn_one_hots(b)
                    pe.wait_ge(s_ohc.sem, 1)
                    products(0, tiles_of(pe, ENG.PE, bt, 0))
                    with pe.Fori(0, G) as i:
                        tiles = tiles_of(pe, ENG.PE, bt, i * C + U)
                        for k in range(T):
                            b = k % 2
                            if mha:
                                pe.wait_ge(s_land[k].sem, i * landed + (s_land[k].n + landed))
                                pe.sem_inc(s_gate2.sem, 1)
                                for j in range(U):
                                    m = pe.transpose(PS[0:ED, 6 + b, j * P:(j + 1) * P], RING2[:, k, j, :], ident[:, :])
                                m.then_inc(s_at.sem, 1)
                            pe.wait_ge(s_ohc.sem, i * T + k + 2)
                            pe.wait_ge(s_done.sem, i * T + k + 4)
                            products(1 - b, tiles[k * U:(k + 1) * U])
                            pe.wait_ge(s_oh.sem, i * T + k + 3)
                            turn_one_hots(b)
                            if mha:
                                pe.wait_ge(s_atc.sem, i * T + k + 1)
                                for j in range(U):
                                    m = pe.matmul(PS[:, 4 + b, j * P:(j + 1) * P], ATT[:, b, j, :], WE,
                                                  start=True, stop=True)
                                m.then_inc(s_e.sem, 1)

                @block.scalar
                def _(act):
                    def copy_one_hots(b):
                        act.activation(OHT[:, b, :, :], turned(b), ACT.Copy).then_inc(s_ohc.sem, 1)

                    for b in range(2):
                        act.wait_ge(s_ohT.sem, b + 1)
                        copy_one_hots(b)
                    with act.Fori(0, G) as i:
                        for k in range(T):
                            b = k % 2
                            if mha:
                                act.wait_ge(s_at.sem, i * T + k + 1)
                                act.activation(ATT[:, b, :, :].rearrange("p a d -> p (a d)"), PS[0:ED, 6 + b, :], ACT.Copy)\
                                   .then_inc(s_atc.sem, 1)
                            act.wait_ge(s_ohT.sem, i * T + k + 3)
                            act.wait_ge(s_q.sem, i * T + k + 1)
                            copy_one_hots(b)

                @block.sync
                def _(sp):
                    if not rules:
                        def stored(i, k):
                            sp.wait_ge(s_spill[k].sem, i * 16 + 16)
                            sp.sem_inc(s_stored.sem, 1)

                        sp.sem_inc(s_stored.sem, T)
                        with sp.Fori(0, G) as i:
                            for k in range(T):
                                if mha:
                                    sp.wait_ge(s_v.sem, i * (T * ops) + k * ops + 1)
                                else:
                                    sp.wait_ge(s_land[k].sem, i * landed + (s_land[k].n + landed))
                                rows = VOUT[:, k, :, :] if mha else RING[:, k, :, 0:D]
                                sp.dma_start(d_spill[bass.ds(i, 1), :, k * U:(k + 1) * U, :]
                                             .rearrange("g p c d -> (g p) c d"), rows).then_inc(s_spill[k].sem, 16)
                                if k:
                                    stored(i, k - 1)
                            stored(i, T - 1)

            for k in range(T):
                s_land[k].n += landed * G

        carry = sb("carry", [P, 4])
        row = sb("row", [1, P + 2 * HD])
        rowf = sb("rowf", [1, P])
        whole_d = sb("whole_d", [P, 2])
        whole_k = sb("whole_k", [P, 2])
        ALPHA = QT[:, 0:G * C]

        def softmax(tag, flag, whole, eps, scale):
            sem = Phase()
            s_v, s_pe, s_a = sem(tag + "_v"), sem(tag + "_pe"), sem(tag + "_a")
            stages = []
            heads = [lambda t, o, h=h: t[0:1, o:o + P].rearrange("p (c h) -> p h c", h=HD)[:, h, :] for h in range(HD)]
            back = lambda ap: ap[:, ::-1]
            with sem.block() as block:
                @block.vector
                def _(dve):
                    v = s_v

                    def ask(what):
                        stages.append((v.n, what))
                        dve.wait_ge(s_pe.sem, len(stages))

                    def carried(last, kind):
                        v.link(dve, dve.tensor_copy(carry[:, 0:1], last))
                        v.link(dve, dve.tensor_copy(carry[:, 1:2], whole[:, 1:2] if kind == "back" else whole[:, 0:1]))
                        ask("row")
                        neutral = -BIG if kind == "max" else 0.0
                        v.link(dve, dve.memset(row[:, :], neutral))
                        if kind == "max":
                            v.link(dve, dve.tensor_scalar(rowf[:, :], PS[0:1, 1, 0:P], BIG, -BIG, ALU.mult, ALU.add))
                        else:
                            v.link(dve, dve.tensor_copy(rowf[:, :], PS[0:1, 1, 0:P]))
                        for h in range(HD):
                            f, x = heads[h](rowf, 0), PS[0:1, 0, 0:P].rearrange("p (c h) -> p h c", h=HD)[:, h, :]
                            if kind == "back":
                                v.inc(dve.tensor_tensor_scan(back(heads[h](row, 0)), back(f), back(x), 0.0, ALU.mult, ALU.add))
                            elif kind == "max":
                                v.inc(dve.tensor_tensor_scan(heads[h](row, 2 * HD), f, x, neutral, ALU.add, ALU.max))
                            else:
                                v.inc(dve.tensor_tensor_scan(heads[h](row, 2 * HD), f, x, 0.0, ALU.mult, ALU.add))
                        v.wait(dve)
                        ask("column")
                        v.link(dve, dve.tensor_copy(carry[:, 2:3], PS[:, 2, 0:1]))

                    def last_value_back():
                        v.link(dve, dve.scalar_tensor_tensor(LAF, flag[:, 1:SEQ + 1], 1.0, FW[:, :], ALU.not_equal, ALU.mult))
                        run = lambda init: dve.tensor_tensor_scan(back(TT), back(flag[:, 1:SEQ + 1]), back(LAF), init,
                                                                  ALU.mult, ALU.add)
                        v.link(dve, run(0.0))
                        carried(TT[:, 0:1], "back")
                        v.link(dve, run(carry[:, 2:3]))

                    v.link(dve, dve.tensor_scalar(TT[:, :], flag[:, 0:SEQ], BIG, -BIG, ALU.mult, ALU.add))
                    v.link(dve, dve.tensor_tensor_scan(FW[:, :], TT[:, :], XT[:, :], -BIG, ALU.add, ALU.max))
                    carried(FW[:, SEQ - 1:SEQ], "max")
                    v.link(dve, dve.tensor_tensor_scan(FW[:, :], TT[:, :], XT[:, :], carry[:, 2:3], ALU.add, ALU.max))
                    last_value_back()
                    v.link(dve, dve.tensor_tensor(XT[:, :], XT[:, :], TT[:, :], ALU.subtract))
                    at.shifted = v.n
                    dve.wait_ge(s_a.sem, 1)
                    sums = lambda init: dve.tensor_tensor_scan(FW[:, :], flag[:, 0:SEQ], XT[:, :], init, ALU.mult, ALU.add)
                    v.link(dve, sums(0.0))
                    carried(FW[:, SEQ - 1:SEQ], "sum")
                    v.link(dve, sums(carry[:, 2:3]))
                    last_value_back()
                    if eps:
                        v.link(dve, dve.tensor_scalar(TT[:, :], TT[:, :], eps, None, ALU.add))
                    v.link(dve, dve.reciprocal(TT[:, :], TT[:, :]))
                    v.link(dve, dve.tensor_tensor(XT[:, :], XT[:, :], TT[:, :], ALU.mult))

                @block.tensor
                def _(pe):
                    for n, what in stages:
                        pe.wait_ge(s_v.sem, n)
                        if what == "row":
                            pe.matmul(PS[0:1, 0, 0:P], carry[:, 0:1], ident[:, :], start=True, stop=True)
                            pe.matmul(PS[0:1, 1, 0:P], carry[:, 1:2], ident[:, :], start=True, stop=True)\
                              .then_inc(s_pe.sem, 1)
                        else:
                            pe.matmul(PS[:, 2, 0:1], row[0:1, HD:HD + P], ones[0:1, 0:1], start=True, stop=True)\
                              .then_inc(s_pe.sem, 1)

                @block.scalar
                def _(act):
                    act.wait_ge(s_v.sem, at.shifted)
                    act.activation(XT[:, :], XT[:, :], ACT.Exp, scale=scale).then_inc(s_a.sem, 1)

        at = Marks()

        VIN = over(XT, 0, [T, U, D])
        MSG = over(XT, 2048, [2, U, W0])
        IDX3 = over(XT, 3200, [T, U], U32)
        OH4 = over(FW, 0, [T, U, P])
        ACC2 = over(TT, 0, [NT, D])

        def aggregate(tag, labels, heads, table):
            sem = Phase()
            s_v, s_sum, s_gate = sem(tag + "_v"), sem(tag + "_sum"), sem(tag + "_gate")
            s_land = [sem(f"{tag}_land{k}") for k in range(T)] if table is None else sem.rows_moved(T)
            landed = 16 if table is None else 16 * U
            s_oh, s_dist, s_sq = sem(tag + "_oh"), sem(tag + "_dist"), sem(tag + "_sq")
            hot = lambda k: (OH4[:, k] if spilled else OH[:, k % 2])
            spilled = table is None
            maker = 1 if spilled else 3
            order = []
            for k in range(T):
                order += [("build", (k + 1) % T), ("add", k)]
            after, n = {}, 0
            for what, k in order:
                n += maker if what == "build" else U
                after[what, k] = n
            per = n
            sums = lambda b: PS[:, 2 * b:2 * b + 2, :].rearrange("p b (a d) -> p (b a) d", d=256)
            start = (1 if spilled else 2) + maker + U
            ready = lambda i, k: i * per + (start + (after["build", k] if k else after["build", 0] - per))

            with sem.block() as block:
                @block.vector
                def _(dve):
                    def build(t, i, k):
                        b = k % 2
                        if not spilled:
                            t.inc(one_hot(dve, OH[:, b, :, :], labels, i * C + k * U))
                        dve.wait_ge(s_land[k].sem, i * landed + (s_land[k].n + landed))
                        if heads:
                            w = D // heads
                            la = LA[:, bass.ds(i, 1), k * U:(k + 1) * U, 0:heads].rearrange("p g u h -> p (g u) h")
                            t.inc(dve.tensor_tensor(MSG[:, b, :, 0:D].rearrange("p a (h c) -> p a h c", h=heads),
                                                    VIN[:, k, :, :].rearrange("p a (h c) -> p a h c", h=heads),
                                                    bc(la, 3, w), ALU.mult))
                        else:
                            t.inc(dve.tensor_tensor(MSG[:, b, :, 0:D], VIN[:, k, :, :],
                                                    bc(ALPHA[:, bass.ds(i * C + k * U, U)], 2, D), ALU.mult))
                        if not spilled:
                            t.inc(ask(dve, IDX3[:, k, :], prj_i, i * C + (C + k * U)))

                    def turn_of(i, last):
                        tiles = tiles_of(dve, ENG.DVE, bt, i * C)
                        t = Step(s_v, 0 if last else i, per)
                        for what, k in order:
                            if what == "build":
                                if k:
                                    build(t, i, k)
                                elif not last:
                                    build(t, i + 1, 0)
                            else:
                                dve.wait_ge(s_sum.sem, i * T + (k + 1))
                                for j in range(U):
                                    to = (ACC, ACC2)[j % 2]
                                    acc = to[:, bass.ds(tiles[k * U + j], 1), 0:D]
                                    t.wait_for(dve, t.k - 1)
                                    t.inc(dve.tensor_tensor(acc, acc, sums(k % 2)[:, j:j + 1, 0:D], ALU.add))
                        return t

                    s_v.inc(dve.memset(ACC2, 0.0))
                    if not spilled:
                        for k in range(1, T):
                            ask(dve, IDX3[:, k, :], prj_i, k * U)
                        s_v.inc(ask(dve, IDX3[:, 0, :], prj_i, 0))
                    build(s_v, 0, 0)
                    s_v.wait(dve)
                    dve.sem_inc(s_v.sem, U)
                    s_v.n += U
                    assert s_v.n == start
                    with dve.Fori(0, G - 1) as i:
                        t = turn_of(i, False)
                    t.end(G - 1)
                    t = turn_of(G - 1, True)
                    t.wait(dve)
                    dve.tensor_tensor(ACC[:, :, 0:D], ACC[:, :, 0:D], ACC2, ALU.add)

                @block.tensor
                def _(pe):
                    with pe.Fori(0, G) as i:
                        for k in range(T):
                            b = k % 2
                            pe.wait_ge(s_v.sem, ready(i, k))
                            if spilled:
                                pe.wait_ge(s_oh.sem, i * T + (k + 1))
                            for j in range(U):
                                m = pe.matmul(sums(b)[:, j, 0:D], hot(k)[:, j, :], MSG[:, b, j, 0:D], start=True, stop=True)
                            m.then_inc(s_sum.sem, 1)

                if spilled:
                    @block.gpsimd
                    def _(pool):
                        for k in range(T):
                            distance(pool, hot(k), labels, k * U).then_inc(s_dist.sem, 1)
                        with pool.Fori(1, G) as i:
                            for k in range(T):
                                pool.wait_ge(s_sum.sem, i * T + (k + 1 - T))
                                distance(pool, hot(k), labels, i * C + k * U).then_inc(s_dist.sem, 1)

                    @block.scalar
                    def _(act):
                        act.sem_inc(s_sq.sem, 1)
                        with act.Fori(0, G) as i:
                            for k in range(T):
                                act.wait_ge(s_dist.sem, i * T + (k + 1))
                                act.activation(hot(k), hot(k), ACT.Square).then_inc(s_sq.sem, 1)
                                act.wait_ge(s_sq.sem, i * T + (k + 2))
                                act.activation(hot(k), hot(k), ACT.Relu, bias=ones[:, 0:1], scale=-1.0)\
                                   .then_inc(s_oh.sem, 1)

                    @block.sync
                    def _(sp):
                        def load(i, k):
                            sp.dma_start(VIN[:, k, :, :], d_spill[bass.ds(i, 1), :, k * U:(k + 1) * U, :]
                                         .rearrange("g p c d -> (g p) c d")).then_inc(s_land[k].sem, 16)

                        for k in range(T):
                            load(0, k)
                        with sp.Fori(1, G) as i:
                            for k in range(T):
                                sp.wait_ge(s_v.sem, ready(i - 1, k))
                                load(i, k)
                else:
                    @block.gpsimd
                    def _(pool):
                        pool.wait_ge(s_v.sem, 2)
                        pool.sem_inc(s_gate.sem, 1)
                        for k in range(T):
                            gather(pool, IDX3[:, k, :], table[:, :], VIN[:, k, :, :], s_land[k])
                        with pool.Fori(1, G) as i:
                            for k in range(T):
                                pool.wait_ge(s_v.sem, ready(i - 1, k))
                                pool.sem_inc(s_gate.sem, 1)
                                gather(pool, IDX3[:, k, :], table[:, :], VIN[:, k, :, :], s_land[k])

            for k in range(T):
                s_land[k].n += landed * G

        def layer0():
            W1 = over(FW, 0, [3, D])
            W1T = over(XT, 0, [3, D])
            w2 = over(FW, 400, [1])
            REL = over(FW, 512, [4, D], F32, ROWS)
            RELT = over(FW, 1024, [4, ROWS])
            WREL = over(FW, 2048, [W0])
            BX = over(FW, 2304, [4, W0], F32, ROWS)
            sem = Phase()
            s_l, s_v, s_pe = sem("l0w_l"), sem("l0w_v"), sem("l0w_pe")
            with sem.block() as block:
                @block.sync
                def _(sp):
                    s_l.inc(sp.dma_start(W1, A["L0_gnn_W_e1"].rearrange("d (a f) -> d a f", a=3)), 16)
                    s_l.inc(sp.dma_start(w2, A["L0_gnn_W_e2"].rearrange("a d -> d a")), 16)
                    s_l.inc(sp.dma_start(REL, A["L0_gnn_rel_embedding"].rearrange("(t p) d -> p t d", p=ROWS)), 16)
                    sp.wait_ge(s_v.sem, 8)
                    s_l.inc(sp.dma_start(d_rel[0:RELS, :].rearrange("(t p) d -> p t d", p=ROWS), BX), 16)
                    s_l.wait(sp)

                @block.tensor
                def _(pe):
                    pe.wait_ge(s_l.sem, 48)
                    for a in range(3):
                        pe.transpose(PS[:, 0, a * P:(a + 1) * P], W1[:, a, :], ident[:, :])
                        pe.matmul(PS[:, 1, a:a + 1], W1[:, a, :], w2, start=True, stop=True)
                    for r in range(4):
                        m = pe.transpose(PS[:, 2, r * P:r * P + ROWS], REL[:, r, :], ident[0:ROWS, 0:ROWS])
                    m.then_inc(s_pe.sem, 1)
                    pe.wait_ge(s_v.sem, 7)
                    for r in range(4):
                        m = pe.matmul(PS[0:ROWS, 3 + r, 0:D + 1], RELT[:, r, :], WREL[:, 0:D + 1], start=True, stop=True)
                    m.then_inc(s_pe.sem, 1)

                @block.vector
                def _(dve):
                    s_v.inc(dve.memset(BIAS, 0.0))
                    s_v.inc(dve.memset(WCAT, 0.0))
                    s_v.inc(dve.memset(BX, 0.0))
                    s_v.wait(dve)
                    dve.wait_ge(s_pe.sem, 1)
                    dve.tensor_copy(WCAT[:, 0:D], PS[:, 0, 0:D])
                    dve.tensor_copy(WCAT[:, D:D + 1], PS[:, 1, 0:1])
                    dve.tensor_copy(WCAT[:, D + 1:2 * D + 1], PS[:, 0, 2 * D:3 * D])
                    s_v.inc(dve.tensor_copy(WCAT[:, 2 * D + 1:2 * D + 2], PS[:, 1, 2:3]))
                    s_v.inc(dve.memset(BIAS[:, 2 * D + 2:2 * D + 3], 1.0))
                    dve.tensor_copy(WREL[:, 0:D], PS[:, 0, D:2 * D])
                    s_v.inc(dve.tensor_copy(WREL[:, D:D + 1], PS[:, 1, 1:2]))
                    s_v.inc(dve.tensor_copy(RELT, PS[:, 2, :].rearrange("p (r n) -> p r n", r=4)[:, :, 0:ROWS]))
                    dve.wait_ge(s_pe.sem, 2)
                    s_v.inc(dve.tensor_copy(BX[:, :, 0:D + 1], PS[0:ROWS, 3:7, 0:D + 1]))

            project("l0p", X, 2 * D + 3, D + 1, None, [(D + 1, 2 * D + 3, d_dst)])

            RA = over(XT, 0, [T, U, W0])
            RB = over(XT, 2304, [T, U, W0])
            I1, I2 = over(XT, 4608, [T, U], U32), over(XT, 4624, [T, U], U32)
            SC = over(XT, 4640, [T, 3, U])
            ONE = over(FW, 0, [T, U, P])
            ONET = over(FW, 2048, [T, U, P])
            qt = QT[:, 0:NT * (D + 1)].rearrange("p (t q) -> p t q", q=D + 1)
            sem = Phase()
            s_done, s_v, s_oh, s_t, s_sc, s_w, s_sum = (sem("l0e" + x) for x in
                                                        ("_done", "_v", "_oh", "_t", "_sc", "_w", "_sum"))
            s_tc, s_gate = sem("l0e_tc"), sem("l0e_gate")
            s_land = sem.rows_moved(T)
            landed = 32 * U
            order = [("rows", 0), ("messages", 0)]
            for k in range(1, T):
                order += [("rows", k), ("add", k - 1), ("messages", k)]
            order += [("add", T - 1)]
            after, n = {}, 0
            for part, k in order:
                n += {"rows": 3, "messages": 1, "add": U}[part]
                after[part, k] = n
            per = n
            sums = lambda b: PS[:, 2 * b:2 * b + 2, :].rearrange("p b (a d) -> p (b a) d", d=256)
            with sem.block() as block:
                @block.gpsimd
                def _(pool):
                    with pool.Fori(0, EG) as i:
                        for k in range(T):
                            pool.wait_ge(s_done.sem, i * T + k + 1)
                            pool.sem_inc(s_gate.sem, 1)
                            gather(pool, I1[:, k, :], d_dst[:, :], RA[:, k, :, :], s_land[k])
                            gather(pool, I2[:, k, :], d_rel[:, :], RB[:, k, :, :], s_land[k])

                @block.vector
                def _(dve):
                    def ask_step(k, at):
                        ask(dve, I1[:, k, :], SDST, at)
                        ask(dve, I2[:, k, :], SREL, at).then_inc(s_done.sem, 1)

                    for k in range(T):
                        ask_step(k, k * U)
                    for k in range(2):
                        one_hot(dve, ONE[:, k, :, :], sdl, k * U).then_inc(s_oh.sem, 1)
                    s_v.link(dve, dve.memset(ACC[:, :, :], 0.0))
                    with dve.Fori(0, EG) as i:
                        tiles = tiles_of(dve, ENG.DVE, sbt, i * C)
                        t = Step(s_v, i, per)
                        for part, k in order:
                            total, leaky, weight = (SC[:, k, n, :] for n in range(3))
                            if part == "rows":
                                dve.wait_ge(s_land[k].sem, i * landed + (s_land[k].n + landed))
                                t.link(dve, dve.tensor_tensor(RA[:, k, :, :], RA[:, k, :, :], RB[:, k, :, :], ALU.add))
                                dve.wait_ge(s_sc.sem, i * T + k + 1)
                                t.link(dve, dve.tensor_tensor(total, RA[:, k, :, D], PS[:, 6 + k % 2, k * U:(k + 1) * U], ALU.add))
                                t.inc(dve.scalar_tensor_tensor(leaky, total, 0.2, total, ALU.mult, ALU.max))
                            elif part == "messages":
                                dve.wait_ge(s_w.sem, i * T + k + 1)
                                t.inc(dve.tensor_tensor(RA[:, k, :, :], RA[:, k, :, :], bc(weight, 2, W0), ALU.mult))
                                one_hot(dve, ONE[:, (k + 2) % T, :, :], sdl, i * C + (k + 2) * U).then_inc(s_oh.sem, 1)
                            else:
                                dve.wait_ge(s_sum.sem, i * T + k + 1)
                                for j in range(U):
                                    acc = ACC[:, bass.ds(tiles[k * U + j], 1), :]
                                    t.link(dve, dve.tensor_tensor(acc, acc, sums(k % 2)[:, j:j + 1, 0:W0], ALU.add))
                                ask_step(k, i * C + (C + k * U))
                    t.end(EG)

                @block.tensor
                def _(pe):
                    def turn_one_hots(k):
                        for j in range(U):
                            m = pe.transpose(PS[:, 4, j * P:(j + 1) * P], ONE[:, k, j, :], ident[:, :])
                        m.then_inc(s_t.sem, 1)

                    def source_scores(k, tiles):
                        for j in range(U):
                            m = pe.matmul(PS[:, 6 + k % 2, k * U + j:k * U + j + 1], ONET[:, k, j, :],
                                          qt[:, bass.ds(tiles[j], 1), D:D + 1].rearrange("p a q -> p (a q)"),
                                          start=True, stop=True)
                        m.then_inc(s_sc.sem, 1)

                    base = 1
                    pe.wait_ge(s_oh.sem, 1)
                    turn_one_hots(0)
                    pe.wait_ge(s_tc.sem, 1)
                    source_scores(0, tiles_of(pe, ENG.PE, sbt, 0))
                    with pe.Fori(0, EG) as i:
                        tiles = tiles_of(pe, ENG.PE, sbt, i * C + U)
                        for k in range(T):
                            nxt = (k + 1) % T
                            pe.wait_ge(s_oh.sem, i * T + k + 2)
                            turn_one_hots(nxt)
                            pe.wait_ge(s_tc.sem, i * T + k + 2)
                            source_scores(nxt, tiles[k * U:(k + 1) * U])
                            pe.wait_ge(s_v.sem, i * per + (base + after["messages", k]))
                            for j in range(U):
                                m = pe.matmul(sums(k % 2)[:, j, 0:W0], ONE[:, k, j, :], RA[:, k, j, :], start=True, stop=True)
                            m.then_inc(s_sum.sem, 1)

                @block.scalar
                def _(act):
                    def copy_one_hots(k):
                        act.activation(ONET[:, k, :, :].rearrange("p a d -> p (a d)"), PS[:, 4, :], ACT.Copy)\
                           .then_inc(s_tc.sem, 1)

                    act.wait_ge(s_t.sem, 1)
                    copy_one_hots(0)
                    with act.Fori(0, EG) as i:
                        for k in range(T):
                            act.wait_ge(s_t.sem, i * T + k + 2)
                            copy_one_hots((k + 1) % T)
                            act.wait_ge(s_v.sem, i * per + (1 + after["rows", k]))
                            act.activation(SC[:, k, 2, :], SC[:, k, 1, :], ACT.Exp, scale=-1.0).then_inc(s_w.sem, 1)

            for k in range(T):
                s_land[k].n += landed * EG

            sem = Phase()
            s_v, s_a = sem("l0f_v"), sem("l0f_a")
            norms = Norms(s_v, s_a)
            S, Z = over(TT, 4200, [NT]), over(TT, 4232, [NT])
            own = over(FW, 0, [NT, D])
            with sem.block() as block:
                @block.vector
                def _(dve):
                    v = s_v
                    v.link(dve, dve.tensor_copy(S, ACC[:, :, D + 1]))
                    v.inc(dve.tensor_tensor(own, qt[:, :, 0:D], bc(S, 2, D), ALU.mult))
                    v.inc(dve.tensor_scalar(Z, S, 0.0, 1e-12, ALU.is_equal, ALU.mult))
                    v.wait(dve)
                    v.link(dve, dve.tensor_tensor(Z, Z, S, ALU.add))
                    v.link(dve, dve.reciprocal(Z, Z))
                    v.link(dve, dve.tensor_tensor(own, own, ACC[:, :, 0:D], ALU.add))
                    v.link(dve, dve.tensor_tensor(own, own, bc(Z, 2, D), ALU.mult))
                    v.link(dve, dve.tensor_tensor(X[:, :, :], X[:, :, :], own, ALU.add))
                    norms.norm(dve, X[:, :, :], own)

                @block.scalar
                def _(act):
                    norms.roots(act)

        def layer1():
            sem = Phase()
            s_l, s_v = sem("l1w_l"), sem("l1w_v")
            names = ("q", "k", "v", "skip")
            with sem.block() as block:
                @block.sync
                def _(sp):
                    for n, w in enumerate(names):
                        s_l.inc(sp.dma_start(WCAT[:, n * D:(n + 1) * D], A["L1_gnn_W" + w][:, :]), 16)
                        s_l.inc(sp.dma_start(BIAS[:, n * D:(n + 1) * D], row_of("L1_gnn_b" + w)), 16)
                    s_l.wait(sp)

                @block.vector
                def _(dve):
                    dve.wait_ge(s_l.sem, 128)
                    s_v.inc(dve.tensor_scalar(WCAT[:, 0:D], WCAT[:, 0:D], 0.25, None, ALU.mult))
                    s_v.inc(dve.tensor_scalar(BIAS[:, 0:D], BIAS[:, 0:D], 0.25, None, ALU.mult))

            project("l1p", X, 4 * D, D, (3 * D, 4 * D), [(D, 3 * D, d_kv)])

            sem = Phase()
            s_l = sem("l1e_l")
            with sem.block() as block:
                @block.sync
                def _(sp):
                    s_l.inc(sp.dma_start(WE, A["L1_gnn_We"][:, :]), 16)
                    s_l.wait(sp)

            scores("l1s", "mha", d_kv, 2 * D, D)

            sem = Phase()
            s_v = sem("l1m_v")
            off = over(FW, 0, [G, C])
            with sem.block() as block:
                @block.vector
                def _(dve):
                    s_v.link(dve, dve.tensor_scalar(off, dlm[:, 0:G * C].rearrange("p (g c) -> p g c", c=C),
                                                    NEG, -BIG, ALU.is_ge, ALU.mult))
                    s_v.inc(dve.tensor_tensor(LA[:, :, :, :], LA[:, :, :, :], bc(off, 3, HD), ALU.add))

            turn("l1ta", LAF, XT)
            softmax("l1x", cD, whole_d, 0.0, 1.0)
            turn("l1tb", XT, LAF)
            aggregate("l1g", dlm, HD, None)

            RWS = over(FW, 3200, [4, D])
            WF1 = over(FW, 3712, [4 * D])
            WF2 = over(FW, 4224, [4, D])
            BF1 = over(FW, 4736, [4])
            BF2 = over(TT, 4300, [D], F32, 1)
            H = ACC[:, :, 0:D]
            sem = Phase()
            s_l, s_v, s_a = sem("l1f_l"), sem("l1f_v"), sem("l1f_a")
            norms = Norms(s_v, s_a)
            with sem.block() as block:
                @block.sync
                def _(sp):
                    for n, w in enumerate(("g1", "b1", "g2", "b2")):
                        s_l.inc(sp.dma_start(RWS[:, n, :], rows_of("L1_gnn_" + w)), 16)
                    s_l.inc(sp.dma_start(WF1, A["L1_gnn_Wf1"][:, :]), 16)
                    s_l.inc(sp.dma_start(WF2, A["L1_gnn_Wf2"].rearrange("(c p) d -> p c d", p=P)), 16)
                    s_l.inc(sp.dma_start(BF1, A["L1_gnn_bf1"].rearrange("(c p) -> p c", p=P),
                                         allow_slow_non_contiguous=True), 16)
                    s_l.inc(sp.dma_start(BF2, row_of("L1_gnn_bf2")), 16)
                    s_l.wait(sp)

                @block.vector
                def _(dve):
                    dve.wait_ge(s_l.sem, 128)
                    norms.norm(dve, H, over(FW, 0, [NT, D]), RWS[:, 0, :], RWS[:, 1, :])

                @block.scalar
                def _(act):
                    norms.roots(act)

            hT = over(TT, 0, [P])
            gT = over(TT, 128, [4, P])
            hin = over(TT, 640, [1, P])
            sem = Phase()
            s_t, s_tc, s_up, s_g, s_dn, s_add = (sem("ffn" + x) for x in ("_t", "_tc", "_up", "_g", "_dn", "_add"))
            s_here = sem("ffn_here")
            with sem.block() as block:
                @block.gpsimd
                def _(pool):
                    with pool.Fori(0, NT) as i:
                        pool.wait_ge(s_t.sem, i + 1)
                        pool.tensor_copy(hin, H[:, bass.ds(i, 1), :]).then_inc(s_here.sem, 1)

                @block.tensor
                def _(pe):
                    pe.sem_inc(s_t.sem, 1)
                    with pe.Fori(0, NT) as i:
                        pe.wait_ge(s_here.sem, i + 1)
                        pe.transpose(PS[:, 0, 0:P], hin.rearrange("p a d -> p (a d)"), ident[:, :]).then_inc(s_t.sem, 1)
                        pe.wait_ge(s_tc.sem, i + 1)
                        for c in range(4):
                            m = pe.matmul(PS[:, 1, c * P:(c + 1) * P], WF1[:, c * P:(c + 1) * P], hT, start=True, stop=True)
                        m.then_inc(s_up.sem, 1)
                        pe.wait_ge(s_g.sem, i * 4 + 4)
                        pe.wait_ge(s_add.sem, i + 1)
                        for c in range(4):
                            pe.matmul(PS[:, 2, 0:D], gT[:, c, :], WF2[:, c, :], start=c == 0, stop=False)
                        pe.matmul(PS[:, 2, 0:D], ones[0:1, :], BF2, start=False, stop=True).then_inc(s_dn.sem, 1)

                @block.scalar
                def _(act):
                    with act.Fori(0, NT) as i:
                        act.wait_ge(s_up.sem, i + 1)
                        for c in range(4):
                            act.activation(gT[:, c, :], PS[:, 1, c * P:(c + 1) * P], ACT.Gelu, bias=BF1[:, c:c + 1])\
                               .then_inc(s_g.sem, 1)

                @block.vector
                def _(dve):
                    dve.sem_inc(s_add.sem, 1)
                    with dve.Fori(0, NT) as i:
                        dve.wait_ge(s_t.sem, i + 2)
                        dve.tensor_copy(hT, PS[:, 0, 0:P]).then_inc(s_tc.sem, 1)
                        dve.wait_ge(s_dn.sem, i + 1)
                        dve.tensor_tensor(HID[:, bass.ds(i, 1), :], H[:, bass.ds(i, 1), :], PS[:, 2:3, 0:D], ALU.add)\
                           .then_inc(s_add.sem, 1)

            sem = Phase()
            s_v, s_a = sem("l1n_v"), sem("l1n_a")
            norms = Norms(s_v, s_a)
            with sem.block() as block:
                @block.vector
                def _(dve):
                    norms.norm(dve, HID, over(FW, 0, [NT, D]), RWS[:, 2, :], RWS[:, 3, :])
                    s_v.link(dve, dve.tensor_tensor(X[:, :, :], X[:, :, :], HID, ALU.add))
                    norms.norm(dve, X[:, :, :], over(FW, 0, [NT, D]))

                @block.scalar
                def _(act):
                    norms.roots(act)

        def layer2():
            WR = over(XT, 0, [TYPES, D])
            WK2, WK3 = over(FW, 0, [D]), over(FW, 128, [D])
            WQ = over(FW, 256, [D])
            WQT = over(FW, 384, [D])
            KM = over(FW, 512, [TYPES + 4])
            HREL = over(FW, 576, [TYPES])
            HRUL = over(FW, 640, [4])
            BQ = over(FW, 656, [1])
            RID = over(FW, 660, [1], U32, 4)
            RULE = over(FW, 700, [D], F32, 4)
            M = TYPES + 4
            sem = Phase()
            s_l, s_v, s_pe, s_id = sem("l2w_l"), sem("l2w_v"), sem("l2w_pe"), sem("l2w_id")
            s_r, = sem.rows_moved(1)
            with sem.block() as block:
                @block.sync
                def _(sp):
                    s_id.inc(sp.dma_start(RID.bitcast(I32), A["L2_gnn_rule_ids"].rearrange("(p a) -> p a", a=1)), 16)
                    wk = A["L2_gnn_Wk_w"].rearrange("(a f) d -> a f d", a=3)
                    for t, src in ((WR, A["L2_gnn_W_r"].rearrange("r f o -> f r o")), (WQ, A["L2_gnn_Wq_w"][:, :]),
                                   (WCAT[:, 0:D], A["L2_gnn_Wq_w"][:, :]), (WCAT[:, LQ:LQ + D], wk[0]), (WK2, wk[1]), (WK3, wk[2]),
                                   (BIAS[:, 0:D], row_of("L2_gnn_Wq_b")), (BIAS[:, LQ:LQ + D], row_of("L2_gnn_Wk_b")),
                                   (BQ, A["L2_gnn_Wq_b"].rearrange("(p a) -> p a", a=1))):
                        s_l.inc(sp.dma_start(t, src), 16)
                    s_l.wait(sp)

                @block.gpsimd
                def _(pool):
                    pool.wait_ge(s_id.sem, 16)
                    pool.indirect_dma_start(out=RULE, out_offset=None, in_=A["L2_gnn_rule_emb"][:, :],
                                            in_offset=bass.IndirectOffsetOnAxis(ap=RID, axis=0)).then_inc(s_r.sem, 16)
                    s_r.n += 16
                    s_r.wait(pool)

                @block.vector
                def _(dve):
                    v = s_v
                    dve.wait_ge(s_l.sem, 9 * 16)
                    v.link(dve, dve.tensor_reduce(HREL, WR, AX.X, ALU.add))
                    v.link(dve, dve.tensor_scalar(HREL, HREL, 1.0 / D, None, ALU.mult))
                    dve.wait_ge(s_pe.sem, 1)
                    v.inc(dve.tensor_copy(HRUL, PS[:, 0, 0:4]))
                    v.inc(dve.tensor_copy(WQT, PS[:, 1, 0:D]))
                    dve.wait_ge(s_pe.sem, 2)
                    v.inc(dve.tensor_copy(KM[:, 0:TYPES], PS[:, 2, 0:TYPES]))
                    v.inc(dve.tensor_copy(KM[:, TYPES:M], PS[:, 2, TYPES:M]))
                    dve.wait_ge(s_pe.sem, 3)
                    v.inc(dve.tensor_copy(WCAT[:, D:LQ], PS[:, 3, 0:M]))
                    v.inc(dve.tensor_copy(BIAS[:, D:LQ], PS[0:1, 4, 0:M]))

                @block.tensor
                def _(pe):
                    pe.wait_ge(s_l.sem, 9 * 16)
                    s_r.wait(pe)
                    pe.transpose(PS[:, 0, 0:4], RULE, ident[0:4, 0:4])
                    pe.transpose(PS[:, 1, 0:D], WQ, ident[:, :]).then_inc(s_pe.sem, 1)
                    pe.wait_ge(s_v.sem, 4)
                    pe.matmul(PS[:, 2, 0:TYPES], WK2, HREL, start=True, stop=True)
                    pe.matmul(PS[:, 2, TYPES:M], WK3, HRUL, start=True, stop=True).then_inc(s_pe.sem, 1)
                    pe.wait_ge(s_v.sem, 6)
                    pe.matmul(PS[:, 3, 0:M], WQT, KM, start=True, stop=True)
                    pe.matmul(PS[0:1, 4, 0:M], BQ, KM, start=True, stop=True).then_inc(s_pe.sem, 1)

            stages = [over(FW, 1024, [4, 512]), over(FW, 1024 + 2048, [4, 512])]
            xT = over(FW, 5200, [P])
            sem = Phase()
            s_here, s_stored = sem("pr_here"), sem("pr_stored")
            xin = over(FW, 5330, [1, P])
            s_t, s_tc, s_pe, s_c = sem("pr_t"), sem("pr_tc"), sem("pr_pe"), [sem(f"pr_c{h}") for h in range(2)]
            s_st = [sem(f"pr_st{h}") for h in range(2)]
            WRF = WR.rearrange("p r o -> p (r o)")
            target = d_proj[:, :].rearrange("(t p r) o -> t p (r o)", p=P, r=TYPES)
            with sem.block() as block:
                @block.gpsimd
                def _(pool):
                    with pool.Fori(0, NT) as i:
                        pool.wait_ge(s_t.sem, i + 1)
                        pool.tensor_copy(xin, X[:, bass.ds(i, 1), :]).then_inc(s_here.sem, 1)

                @block.tensor
                def _(pe):
                    pe.sem_inc(s_t.sem, 1)
                    with pe.Fori(0, NT) as i:
                        pe.wait_ge(s_here.sem, i + 1)
                        pe.transpose(PS[:, 4, 0:P], xin.rearrange("p a d -> p (a d)"), ident[:, :]).then_inc(s_t.sem, 1)
                        pe.wait_ge(s_tc.sem, i + 1)
                        for n in range(8):
                            pe.wait_ge(s_c[n % 2].sem, i * 4 + n // 2 + 1)
                            pe.matmul(PS[:, n % 2 + 2 * (n // 2 % 2), :], xT, WRF[:, n * 512:(n + 1) * 512],
                                      start=True, stop=True).then_inc(s_pe.sem, 1)

                def copies(eng, copy, h):
                    eng.sem_inc(s_c[h].sem, 2)
                    with eng.Fori(0, NT) as i:
                        if h == 1:
                            eng.wait_ge(s_t.sem, i + 2)
                            copy(xT, PS[:, 4, 0:P]).then_inc(s_tc.sem, 1)
                        for n in range(h, 8, 2):
                            m = n // 4
                            eng.wait_ge(s_stored.sem, i * 2 + m + 1)
                            eng.wait_ge(s_pe.sem, i * 8 + n + 1)
                            copy(stages[m][:, n % 4, :], PS[:, n % 2 + 2 * (n // 2 % 2), :]).then_inc(s_c[h].sem, 1)

                @block.vector
                def _(dve):
                    copies(dve, dve.tensor_copy, 0)

                @block.scalar
                def _(act):
                    copies(act, lambda o, i: act.activation(o, i, ACT.Copy), 1)

                @block.sync
                def _(sp):
                    sp.sem_inc(s_stored.sem, 2)
                    with sp.Fori(0, NT) as i:
                        for m in range(2):
                            for h in range(2):
                                sp.wait_ge(s_c[h].sem, i * 4 + (2 * m + 4))
                            sp.dma_start(target[bass.ds(i, 1), :, m * 2048:(m + 1) * 2048].rearrange("t p o -> (t p) o"),
                                         stages[m].rearrange("p a o -> p (a o)")).then_inc(s_st[m].sem, 16)
                        for m in range(2):
                            sp.wait_ge(s_st[m].sem, i * 16 + 16)
                            sp.sem_inc(s_stored.sem, 1)

            project("l2p", X, LQ + D, LQ, None, [(LQ, LQ + D, d_kn)])
            scores("l2s", "rules", d_kn, D, LQ)
            turn("l2ta", LAF, XT)
            softmax("l2x", cK, whole_k, 0.0, float(D) ** -0.5)
            turn("l2tb", XT, LAF)

            ROW2 = over(FW, 3200, [3, D])
            sem = Phase()
            s_l, s_v = sem("l2m_l"), sem("l2m_v")
            with sem.block() as block:
                @block.vector
                def _(dve):
                    al = ALPHA.rearrange("p (g c) -> p g c", c=C)
                    s_v.link(dve, dve.tensor_reduce(al, LA[:, :, :, 0:4], AX.X, ALU.add))
                    s_v.inc(dve.tensor_scalar(al, al, 0.25, None, ALU.mult))
                    s_v.inc(dve.memset(ACC[:, :, :], 0.0))

            aggregate("l2g", dlm, 0, d_proj)

            sem = Phase()
            s_l, s_v, s_a = sem("l2f_l"), sem("l2f_v"), sem("l2f_a")
            norms = Norms(s_v, s_a)
            H = ACC[:, :, 0:D]
            with sem.block() as block:
                @block.sync
                def _(sp):
                    for n, w in enumerate(("bias", "ln_gamma", "ln_beta")):
                        s_l.inc(sp.dma_start(ROW2[:, n, :], rows_of("L2_gnn_" + w)), 16)

                @block.vector
                def _(dve):
                    dve.wait_ge(s_l.sem, 48)
                    s_v.link(dve, dve.tensor_tensor(H, H, bc(ROW2[:, 0, :], 1, NT), ALU.add))
                    norms.norm(dve, H, over(FW, 0, [NT, D]), ROW2[:, 1, :], ROW2[:, 2, :])
                    s_v.link(dve, dve.tensor_scalar(H, H, 0.0, None, ALU.max))
                    s_v.link(dve, dve.tensor_tensor(X[:, :, :], X[:, :, :], H, ALU.add))
                    norms.norm(dve, X[:, :, :], over(FW, 0, [NT, D]))

                @block.scalar
                def _(act):
                    norms.roots(act)

        def gatv2(n, src, final):
            tag = f"l3{n}"
            sem = Phase()
            s_l, s_v = sem(tag + "w_l"), sem(tag + "w_v")
            with sem.block() as block:
                @block.sync
                def _(sp):
                    s_l.inc(sp.dma_start(WCAT[:, 0:D], A[f"L3_gnn_W{n}_r"][:, :]), 16)
                    s_l.inc(sp.dma_start(WCAT[:, D:2 * D], A[f"L3_gnn_W{n}_l"][:, :]), 16)
                    s_l.wait(sp)

                @block.vector
                def _(dve):
                    s_v.inc(dve.memset(BIAS, 0.0))

            project(tag + "p", src, 2 * D, D, None, [(D, 2 * D, d_xl)])

            sem = Phase()
            s_l = sem(tag + "a_l")
            with sem.block() as block:
                @block.sync
                def _(sp):
                    s_l.inc(sp.dma_start(ATTW, A[f"L3_gnn_att{n}"].rearrange("h c -> (h c)").rearrange("(a m) -> a m", a=1)
                                         .to_broadcast([P, D])), 16)
                    s_l.wait(sp)

            scores(tag + "s", "gatv2", d_xl, D, D)
            turn(tag + "ta", LAF, XT)
            softmax(tag + "x", cD, whole_d, 1e-16, 1.0)
            turn(tag + "tb", XT, LAF)

            sem = Phase()
            s_v = sem(tag + "z_v")
            with sem.block() as block:
                @block.vector
                def _(dve):
                    s_v.inc(dve.memset(ACC[:, :, :], 0.0))

            aggregate(tag + "g", dl, 4, None)

            ROW1 = over(FW, 3200, [D])
            sem = Phase()
            s_l, s_v, s_a = sem(tag + "f_l"), sem(tag + "f_v"), sem(tag + "f_a")
            norms = Norms(s_v, s_a)
            H = ACC[:, :, 0:D]
            with sem.block() as block:
                @block.sync
                def _(sp):
                    s_l.inc(sp.dma_start(ROW1, rows_of(f"L3_gnn_b{n}")), 16)
                    s_l.wait(sp)
                    if final:
                        sp.wait_ge(s_v.sem, at.final)
                        s_l.inc(sp.dma_start(out[0:(NT - 1) * P, :].rearrange("(t p) d -> p t d", p=P), X[:, 0:NT - 1, :]), 16)
                        s_l.inc(sp.dma_start(out[(NT - 1) * P:N, :], X[0:NLAST, NT - 1, :]), 16)
                        s_l.wait(sp)

                at.final = 11

                @block.vector
                def _(dve):
                    dve.wait_ge(s_l.sem, 16)
                    s_v.link(dve, dve.tensor_tensor(H, H, bc(ROW1, 1, NT), ALU.add))
                    if final:
                        s_v.link(dve, dve.tensor_scalar(H, H, 0.0, None, ALU.max))
                        s_v.link(dve, dve.tensor_tensor(X[:, :, :], X[:, :, :], H, ALU.add))
                        norms.norm(dve, X[:, :, :], over(FW, 0, [NT, D]))
                        assert s_v.n == at.final
                    else:
                        s_v.inc(dve.tensor_scalar(HID, H, 0.0, None, ALU.max))

                @block.scalar
                def _(act):
                    norms.roots(act)

        constants()
        records_by_src()
        sort_pass("ss", ECOL, 7, 5, NT, d_slist, sbt, 1)
        source_tables()
        layer0()
        records_by_dst()
        sort_pass("s0", ACOL, 0, 6, TYPES + 1, d_pass[0], None, 0)
        load_records("r0", d_pass[0])
        sort_pass("s1", ACOL, 6, 6, 64, d_pass[1], None, 0)
        load_records("r1", d_pass[1])
        sort_pass("s2", ACOL, 12, 6, 2 * NT, d_list, bt, 2)
        LIST = over(XT, 0, [C, G, 4], I32)
        keys("kk", LIST, 0, True)
        turn("kt", TT, LAF)
        flags("kf", cK, whole_k)
        keys("dk", LIST, 6, False)
        turn("dt", TT, LAF)
        flags("df", cD, whole_d)
        layer1()
        layer2()
        gatv2(1, X, False)
        gatv2(2, HID, True)


_OUTS = [((N, D), "float32")]


def kernel(**inputs):
    import numpy as np
    import concourse.bacc as bacc
    from concourse.bass_utils import run_bass_kernel_spmd

    nc = bacc.Bacc("TRN2", target_bir_lowering=False, num_devices=1)
    arrays, aps = {}, {}
    for name, a in inputs.items():
        a = np.ascontiguousarray(a)
        arrays[f"in_{name}"] = a
        aps[name] = nc.dram_tensor(f"in_{name}", a.shape, mybir.dt.from_np(a.dtype), kind="ExternalInput").ap()
    out = nc.dram_tensor("out_x", (N, D), F32, kind="ExternalOutput").ap()
    gnn_kernel(nc, aps, out)
    r = run_bass_kernel_spmd(nc, [arrays], core_ids=[0])
    return r.results[0]["out_x"]
```

```python
import concourse.bass as bass
from concourse import mybir
from contextlib import ExitStack, contextmanager

F32, BF16 = mybir.dt.float32, mybir.dt.bfloat16
I32, U32, U16, U8 = mybir.dt.int32, mybir.dt.uint32, mybir.dt.uint16, mybir.dt.uint8
ALU = mybir.AluOpType
ACT = mybir.ActivationFunctionType
AX = mybir.AxisListType
ENG = mybir.EngineType

P = 128
N, E, D = 3125, 100000, 128
NT = (N + P - 1) // P
NPAD = NT * P
NLAST = N - (NT - 1) * P
RELS, TYPES = 500, 32
ED = 64
ROWS = 125
ECOL, NCOL = E // ROWS, N // ROWS
ACOL = ECOL + NCOL
ALL = E + N
U = 4
C = 16
HD = 8
G = -(-(ALL // P + NT) // C)
SLOTS = G * C * P
SEQ = G * P
EG = -(-(E // P + NT) // C)
ESLOTS = EG * C * P
NIL = 4095
BIG = 1.0e30
NEG = 256.0
STEPS = C // U
W0 = 130
LQ = 164


class Count:

    def __init__(self, sem):
        self.sem, self.n = sem, 0

    def inc(self, ins, k=1):
        ins.then_inc(self.sem, k)
        self.n += k

    def wait(self, eng):
        eng.wait_ge(self.sem, self.n)

    def link(self, eng, ins):
        self.inc(ins)
        self.wait(eng)


class Marks:
    pass


class Step:

    def __init__(self, count, i, per):
        self.count, self.i, self.per, self.k = count, i, per, 0

    def inc(self, ins):
        ins.then_inc(self.count.sem, 1)
        self.k += 1

    def wait(self, eng):
        eng.wait_ge(self.count.sem, self.i * self.per + (self.count.n + self.k))

    def link(self, eng, ins):
        self.inc(ins)
        self.wait(eng)

    def wait_for(self, eng, k):
        eng.wait_ge(self.count.sem, self.i * self.per + (self.count.n + k))

    def end(self, turns):
        assert self.k == self.per, (self.k, self.per)
        self.count.n += turns * self.per


def bc(ap, axis, n):
    u = ap.unsqueeze(axis)
    shape = list(u.shape)
    shape[axis] = n
    return u.to_broadcast(shape)


def gnn_kernel(nc, A, out):
    ctx = ExitStack()
    with ctx:
        nc_dram = lambda name, shape, dt=F32: nc.dram_tensor("scr_" + name, shape, dt, kind="Internal")

        def sb(name, shape, dt=F32):
            return ctx.enter_context(nc.sbuf_tensor("sb_" + name, shape, dt))

        moved = [Count(ctx.enter_context(nc.semaphore(f"rows_moved{k}"))) for k in range(5)]

        class Phase:

            def __init__(self):
                self.stack, self.counts = ExitStack(), []

            def rows_moved(self, n):
                return moved[:n]

            def __call__(self, name):
                self.counts.append(Count(self.stack.enter_context(nc.semaphore(name))))
                return self.counts[-1]

            @contextmanager
            def block(self, beside=0):
                with nc.Block() as block:
                    if beside:
                        tag = self.counts[0].sem.name
                        s_fill, s_gate = self(tag + "_fill"), self(tag + "_gate")

                        @block.gpsimd
                        def _(pool):
                            under_way[0].turns(pool, s_fill, s_gate, beside)

                    yield block
                with nc.Block() as block:
                    @block.sync
                    def _(sp):
                        for c in self.counts:
                            sp.sem_clear(c.sem)
                self.stack.close()

        d_pass = [nc_dram(f"pass{i}", [ALL, 4], I32) for i in range(2)]
        d_list = nc_dram("list", [SLOTS, 4], I32)
        d_slist = nc_dram("slist", [ESLOTS, 4], I32)
        d_dst = nc_dram("tab_dst", [NPAD, W0])
        d_rel = nc_dram("tab_rel", [RELS, W0])
        d_kv = nc_dram("tab_kv", [NPAD, 2 * D])
        d_kn = nc_dram("tab_kn", [NPAD, D])
        d_xl = nc_dram("tab_xl", [NPAD, D])
        d_proj = nc_dram("tab_proj", [NPAD * TYPES, D])
        d_spill = nc_dram("spill", [G, P, C, D])

        X = sb("x", [P, NT, D])
        ACC = sb("acc", [P, NT, W0])
        QT = sb("qt", [P, NT * LQ])
        ident = sb("ident", [P, P])
        ident16 = sb("ident16", [P, P], BF16)
        iota = sb("iota", [P, P])
        iota16 = sb("iota16", [P, P], BF16)
        ones = sb("ones", [P, P])
        lower = sb("lower", [P, P])
        up8 = sb("up8", [P, P])
        down8 = sb("down8", [P, P])
        src_i = sb("src_i", [P, G * C + C], U32)
        eid_i = sb("eid_i", [P, G * C + C], U32)
        prj_i = sb("prj_i", [P, G * C + C], U32)
        dl = sb("dl", [P, G * C + 2 * U], BF16)
        dlm = sb("dlm", [P, G * C + U], BF16)
        typ = sb("typ", [P, G * C], BF16)
        bt = sb("bt", [1, G * C + U], I32)
        sbt = sb("sbt", [1, EG * C + U], I32)
        sdl = sb("sdl", [P, EG * C + 2 * U], BF16)
        cD = sb("cD", [P, SEQ + 1], U8)
        cK = sb("cK", [P, SEQ + 1], U8)
        LA = sb("la", [P, G, C, HD])
        XT = sb("xt", [P, SEQ])
        FW = sb("fw", [P, SEQ])
        TT = sb("tt", [P, SEQ])
        KEPT = sb("kept", [P, 4 * ECOL + ACOL])
        RINGS = sb("rings", [ROWS, 5 * 5 * 5], I32)
        PS = ctx.enter_context(nc.psum_tensor("psum", [P, 8, 512], F32))

        def over(buf, at, shape, dt=F32, parts=P):
            n = 1
            for s in shape:
                n *= s
            if dt in (BF16, U16):
                v = buf[0:parts, at:at + (n + 1) // 2].bitcast(dt)[:, 0:n]
            else:
                v = buf[0:parts, at:at + n]
                if dt != F32:
                    v = v.bitcast(dt)
            if len(shape) == 1:
                return v
            names = "abcd"[:len(shape)]
            sizes = {m: s for m, s in zip(names[1:], shape[1:])}
            return v.rearrange(f"p ({' '.join(names)}) -> p {' '.join(names)}", **sizes)

        def constants():
            sem = Phase()
            s_x, s_p, s_v = sem("c_x"), sem("c_pool"), sem("c_vec")
            with sem.block() as block:
                @block.vector
                def _(dve):
                    s_v.link(dve, dve.memset(X[:, NT - 1, :], 0.0))
                    s_v.inc(dve.memset(ones[:, :], 1.0))
                    s_v.inc(dve.memset(LA[:, :, :, :], 0.0))
                    for index in (src_i, eid_i, prj_i):
                        s_v.inc(dve.memset(index[:, :], 0))
                    dve.wait_ge(s_p.sem, 9)
                    s_v.inc(dve.tensor_copy(ident16[:, :], ident[:, :]))
                    s_v.inc(dve.tensor_copy(iota16[:, :], iota[:, :]))

                @block.gpsimd
                def _(pool):
                    s_p.inc(pool.memset(ident[:, :], 0.0))
                    s_p.inc(pool.iota(iota[:, :], [[1, P]], base=0, channel_multiplier=0,
                                      allow_small_or_imprecise_dtypes=True))
                    s_p.inc(pool.memset(lower[:, :], 1.0))
                    s_p.inc(pool.memset(up8[:, :], 0.0))
                    s_p.inc(pool.memset(down8[:, :], 0.0))
                    s_p.wait(pool)
                    for t, base in ((ident, 0), (up8, HD), (down8, -HD)):
                        s_p.inc(pool.affine_select(out=t[:, :], in_=t[:, :], compare_op=ALU.not_equal,
                                                   fill=1.0, base=base, pattern=[[-1, P]], channel_multiplier=1))
                    s_p.inc(pool.affine_select(out=lower[:, :], in_=lower[:, :], compare_op=ALU.is_ge,
                                               fill=0.0, base=-1, pattern=[[1, P]], channel_multiplier=-1))

                @block.sync
                def _(sp):
                    sp.wait_ge(s_v.sem, 1)
                    s_x.inc(sp.dma_start(X[:, 0:NT - 1, :],
                                         A["x"][0:(NT - 1) * P, :].rearrange("(t p) d -> p t d", p=P)), 16)
                    s_x.inc(sp.dma_start(X[0:NLAST, NT - 1, :], A["x"][(NT - 1) * P:N, :]), 16)
                    s_x.wait(sp)

        REC = lambda cols, buf=XT: over(buf, 0, [cols, 4], I32, ROWS)
        EARLY = LA[:, :, :, :].rearrange("p a b c -> p (a b c)")
        ring_pos = RINGS[:, 0:25].rearrange("p (k c) -> p k c", c=5)
        ring_rec = RINGS[:, 25:125].rearrange("p (k c w) -> p k c w", c=5, w=4)
        under_way = []

        class Scatter:

            def __init__(self, rec, pos, cols, target):
                self.rec, self.pos, self.target = rec, pos, target
                self.total, self.done = cols // 25, 0

            def fill(self, eng, i, k):
                at = bass.ds(i * 25 + k * 5, 5)
                eng.tensor_copy(ring_pos[:, k, :], self.pos[:, at])
                return eng.tensor_copy(ring_rec[:, k, :, :], self.rec[:, at, :])

            def send(self, pool, k):
                for j in range(5):
                    pool.indirect_dma_start(
                        out=self.target[:, :], out_offset=bass.IndirectOffsetOnAxis(
                            ap=ring_pos[:, k, j:j + 1].bitcast(U32), axis=0),
                        in_=ring_rec[:, k, j, :], in_offset=None).then_inc(moved[k].sem, 16)

            def start(self):
                self.base = [s.n for s in moved]
                under_way[:] = [self]

            def turns(self, pool, s_fill, s_gate, n):
                first = self.done

                def turn_of(i, peeled):
                    for k in range(5):
                        if not peeled:
                            pool.wait_ge(moved[k].sem, i * 80 + self.base[k])
                        self.fill(pool, i, k).then_inc(s_fill.sem, 1)
                        pool.wait_ge(s_fill.sem, i * 5 + (k + 1 - first * 5))
                        pool.sem_inc(s_gate.sem, 1)
                        self.send(pool, k)

                if first == 0:
                    turn_of(0, True)
                if (first or 1) < first + n:
                    with pool.Fori(first or 1, first + n) as i:
                        turn_of(i, False)
                self.done += n

            def rest(self, tag):
                sem = Phase()
                s_ring, s_gate = sem(tag + "_ring"), sem(tag + "_gate")
                first = self.done
                with sem.block() as block:
                    @block.vector
                    def _(dve):
                        def turn_of(i, peeled):
                            for k in range(5):
                                if not peeled:
                                    dve.wait_ge(moved[k].sem, i * 80 + self.base[k])
                                self.fill(dve, i, k).then_inc(s_ring.sem, 1)

                        if first == 0:
                            turn_of(0, True)
                        with dve.Fori(first or 1, self.total) as i:
                            turn_of(i, False)

                    @block.gpsimd
                    def _(pool):
                        with pool.Fori(first, self.total) as i:
                            for k in range(5):
                                pool.wait_ge(s_ring.sem, i * 5 + (k + 1 - first * 5))
                                pool.sem_inc(s_gate.sem, 1)
                                self.send(pool, k)
                        for k in range(5):
                            moved[k].n += 80 * self.total
                            moved[k].wait(pool)

        def records_by_dst():
            sem = Phase()
            s_l, s_v = sem("rd_l"), sem("rd_v")
            rec = REC(ACOL, EARLY)
            raw = [over(FW, i * ECOL, [ECOL], I32, ROWS) for i in range(3)]
            tmp = over(FW, 3 * ECOL, [ECOL], I32, ROWS)
            with sem.block(1) as block:
                @block.sync
                def _(sp):
                    for t, name in zip(raw, ("dst", "edge_type_32", "src")):
                        s_l.inc(sp.dma_start(t, A[name].rearrange("(p c) -> p c", p=ROWS)), 16)

                @block.vector
                def _(dve):
                    dve.wait_ge(s_l.sem, 48)
                    s_v.inc(dve.tensor_scalar(tmp, raw[0], 64.0, None, ALU.mult))
                    s_v.inc(dve.tensor_copy(rec[:, 0:ECOL, 1], raw[2]))
                    s_v.wait(dve)
                    s_v.link(dve, dve.scalar_tensor_tensor(rec[:, 0:ECOL, 0], raw[0], 64.0, raw[1], ALU.mult, ALU.add))
                    s_v.inc(dve.scalar_tensor_tensor(rec[:, 0:ECOL, 3], raw[2], float(TYPES), raw[1], ALU.mult, ALU.add))

        def records_by_src():
            sem = Phase()
            s_l, s_v, s_p = sem("rs_l"), sem("rs_v"), sem("rs_p")
            rec, by_dst = REC(ECOL, KEPT), REC(ACOL, EARLY)
            raw = [over(FW, i * ECOL, [ECOL], I32, ROWS) for i in range(3)]
            with sem.block() as block:
                @block.sync
                def _(sp):
                    for t, name in zip(raw, ("src", "dst", "edge_type_500")):
                        s_l.inc(sp.dma_start(t, A[name].rearrange("(p c) -> p c", p=ROWS)), 16)

                @block.gpsimd
                def _(pool):
                    s_p.inc(pool.iota(by_dst[:, 0:ECOL, 2], [[1, ECOL]], base=0, channel_multiplier=ECOL))
                    s_p.inc(pool.memset(by_dst[:, ECOL:ACOL, 2], 0))
                    s_p.inc(pool.iota(by_dst[:, ECOL:ACOL, 1], [[1, NCOL]], base=0, channel_multiplier=NCOL))
                    s_p.inc(pool.memset(by_dst[:, ECOL:ACOL, 3], 0))
                    s_p.inc(pool.iota(by_dst[:, ECOL:ACOL, 0], [[64, NCOL]], base=TYPES, channel_multiplier=64 * NCOL))

                @block.vector
                def _(dve):
                    dve.wait_ge(s_l.sem, 48)
                    for w in range(3):
                        s_v.inc(dve.tensor_copy(rec[:, 0:ECOL, w], raw[w]))
                    s_v.inc(dve.memset(rec[:, 0:ECOL, 3], 0))

        class Places:

            def __init__(self, count, s_gate, unit, dig, mask, run, pos, off):
                self.count, self.s_gate, self.unit, self.dig = count, s_gate, unit, dig
                self.mask, self.run, self.pos, self.off = mask, run, pos, off

            def masks(self, dve, t, pair, o):
                for h in range(2):
                    t.wait_for(dve, o + h - 1)
                    t.inc(dve.tensor_scalar(self.mask[h], self.dig, iota[0:ROWS, bass.ds(pair * 2 + h, 1)], None, ALU.is_equal))

            def counts(self, dve, t, pair, o):
                for h in range(2):
                    t.wait_for(dve, o + 1 + h)
                    t.inc(dve.tensor_tensor_scan(self.run[h], self.unit, self.mask[h], self.off[:, bass.ds(pair * 2 + h, 1)],
                                                 ALU.mult, ALU.add))

            def positions(self, dve, t, pair, o):
                for h in range(2):
                    t.wait_for(dve, o + 3 + 2 * h)
                    dve.sem_inc(self.s_gate.sem, 1)
                    t.inc(dve.copy_predicated(self.pos, self.mask[h], self.run[h]))

        def rank(tag, buf, cols, shift, bits, bins, target, into, bucket, beside=0, later=False):
            sem = Phase()
            s_v, s_pe, s_pool, s_init = sem(tag + "_v"), sem(tag + "_pe"), sem(tag + "_pool"), sem(tag + "_init")
            s_gate = sem(tag + "_gate")
            rec = REC(cols, buf)
            key = over(FW, 0, [cols], I32, ROWS)
            work, o = (TT, ACOL + 384) if later else (FW, ACOL)
            half = (ACOL + 1) // 2
            pos = over(work, o, [cols], F32, ROWS)
            run = [over(work, o + (1 + h) * ACOL, [cols], F32, ROWS) for h in range(2)]
            dig = over(work, o + 3 * ACOL, [cols], BF16, ROWS)
            mask = [over(work, o + 3 * ACOL + (1 + h) * half, [cols], U16, ROWS) for h in range(2)]
            unit = over(TT, 0, [cols], F32, ROWS)
            small = [over(TT, ACOL + 64 * i, [64], F32, ROWS) for i in range(4)]
            cnt, off, tot, beg = small
            pair = over(TT, ACOL + 256, [64], F32, ROWS)
            pair_i = over(TT, ACOL + 320, [64], I32, ROWS)
            pos_i = over(buf, 4 * cols, [cols], I32, ROWS)
            nt = (G if into is bt else EG) * C
            tcols = -(-nt // ROWS)
            free = FW if later else TT
            tile_no, tiles = over(free, 4 * ACOL, [tcols], F32, ROWS), over(free, 4 * ACOL + 16, [tcols], F32, ROWS)
            begun = over(free, 4 * ACOL + 32, [tcols, NT], F32, ROWS)
            flat = over(free, 4 * ACOL + 512, [tcols * ROWS], F32, 1)
            nil = over(EARLY if buf is XT else XT, 0, [G * C, 4], I32)
            slots = 0 if not bucket else target.shape[0]
            pairs = (bins + 1) // 2
            at = Marks()

            with sem.block(beside) as block:
                if bucket:
                    @block.sync
                    def _(sp):
                        sp.wait_ge(s_v.sem, 2)
                        s_init.inc(sp.dma_start(target[:, :].rearrange("(p c) w -> p c w", p=P),
                                                nil[:, 0:slots // P, :]), 16)
                        s_init.wait(sp)

                @block.vector
                def _(dve):
                    if bucket:
                        s_v.link(dve, dve.memset(nil[:, :, :], 0))
                        s_v.link(dve, dve.memset(nil[:, :, 0], NIL << shift if bucket == 1 else NIL << 6))
                    s_v.link(dve, dve.tensor_scalar(key, rec[:, :, 0], shift, (1 << bits) - 1,
                                                    ALU.logical_shift_right, ALU.bitwise_and))
                    s_v.inc(dve.tensor_copy(dig, key))
                    s_v.inc(dve.memset(unit, 1.0))
                    s_v.inc(dve.memset(cnt, 0.0))
                    s_v.inc(dve.memset(pos, 0.0))
                    s_v.wait(dve)
                    with dve.Fori(0, pairs) as i:
                        t = Step(s_v, i, 2)
                        for h in range(2):
                            b = i * 2 + h
                            t.wait_for(dve, h - 1)
                            t.inc(dve.tensor_scalar(mask[h], dig, iota[0:ROWS, bass.ds(b, 1)], None,
                                                    ALU.is_equal, ALU.add, accum_out=cnt[:, bass.ds(b, 1)]))
                    t.end(pairs)
                    s_v.wait(dve)
                    at.counted = s_v.n
                    dve.wait_ge(s_pe.sem, 2)
                    s_v.link(dve, dve.tensor_copy(tot, PS[0:ROWS, 1, 0:64]))
                    if bucket:
                        nb = bins // bucket
                        if bucket == 2:
                            even, odd = (tot.rearrange("p (a b) -> p b a", b=2)[:, i, 0:nb] for i in range(2))
                            s_v.link(dve, dve.tensor_tensor(pair[:, 0:nb], even, odd, ALU.add))
                        else:
                            s_v.link(dve, dve.tensor_copy(pair[:, 0:nb], tot[:, 0:nb]))
                        s_v.link(dve, dve.tensor_scalar(pair[:, 0:nb], pair[:, 0:nb], float(P - 1), None, ALU.add))
                        s_v.link(dve, dve.tensor_copy(pair_i[:, 0:nb], pair[:, 0:nb]))
                        s_v.link(dve, dve.tensor_scalar(pair_i[:, 0:nb], pair_i[:, 0:nb], 7, 7,
                                                        ALU.logical_shift_right, ALU.logical_shift_left))
                        s_v.link(dve, dve.tensor_copy(pair[:, 0:nb], pair_i[:, 0:nb]))
                        s_v.link(dve, dve.tensor_tensor_scan(off[:, 0:nb], unit[:, 0:nb], pair[:, 0:nb], 0.0,
                                                             ALU.mult, ALU.add))
                        s_v.link(dve, dve.tensor_tensor(off[:, 0:nb], off[:, 0:nb], pair[:, 0:nb], ALU.subtract))
                        if bucket == 2:
                            b_even, b_odd = (beg.rearrange("p (a b) -> p b a", b=2)[:, i, 0:nb] for i in range(2))
                            s_v.inc(dve.tensor_copy(b_even, off[:, 0:nb]))
                            s_v.inc(dve.tensor_tensor(b_odd, off[:, 0:nb], even, ALU.add))
                            s_v.wait(dve)
                        else:
                            s_v.link(dve, dve.tensor_copy(beg[:, 0:nb], off[:, 0:nb]))
                        s_v.link(dve, dve.tensor_scalar(pair[:, 0:nb], off[:, 0:nb], 1.0 / P, None, ALU.mult))
                        dve.wait_ge(s_pool.sem, 1)
                        s_v.link(dve, dve.tensor_tensor(begun, bc(tile_no, 2, nb), bc(pair[:, 0:nb], 1, tcols), ALU.is_ge))
                        s_v.link(dve, dve.tensor_reduce(tiles, begun, AX.X, ALU.add))
                        s_v.link(dve, dve.tensor_scalar(tiles, tiles, -1.0, None, ALU.add))
                        at.tiles = s_v.n
                        s_v.inc(dve.memset(into[:, :], 0))
                        dve.wait_ge(s_pe.sem, 3)
                        s_v.inc(dve.tensor_copy(flat[:, 0:4 * ROWS], PS[0:1, 2, 0:4 * ROWS]))
                        s_v.link(dve, dve.tensor_copy(flat[:, 4 * ROWS:], PS[0:1, 3, 0:(tcols - 4) * ROWS]))
                        if into is bt:
                            s_v.link(dve, dve.tensor_copy(into[:, 0:nt].rearrange("p (g c) -> p c g", c=C),
                                                          flat[:, 0:nt].rearrange("p (c g) -> p c g", c=C)))
                        else:
                            s_v.link(dve, dve.tensor_copy(into[:, 0:nt], flat[:, 0:nt]))
                    else:
                        s_v.link(dve, dve.tensor_tensor_scan(beg[:, 0:bins], unit[:, 0:bins], tot[:, 0:bins], 0.0,
                                                             ALU.mult, ALU.add))
                        s_v.link(dve, dve.tensor_tensor(beg[:, 0:bins], beg[:, 0:bins], tot[:, 0:bins], ALU.subtract))
                    if bins % 2:
                        s_v.link(dve, dve.memset(beg[:, bins:bins + 1], 0.0))
                    s_v.link(dve, dve.scalar_tensor_tensor(off[:, 0:2 * pairs], beg[:, 0:2 * pairs], -1.0,
                                                           PS[0:ROWS, 0, 0:2 * pairs],
                                                           ALU.add, ALU.add))
                    if not later:
                        places = Places(s_v, s_gate, unit, dig, mask, run, pos, off)
                        with dve.Fori(0, pairs) as i:
                            t = Step(s_v, i, 6)
                            places.masks(dve, t, i, 0)
                            places.counts(dve, t, i, 0)
                            places.positions(dve, t, i, 0)
                        t.end(pairs)
                        s_v.wait(dve)
                        s_v.link(dve, dve.tensor_copy(pos_i, pos))

                @block.tensor
                def _(pe):
                    pe.wait_ge(s_v.sem, at.counted)
                    s_pe.inc(pe.matmul(PS[0:ROWS, 0, 0:64], lower[0:ROWS, 0:ROWS], cnt, start=True, stop=True))
                    s_pe.inc(pe.matmul(PS[0:ROWS, 1, 0:64], ones[0:ROWS, 0:ROWS], cnt, start=True, stop=True))
                    if bucket:
                        pe.wait_ge(s_v.sem, at.tiles)
                        for c in range(tcols):
                            m = pe.matmul(PS[0:1, 2 + c // 4, c % 4 * ROWS:(c % 4 + 1) * ROWS], tiles[:, c:c + 1],
                                          ident[0:ROWS, 0:ROWS], start=True, stop=True)
                        s_pe.inc(m)

                if bucket:
                    @block.gpsimd
                    def _(pool):
                        s_pool.inc(pool.iota(tile_no, [[ROWS, tcols]], base=0, channel_multiplier=1,
                                             allow_small_or_imprecise_dtypes=True))

            scatter = Scatter(rec, pos_i, cols, target)
            if later:
                scatter.pairs = pairs
                scatter.places = lambda count, gate: Places(count, gate, unit, dig, mask, run, pos, off)
                scatter.settle = lambda dve: dve.tensor_copy(pos_i, pos)
            return scatter

        def load_records(tag, source, buf=XT):
            sem = Phase()
            s_l = sem(tag + "_l")
            with sem.block() as block:
                @block.sync
                def _(sp):
                    s_l.inc(sp.dma_start(REC(ACOL, buf), source[:, :].rearrange("(p c) w -> p c w", p=ROWS)), 16)
                    s_l.wait(sp)

        def read_list(tag, source, rec):
            tiles = rec.shape[1]
            Q = tiles // 8
            assert Q * 8 == tiles and 4 * Q <= 512
            raw = over(TT, 0, [8 * P * 4], I32, Q)
            words = over(FW, 0, [4, 8, P], F32, Q)
            by_word = raw.rearrange("q (b e w) -> q w b e", e=P, w=4)
            to = rec.rearrange("p (q b) w -> p w b q", b=8)
            sem = Phase()
            s_l, s_w, s_t, s_c = sem(tag + "_l"), sem(tag + "_w"), sem(tag + "_t"), sem(tag + "_c")
            with sem.block() as block:
                @block.sync
                def _(sp):
                    s_l.inc(sp.dma_start(raw, source[:, :].rearrange("(q r) w -> q (r w)", q=Q)), 16)

                @block.vector
                def _(dve):
                    dve.wait_ge(s_l.sem, 16)
                    for w in range(4):
                        s_w.inc(dve.tensor_copy(words[:, w, :, :], by_word[:, w, :, :]))
                    for n in range(8):
                        dve.wait_ge(s_t.sem, n + 1)
                        s_c.inc(dve.tensor_copy(to[:, n // 2, n % 2 * 4:(n % 2 + 1) * 4, :],
                                                PS[:, n, 0:4 * Q].rearrange("p (b q) -> p b q", b=4)))

                @block.tensor
                def _(pe):
                    for n in range(8):
                        pe.wait_ge(s_w.sem, n // 2 + 1)
                        for b in range(4):
                            m = pe.transpose(PS[:, n, b * Q:(b + 1) * Q], words[:, n // 2, n % 2 * 4 + b, :], ident[0:Q, 0:Q])
                        m.then_inc(s_t.sem, 1)

        LAF = LA[:, :, :, :].rearrange("p g c h -> p (g c h)")

        PLACE = sb("place", [P, 2, 2 * P])

        def turn(tag, src, dst):
            sem = Phase()
            s_turned = [sem(f"{tag}_turned{h}") for h in range(2)]
            s_copied = [sem(f"{tag}_copied{h}") for h in range(2)]
            s_here = [sem(f"{tag}_here{h}") for h in range(2)]
            with sem.block() as block:
                @block.vector
                def _(dve):
                    for h in range(2):
                        dve.sem_inc(s_here[h].sem, 1)
                    with dve.Fori(0, G // 4) as i:
                        for h in range(2):
                            dve.wait_ge(s_turned[h].sem, i + 1)
                            dve.tensor_copy(PLACE[:, h, :], src[:, bass.ds((i * 4 + 2 * h) * P, 2 * P)])\
                                .then_inc(s_here[h].sem, 1)

                @block.tensor
                def _(pe):
                    for h in range(2):
                        pe.sem_inc(s_turned[h].sem, 1)
                    with pe.Fori(0, G // 4) as i:
                        for h in range(2):
                            pe.wait_ge(s_copied[h].sem, i + 1)
                            pe.wait_ge(s_here[h].sem, i + 2)
                            for j in range(2):
                                m = pe.transpose(PS[:, h, j * P:(j + 1) * P], PLACE[:, h, j * P:(j + 1) * P], ident[:, :])
                            m.then_inc(s_turned[h].sem, 1)

                @block.scalar
                def _(act):
                    for h in range(2):
                        act.sem_inc(s_copied[h].sem, 1)
                    with act.Fori(0, G // 4) as i:
                        for h in range(2):
                            act.wait_ge(s_turned[h].sem, i + 2)
                            act.activation(dst[:, bass.ds((i * 4 + 2 * h) * P, 2 * P)], PS[:, h, 0:2 * P], ACT.Copy)\
                               .then_inc(s_copied[h].sem, 1)

        def keys(tag, rec, shift, first):
            sem = Phase()
            s_v = sem(tag + "_v")
            keyf, tmp = over(FW, 0, [G, C]), over(FW, 2 * G * C, [G, C])
            keyi = over(FW, G * C, [G, C], I32)
            rep = over(TT, 0, [G, C, HD])
            by_group = rec.rearrange("p c g w -> p w g c")
            gc = lambda t: t[:, 0:G * C].rearrange("p (g c) -> p g c", c=C)
            with sem.block() as block:
                @block.vector
                def _(dve):
                    if first:
                        for index, w in ((src_i, 1), (eid_i, 2), (prj_i, 3)):
                            s_v.inc(dve.tensor_copy(gc(index), by_group[:, w]))
                        s_v.inc(dve.memset(dl[:, G * C:], NEG))
                        s_v.inc(dve.memset(dlm[:, G * C:], NEG))
                        s_v.inc(dve.tensor_copy(keyf, by_group[:, 0]))
                        s_v.link(dve, dve.tensor_copy(keyi, by_group[:, 0]))
                        s_v.link(dve, dve.tensor_scalar(keyi, keyi, 63, None, ALU.bitwise_and))
                        s_v.link(dve, dve.tensor_copy(gc(typ), keyi))
                        s_v.link(dve, dve.tensor_copy(keyi, by_group[:, 0]))
                        s_v.link(dve, dve.tensor_scalar(keyi, keyi, 6, P - 1, ALU.logical_shift_right, ALU.bitwise_and))
                        s_v.link(dve, dve.tensor_copy(tmp, keyi))
                        s_v.link(dve, dve.tensor_scalar(keyf, keyf, float(NIL * 64), NEG, ALU.is_ge, ALU.mult))
                        s_v.link(dve, dve.tensor_tensor(gc(dl), tmp, keyf, ALU.add))
                        s_v.link(dve, dve.tensor_scalar(tmp, gc(typ), float(TYPES), NEG, ALU.is_equal, ALU.mult))
                        s_v.link(dve, dve.tensor_tensor(gc(dlm), gc(dl), tmp, ALU.add))
                    s_v.link(dve, dve.tensor_copy(keyi, by_group[:, 0]))
                    if shift:
                        s_v.link(dve, dve.tensor_scalar(keyi, keyi, shift, None, ALU.logical_shift_right))
                    s_v.inc(dve.tensor_copy(rep, bc(keyi, 3, HD)))

        def flags(tag, flag, whole):
            sem = Phase()
            s_v, s_pe = sem(tag + "_v"), sem(tag + "_pe")
            with sem.block() as block:
                @block.tensor
                def _(pe):
                    pe.matmul(PS[:, 2, 0:1], up8[:, :], LAF[:, SEQ - 1:SEQ], start=True, stop=True)
                    pe.matmul(PS[:, 2, 1:2], down8[:, :], LAF[:, 0:1], start=True, stop=True).then_inc(s_pe.sem, 1)

                @block.vector
                def _(dve):
                    s_v.inc(dve.tensor_tensor(flag[:, 1:SEQ], LAF[:, 1:SEQ], LAF[:, 0:SEQ - 1], ALU.is_equal))
                    dve.wait_ge(s_pe.sem, 1)
                    s_v.inc(dve.tensor_tensor(flag[:, 0:1], LAF[:, 0:1], PS[:, 2, 0:1], ALU.is_equal))
                    s_v.inc(dve.tensor_tensor(flag[:, SEQ:SEQ + 1], LAF[:, SEQ - 1:SEQ], PS[:, 2, 1:2], ALU.is_equal))
                    s_v.wait(dve)
                    s_v.inc(dve.tensor_reduce(whole[:, 0:1], flag[:, 0:SEQ], AX.X, ALU.min))
                    s_v.inc(dve.tensor_reduce(whole[:, 1:2], flag[:, 1:SEQ + 1], AX.X, ALU.min))

        def source_tables():
            rec = over(XT, 0, [EG * C, 4], I32)
            read_list("sl", d_slist, rec)
            sem = Phase()
            s_v = sem("st_v")
            keyf, tmp = over(FW, 0, [EG * C]), over(FW, 2 * EG * C, [EG * C])
            keyi = over(FW, EG * C, [EG * C], I32)
            with sem.block() as block:
                @block.vector
                def _(dve):
                    s_v.inc(dve.memset(sdl[:, EG * C:], NEG))
                    s_v.inc(dve.tensor_copy(SDST[:, 0:EG * C], rec[:, :, 1]))
                    s_v.inc(dve.tensor_copy(SREL[:, 0:EG * C], rec[:, :, 2]))
                    s_v.inc(dve.tensor_copy(keyf, rec[:, :, 0]))
                    s_v.link(dve, dve.tensor_copy(keyi, rec[:, :, 0]))
                    s_v.link(dve, dve.tensor_scalar(keyi, keyi, P - 1, None, ALU.bitwise_and))
                    s_v.link(dve, dve.tensor_copy(tmp, keyi))
                    s_v.link(dve, dve.tensor_scalar(keyf, keyf, float(NIL), NEG, ALU.is_ge, ALU.mult))
                    s_v.inc(dve.tensor_tensor(sdl[:, 0:EG * C], tmp, keyf, ALU.add))

        SDST, SREL = src_i, eid_i

        WCAT = over(TT, 0, [512])
        BIAS = over(TT, 512, [512], F32, 1)
        XT5 = over(TT, 1024, [5, P])
        FIVE = over(TT, 1664, [5, P])
        STAGE = over(FW, 0, [5, 512])
        HID = over(LAF, 0, [NT, D])

        def project(tag, src, width, keep, adds, sends, beside=0, bias=True):
            sem = Phase()
            s_t, s_pe, s_a, s_v = sem(tag + "_t"), sem(tag + "_pe"), sem(tag + "_a"), sem(tag + "_v")
            s_st = [sem(f"{tag}_st{j}") for j in range(5)]
            s_here, s_stored = sem(tag + "_here"), sem(tag + "_stored")
            turns, whole = NT // 5, 16 * len(sends)
            qt = QT[:, 0:NT * keep].rearrange("p (t q) -> p t q", q=keep)
            with sem.block(beside) as block:
                @block.tensor
                def _(pe):
                    def turn_tile(j):
                        pe.transpose(PS[:, j % 2, 0:P], FIVE[:, j, :], ident[:, :]).then_inc(s_t.sem, 1)

                    with pe.Fori(0, turns) as i:
                        pe.wait_ge(s_here.sem, i + 1)
                        turn_tile(0)
                        for j in range(5):
                            if j < 4:
                                turn_tile(j + 1)
                            pe.wait_ge(s_a.sem, i * 5 + j + 1)
                            pe.wait_ge(s_v.sem, i * 5 + j + 1)
                            m = pe.matmul(PS[:, 2 + j, 0:width], XT5[:, j, :], WCAT[:, 0:width], start=True, stop=not bias)
                            if bias:
                                m = pe.matmul(PS[:, 2 + j, 0:width], ones[0:1, :], BIAS[:, 0:width], start=False, stop=True)
                            m.then_inc(s_pe.sem, 1)

                @block.scalar
                def _(act):
                    act.sem_inc(s_t.sem, 1)
                    with act.Fori(0, turns) as i:
                        act.wait_ge(s_t.sem, i * 5 + 1)
                        act.activation(FIVE, src[:, bass.ds(i * 5, 5), :], ACT.Copy).then_inc(s_here.sem, 1)
                        for j in range(5):
                            act.wait_ge(s_t.sem, i * 5 + j + 2)
                            act.activation(XT5[:, j, :], PS[:, j % 2, 0:P], ACT.Copy).then_inc(s_a.sem, 1)

                @block.vector
                def _(dve):
                    dve.sem_inc(s_v.sem, 5)
                    dve.sem_inc(s_stored.sem, 5)
                    with dve.Fori(0, turns) as i:
                        for j in range(5):
                            dve.wait_ge(s_pe.sem, i * 5 + j + 1)
                            at = bass.ds(i * 5 + j, 1)
                            dve.tensor_copy(qt[:, at, :], PS[:, 2 + j:3 + j, 0:keep])
                            if adds:
                                dve.tensor_tensor(ACC[:, at, 0:D], PS[:, 2 + j:3 + j, adds[0]:adds[1]],
                                                  src[:, at, :], ALU.add)
                            a, b = sends[0][0], sends[-1][1]
                            dve.wait_ge(s_stored.sem, i * 5 + j + 1)
                            dve.tensor_copy(STAGE[:, j:j + 1, 0:b - a], PS[:, 2 + j:3 + j, a:b]).then_inc(s_v.sem, 1)

                @block.sync
                def _(sp):
                    base = sends[0][0]
                    with sp.Fori(0, turns) as i:
                        for j in range(5):
                            sp.wait_ge(s_v.sem, i * 5 + j + 6)
                            for a, b, table in sends:
                                sp.dma_start(table[:, :].rearrange("(t p) d -> p t d", p=P)[:, bass.ds(i * 5 + j, 1), :],
                                             STAGE[:, j:j + 1, a - base:b - base]).then_inc(s_st[j].sem, 16)
                        for j in range(5):
                            sp.wait_ge(s_st[j].sem, i * whole + whole)
                            sp.sem_inc(s_stored.sem, 1)

        class Norms:

            def __init__(self, s_v, s_a):
                self.s_v, self.s_a, self.asked = s_v, s_a, []
                self.mean, self.var = over(TT, 4096, [NT]), over(TT, 4096 + NT, [NT])

            def norm(self, dve, x, scratch, gamma=None, beta=None):
                v, mean, var = self.s_v, self.mean, self.var
                v.link(dve, dve.tensor_reduce(mean, x, AX.X, ALU.add))
                v.link(dve, dve.tensor_scalar(mean, mean, 1.0 / D, None, ALU.mult))
                v.link(dve, dve.tensor_tensor(x, x, bc(mean, 2, D), ALU.subtract))
                v.link(dve, dve.tensor_tensor(scratch, x, x, ALU.mult))
                v.link(dve, dve.tensor_reduce(var, scratch, AX.X, ALU.add))
                v.link(dve, dve.tensor_scalar(var, var, 1.0 / D, 1e-5, ALU.mult, ALU.add))
                self.asked.append(v.n)
                dve.wait_ge(self.s_a.sem, len(self.asked))
                v.link(dve, dve.reciprocal(var, var))
                v.link(dve, dve.tensor_tensor(x, x, bc(var, 2, D), ALU.mult))
                if gamma is not None:
                    v.link(dve, dve.tensor_tensor(x, x, bc(gamma, 1, NT), ALU.mult))
                    v.link(dve, dve.tensor_tensor(x, x, bc(beta, 1, NT), ALU.add))

            def roots(self, act):
                for n in self.asked:
                    act.wait_ge(self.s_v.sem, n)
                    act.activation(self.var, self.var, ACT.Sqrt).then_inc(self.s_a.sem, 1)

        row_of = lambda name: A[name].rearrange("(a n) -> a n", a=1)
        rows_of = lambda name: row_of(name).to_broadcast([P, D])

        T = STEPS
        RING = over(XT, 0, [T, U, 2 * D])
        RING2 = over(XT, T * U * 2 * D, [T, U, ED])
        IDX = over(XT, T * U * (2 * D + ED), [T, U], U32)
        IDX2 = over(XT, T * U * (2 * D + ED + 1), [T, U], U32)
        OH16 = over(FW, 0, [2, U, P], BF16)
        OHT = over(FW, 1024, [2, U, P])
        ATT = over(FW, 2048, [2, U, P], F32, ED)
        SUM = over(FW, 3072, [2, U, D])
        PROD = over(FW, 4096, [2, U, D])
        VOUT = over(TT, 0, [T, U, D])
        WE = over(TT, 2048, [D], F32, ED)
        ATTW = over(TT, 3072, [D])
        TOH = over(TT, 2304, [2, U, TYPES])
        SMALL = over(TT, 2560, [6, U])

        def one_hot(eng, to, labels, at):
            return eng.tensor_tensor(to, bc(iota16[:, :], 1, U), bc(labels[:, bass.ds(at, U)], 2, P), ALU.is_equal)

        def distance(eng, to, labels, at):
            return eng.tensor_tensor(to, bc(iota16[:, :], 1, U), bc(labels[:, bass.ds(at, U)], 2, P), ALU.subtract)

        def ask(dve, idx, rows, at):
            return dve.tensor_copy(idx, rows[:, bass.ds(at, U)])

        def gather(pool, idx, table, ring, s_land):
            for j in range(U):
                pool.indirect_dma_start(out=ring[:, j, :], out_offset=None, in_=table,
                                        in_offset=bass.IndirectOffsetOnAxis(ap=idx[:, j:j + 1], axis=0))\
                    .then_inc(s_land.sem, 16)

        def tiles_of(eng, which, table, at):
            _, tiles = nc.values_load_multi_w_load_instructions(
                table[0:1, bass.ds(at, C)], engines=(which,), min_val=0, max_val=NT - 1,
                skip_runtime_bounds_check_because="the sort writes tile numbers below NT")
            return tiles

        def scores(tag, kind, table, width, qw):
            mha, rules, gat = kind == "mha", kind == "rules", kind == "gatv2"
            sem = Phase()
            s_done = sem(tag + "_done")
            s_gate, s_gate2 = sem(tag + "_gate"), sem(tag + "_gate2")
            s_land = sem.rows_moved(T)
            s_spill, s_stored = [sem(f"{tag}_spill{k}") for k in range(T)], sem(tag + "_stored")
            s_oh, s_ohT, s_ohc, s_q = (sem(tag + x) for x in ("_oh", "_ohT", "_ohc", "_q"))
            s_v, s_at, s_atc, s_e = sem(tag + "_v"), sem(tag + "_at"), sem(tag + "_atc"), sem(tag + "_e")
            qt = QT[:, 0:NT * qw].rearrange("p (t q) -> p t q", q=qw)
            gathers = 2 if mha else 1
            landed = 16 * U * gathers
            ops = {"mha": 3, "rules": 6, "gatv2": 3}[kind]

            def turned(b):
                return PS[:, b, 0:U * P // 2].bitcast(BF16).rearrange("p (a d) -> p a d", d=P)

            def qps(b):
                if rules:
                    return PS[:, 2 + 2 * b:4 + 2 * b, :].rearrange("p b (a d) -> p (b a) d", d=256)
                return PS[:, 2 + b, :].rearrange("p (a d) -> p a d", d=D)

            with sem.block() as block:
                @block.gpsimd
                def _(pool):
                    with pool.Fori(0, G) as i:
                        for k in range(T):
                            if gat:
                                pool.wait_ge(s_stored.sem, i * T + k + 1)
                            pool.wait_ge(s_done.sem, i * T + k + 1)
                            pool.sem_inc(s_gate.sem, 1)
                            gather(pool, IDX[:, k, :], table[:, :], RING[:, k, :, 0:width], s_land[k])
                            if mha:
                                gather(pool, IDX2[:, k, :], A["edge_attr_64"][:, :], RING2[:, k, :, :], s_land[k])

                @block.vector
                def _(dve):
                    def ask_step(k, at):
                        if mha:
                            ask(dve, IDX2[:, k, :], eid_i, at)
                        ask(dve, IDX[:, k, :], src_i, at).then_inc(s_done.sem, 1)

                    for k in range(T):
                        ask_step(k, k * U)
                    for b in range(2):
                        one_hot(dve, OH16[:, b, :, :], dl, b * U).then_inc(s_oh.sem, 1)
                    with dve.Fori(0, G) as i:
                        t = Step(s_v, i, T * ops)
                        for k in range(T):
                            b = k % 2
                            dve.wait_ge(s_ohT.sem, i * T + k + 1)
                            one_hot(dve, OH16[:, b, :, :], dl, i * C + (k + 2) * U).then_inc(s_oh.sem, 1)
                            dve.wait_ge(s_land[k].sem, i * landed + (s_land[k].n + landed))
                            dve.wait_ge(s_q.sem, i * T + k + 1)
                            q = qps(b)
                            la = LA[:, bass.ds(i, 1), k * U:(k + 1) * U, :].rearrange("p g u h -> p (g u) h")
                            x = RING[:, k, :, 0:D]
                            if mha:
                                dve.wait_ge(s_e.sem, i * T + k + 1)
                                edge = PS[:, 4 + b, :].rearrange("p (a d) -> p a d", d=D)
                                dve.wait_ge(s_stored.sem, i * T + k + 1)
                                t.inc(dve.tensor_tensor(VOUT[:, k, :, :], RING[:, k, :, D:2 * D], edge, ALU.add))
                                t.link(dve, dve.tensor_tensor(SUM[:, b, :, :], x, edge, ALU.add))
                                t.link(dve, dve.tensor_tensor(PROD[:, b, :, :], SUM[:, b, :, :], q, ALU.mult))
                                dve.tensor_reduce(la, PROD[:, b, :, :].rearrange("p a (h c) -> p a h c", h=HD), AX.X, ALU.add)
                            elif gat:
                                t.link(dve, dve.tensor_tensor(SUM[:, b, :, :], x, q, ALU.add))
                                t.link(dve, dve.scalar_tensor_tensor(PROD[:, b, :, :], SUM[:, b, :, :], 0.2,
                                                                     SUM[:, b, :, :], ALU.mult, ALU.max))
                                t.link(dve, dve.tensor_tensor(SUM[:, b, :, :], PROD[:, b, :, :], bc(ATTW, 1, U), ALU.mult))
                                dve.tensor_reduce(la[:, :, 0:4], SUM[:, b, :, :].rearrange("p a (h c) -> p a h c", h=4),
                                                         AX.X, ALU.add)
                            else:
                                base, rel, both = (SMALL[:, 3 * b + n, :] for n in range(3))
                                kinds = bc(typ[:, bass.ds(i * C + k * U, U)], 2, TYPES)
                                t.inc(dve.tensor_tensor(PROD[:, b, :, :], x, q[:, :, 0:D], ALU.mult))
                                t.link(dve, dve.tensor_tensor(TOH[:, b, :, :], bc(iota16[:, 0:TYPES], 1, U), kinds, ALU.is_equal))
                                t.inc(dve.tensor_reduce(base, PROD[:, b, :, :], AX.X, ALU.add))
                                t.link(dve, dve.tensor_tensor(TOH[:, b, :, :], TOH[:, b, :, :], q[:, :, D:D + TYPES], ALU.mult))
                                t.link(dve, dve.tensor_reduce(rel, TOH[:, b, :, :], AX.X, ALU.add))
                                t.link(dve, dve.tensor_tensor(both, base, rel, ALU.add))
                                dve.tensor_tensor(la[:, :, 0:4], bc(both, 2, 4), q[:, :, D + TYPES:LQ], ALU.add)
                            ask_step(k, i * C + (C + k * U))
                    t.end(G)

                @block.tensor
                def _(pe):
                    def turn_one_hots(b):
                        for j in range(U):
                            m = pe.transpose(turned(b)[:, j, :], OH16[:, b, j, :], ident16[:, :])
                        m.then_inc(s_ohT.sem, 1)

                    def products(b, tiles):
                        for j in range(U):
                            m = pe.matmul(qps(b)[:, j, 0:qw], OHT[:, b, j, :],
                                          qt[:, bass.ds(tiles[j], 1), :].rearrange("p a q -> p (a q)"),
                                          start=True, stop=True)
                        m.then_inc(s_q.sem, 1)

                    for b in range(2):
                        pe.wait_ge(s_oh.sem, b + 1)
                        turn_one_hots(b)
                    pe.wait_ge(s_ohc.sem, 1)
                    products(0, tiles_of(pe, ENG.PE, bt, 0))
                    with pe.Fori(0, G) as i:
                        tiles = tiles_of(pe, ENG.PE, bt, i * C + U)
                        for k in range(T):
                            b = k % 2
                            if mha:
                                pe.wait_ge(s_land[k].sem, i * landed + (s_land[k].n + landed))
                                pe.sem_inc(s_gate2.sem, 1)
                                for j in range(U):
                                    m = pe.transpose(PS[0:ED, 6 + b, j * P:(j + 1) * P], RING2[:, k, j, :], ident[:, :])
                                m.then_inc(s_at.sem, 1)
                            pe.wait_ge(s_ohc.sem, i * T + k + 2)
                            pe.wait_ge(s_done.sem, i * T + k + 4)
                            products(1 - b, tiles[k * U:(k + 1) * U])
                            pe.wait_ge(s_oh.sem, i * T + k + 3)
                            turn_one_hots(b)
                            if mha:
                                pe.wait_ge(s_atc.sem, i * T + k + 1)
                                for j in range(U):
                                    m = pe.matmul(PS[:, 4 + b, j * P:(j + 1) * P], ATT[:, b, j, :], WE,
                                                  start=True, stop=True)
                                m.then_inc(s_e.sem, 1)

                @block.scalar
                def _(act):
                    def copy_one_hots(b):
                        act.activation(OHT[:, b, :, :], turned(b), ACT.Copy).then_inc(s_ohc.sem, 1)

                    for b in range(2):
                        act.wait_ge(s_ohT.sem, b + 1)
                        copy_one_hots(b)
                    with act.Fori(0, G) as i:
                        for k in range(T):
                            b = k % 2
                            if mha:
                                act.wait_ge(s_at.sem, i * T + k + 1)
                                act.activation(ATT[:, b, :, :].rearrange("p a d -> p (a d)"), PS[0:ED, 6 + b, :], ACT.Copy)\
                                   .then_inc(s_atc.sem, 1)
                            act.wait_ge(s_ohT.sem, i * T + k + 3)
                            act.wait_ge(s_q.sem, i * T + k + 1)
                            copy_one_hots(b)

                @block.sync
                def _(sp):
                    if not rules:
                        def stored(i, k):
                            sp.wait_ge(s_spill[k].sem, i * 16 + 16)
                            sp.sem_inc(s_stored.sem, 1)

                        sp.sem_inc(s_stored.sem, T)
                        with sp.Fori(0, G) as i:
                            for k in range(T):
                                if mha:
                                    sp.wait_ge(s_v.sem, i * (T * ops) + k * ops + 1)
                                else:
                                    sp.wait_ge(s_land[k].sem, i * landed + (s_land[k].n + landed))
                                rows = VOUT[:, k, :, :] if mha else RING[:, k, :, 0:D]
                                sp.dma_start(d_spill[bass.ds(i, 1), :, k * U:(k + 1) * U, :]
                                             .rearrange("g p c d -> (g p) c d"), rows).then_inc(s_spill[k].sem, 16)
                                if k:
                                    stored(i, k - 1)
                            stored(i, T - 1)

            for k in range(T):
                s_land[k].n += landed * G

        carry = sb("carry", [P, 4])
        row = sb("row", [1, P + 2 * HD])
        rowf = sb("rowf", [1, P])
        whole_d = sb("whole_d", [P, 2])
        whole_k = sb("whole_k", [P, 2])
        ALPHA = QT[:, 0:G * C]

        def softmax(tag, flag, whole, divide, scale=1.0):
            sem = Phase()
            s_v, s_pe, s_a = sem(tag + "_v"), sem(tag + "_pe"), sem(tag + "_a")
            stages = []
            heads = [lambda t, o, h=h: t[0:1, o:o + P].rearrange("p (c h) -> p h c", h=HD)[:, h, :] for h in range(HD)]
            back = lambda ap: ap[:, ::-1]
            with sem.block() as block:
                @block.vector
                def _(dve):
                    v = s_v

                    def product(what):
                        stages.append((v.n, what))
                        dve.wait_ge(s_pe.sem, len(stages))

                    def carried(last, kind):
                        v.link(dve, dve.tensor_copy(carry[:, 0:1], last))
                        v.link(dve, dve.tensor_copy(carry[:, 1:2], whole[:, 1:2] if kind == "back" else whole[:, 0:1]))
                        product("row")
                        neutral = -BIG if kind == "max" else 0.0
                        v.link(dve, dve.memset(row[:, :], neutral))
                        if kind == "max":
                            v.link(dve, dve.tensor_scalar(rowf[:, :], PS[0:1, 1, 0:P], BIG, -BIG, ALU.mult, ALU.add))
                        else:
                            v.link(dve, dve.tensor_copy(rowf[:, :], PS[0:1, 1, 0:P]))
                        for h in range(HD):
                            f, x = heads[h](rowf, 0), PS[0:1, 0, 0:P].rearrange("p (c h) -> p h c", h=HD)[:, h, :]
                            if kind == "back":
                                v.inc(dve.tensor_tensor_scan(back(heads[h](row, 0)), back(f), back(x), 0.0, ALU.mult, ALU.add))
                            elif kind == "max":
                                v.inc(dve.tensor_tensor_scan(heads[h](row, 2 * HD), f, x, neutral, ALU.add, ALU.max))
                            else:
                                v.inc(dve.tensor_tensor_scan(heads[h](row, 2 * HD), f, x, 0.0, ALU.mult, ALU.add))
                        v.wait(dve)
                        product("column")
                        v.link(dve, dve.tensor_copy(carry[:, 2:3], PS[:, 2, 0:1]))

                    def last_value_back():
                        v.link(dve, dve.scalar_tensor_tensor(LAF, flag[:, 1:SEQ + 1], 1.0, FW[:, :], ALU.not_equal, ALU.mult))
                        run = lambda init: dve.tensor_tensor_scan(back(TT), back(flag[:, 1:SEQ + 1]), back(LAF), init,
                                                                  ALU.mult, ALU.add)
                        v.link(dve, run(0.0))
                        carried(TT[:, 0:1], "back")
                        v.link(dve, run(carry[:, 2:3]))

                    v.link(dve, dve.tensor_scalar(TT[:, :], flag[:, 0:SEQ], BIG, -BIG, ALU.mult, ALU.add))
                    v.link(dve, dve.tensor_tensor_scan(FW[:, :], TT[:, :], XT[:, :], -BIG, ALU.add, ALU.max))
                    carried(FW[:, SEQ - 1:SEQ], "max")
                    v.link(dve, dve.tensor_tensor_scan(FW[:, :], TT[:, :], XT[:, :], carry[:, 2:3], ALU.add, ALU.max))
                    last_value_back()
                    v.link(dve, dve.tensor_tensor(XT[:, :], XT[:, :], TT[:, :], ALU.subtract))
                    at.shifted = v.n
                    if divide:
                        dve.wait_ge(s_a.sem, 1)
                        sums = lambda init: dve.tensor_tensor_scan(FW[:, :], flag[:, 0:SEQ], XT[:, :], init, ALU.mult, ALU.add)
                        v.link(dve, sums(0.0))
                        carried(FW[:, SEQ - 1:SEQ], "sum")
                        v.link(dve, sums(carry[:, 2:3]))
                        last_value_back()
                        v.link(dve, dve.reciprocal(TT[:, :], TT[:, :]))
                        v.link(dve, dve.tensor_tensor(XT[:, :], XT[:, :], TT[:, :], ALU.mult))

                @block.tensor
                def _(pe):
                    for n, what in stages:
                        pe.wait_ge(s_v.sem, n)
                        if what == "row":
                            pe.matmul(PS[0:1, 0, 0:P], carry[:, 0:1], ident[:, :], start=True, stop=True)
                            pe.matmul(PS[0:1, 1, 0:P], carry[:, 1:2], ident[:, :], start=True, stop=True)\
                              .then_inc(s_pe.sem, 1)
                        else:
                            pe.matmul(PS[:, 2, 0:1], row[0:1, HD:HD + P], ones[0:1, 0:1], start=True, stop=True)\
                              .then_inc(s_pe.sem, 1)

                @block.scalar
                def _(act):
                    act.wait_ge(s_v.sem, at.shifted)
                    act.activation(XT[:, :], XT[:, :], ACT.Exp, scale=scale).then_inc(s_a.sem, 1)

        at = Marks()

        VIN = over(XT, 0, [T, U, D])
        MSG = over(XT, 2048, [T, U, D + HD])
        IDX3 = over(XT, 4240, [T, U], U32)
        OH4 = over(FW, 0, [T, U, P])
        SUMS = over(TT, 0, [NT, D + HD]), over(FW, T * U * P, [NT, D + HD])

        def aggregate(tag, labels, heads, table, add, eps=0.0):
            sem = Phase()
            s_v, s_sum, s_gate = sem(tag + "_v"), sem(tag + "_sum"), sem(tag + "_gate")
            s_land = [sem(f"{tag}_land{k}") for k in range(T)] if table is None else sem.rows_moved(T)
            s_end = sem(tag + "_end")
            W = D + heads
            landed = 16 if table is None else 16 * U
            s_oh, s_dist, s_sq = sem(tag + "_oh"), sem(tag + "_dist"), sem(tag + "_sq")
            hot = lambda k: OH4[:, k]
            spilled = table is None
            maker = 1 if spilled else 3
            order = []
            for k in range(T):
                order += [("build", (k + 2) % T), ("add", k)]
            after, n = {}, 0
            for what, k in order:
                n += maker if what == "build" else U
                after[what, k] = n
            per = n
            sums = lambda k: PS[:, 2 * k:2 * k + 2, :].rearrange("p b (a d) -> p (b a) d", d=256)
            start = (1 if spilled else 2) + 2 * (maker + U)
            ready = lambda i, k: i * per + (start + after["build", k] - (per if k < 2 else 0))

            with sem.block() as block:
                @block.vector
                def _(dve):
                    def build(t, i, k):
                        if not spilled:
                            t.inc(one_hot(dve, hot(k), labels, i * C + k * U))
                        dve.wait_ge(s_land[k].sem, i * landed + (s_land[k].n + landed))
                        if heads:
                            w = D // heads
                            la = LA[:, bass.ds(i, 1), k * U:(k + 1) * U, 0:heads].rearrange("p g u h -> p (g u) h")
                            t.inc(dve.tensor_tensor(MSG[:, k, :, 0:D].rearrange("p a (h c) -> p a h c", h=heads),
                                                    VIN[:, k, :, :].rearrange("p a (h c) -> p a h c", h=heads),
                                                    bc(la, 3, w), ALU.mult))
                        else:
                            t.inc(dve.tensor_tensor(MSG[:, k, :, 0:D], VIN[:, k, :, :],
                                                    bc(ALPHA[:, bass.ds(i * C + k * U, U)], 2, D), ALU.mult))
                        if not spilled:
                            t.inc(ask(dve, IDX3[:, k, :], prj_i, i * C + (C + k * U)))

                    def turn_of(i, last):
                        tiles = None
                        t = Step(s_v, 0 if last else i, per)
                        for what, k in order:
                            if what == "build":
                                if k >= 2:
                                    build(t, i, k)
                                elif not last:
                                    build(t, i + 1, k)
                                if tiles is None:
                                    tiles = tiles_of(dve, ENG.DVE, bt, i * C)
                            else:
                                dve.wait_ge(s_sum.sem, i * T + (k + 1))
                                for j in range(U):
                                    acc = SUMS[j % 2][:, bass.ds(tiles[k * U + j], 1), 0:W]
                                    t.wait_for(dve, t.k - 1)
                                    t.inc(dve.tensor_tensor(acc, acc, sums(k)[:, j:j + 1, 0:W], ALU.add))
                        return t

                    dve.memset(SUMS[0], 0.0)
                    s_v.inc(dve.memset(SUMS[1], 0.0))
                    if not spilled:
                        for k in range(1, T):
                            ask(dve, IDX3[:, k, :], prj_i, k * U)
                        s_v.inc(ask(dve, IDX3[:, 0, :], prj_i, 0))
                    for k in range(2):
                        build(s_v, 0, k)
                        s_v.wait(dve)
                        dve.sem_inc(s_v.sem, U)
                        s_v.n += U
                    assert s_v.n == start
                    with dve.Fori(0, G - 1) as i:
                        t = turn_of(i, False)
                    t.end(G - 1)
                    t = turn_of(G - 1, True)
                    t.wait(dve)
                    total = SUMS[0][:, :, 0:W]
                    s_end.link(dve, dve.tensor_tensor(total, total, SUMS[1][:, :, 0:W], ALU.add))
                    rows = total[:, :, 0:D]
                    if heads:
                        Z = over(XT, 4300, [NT, heads])
                        s_end.link(dve, dve.tensor_scalar(Z, total[:, :, D:W], 1.0, eps, ALU.max, ALU.add))
                        s_end.link(dve, dve.reciprocal(Z, Z))
                        by_head = lambda t: t.rearrange("p a (h c) -> p a h c", h=heads)
                        to = rows if add else ACC[:, :, 0:D]
                        s_end.link(dve, dve.tensor_tensor(by_head(to), by_head(rows), bc(Z, 3, D // heads), ALU.mult))
                    if add:
                        s_end.inc(dve.tensor_tensor(ACC[:, :, 0:D], ACC[:, :, 0:D], rows, ALU.add))
                    elif not heads:
                        s_end.inc(dve.tensor_copy(ACC[:, :, 0:D], rows))

                @block.tensor
                def _(pe):
                    with pe.Fori(0, G) as i:
                        for k in range(T):
                            pe.wait_ge(s_v.sem, ready(i, k))
                            if spilled:
                                pe.wait_ge(s_oh.sem, i * T + (k + 1))
                            for j in range(U):
                                m = pe.matmul(sums(k)[:, j, 0:W], hot(k)[:, j, :], MSG[:, k, j, 0:W], start=True, stop=True)
                            m.then_inc(s_sum.sem, 1)

                if spilled:
                    @block.gpsimd
                    def _(pool):
                        for k in range(T):
                            distance(pool, hot(k), labels, k * U).then_inc(s_dist.sem, 1)
                        with pool.Fori(1, G) as i:
                            for k in range(T):
                                pool.wait_ge(s_sum.sem, i * T + (k + 1 - T))
                                distance(pool, hot(k), labels, i * C + k * U).then_inc(s_dist.sem, 1)

                    @block.scalar
                    def _(act):
                        act.sem_inc(s_sq.sem, 1)
                        with act.Fori(0, G) as i:
                            for k in range(T):
                                act.wait_ge(s_dist.sem, i * T + (k + 1))
                                act.activation(MSG[:, k, :, D:W],
                                               LA[:, bass.ds(i, 1), k * U:(k + 1) * U, 0:heads].rearrange("p g u h -> p (g u) h"),
                                               ACT.Copy)
                                act.activation(hot(k), hot(k), ACT.Square).then_inc(s_sq.sem, 1)
                                act.wait_ge(s_sq.sem, i * T + (k + 2))
                                act.activation(hot(k), hot(k), ACT.Relu, bias=ones[:, 0:1], scale=-1.0)\
                                   .then_inc(s_oh.sem, 1)

                    @block.sync
                    def _(sp):
                        def load(i, k):
                            sp.dma_start(VIN[:, k, :, :], d_spill[bass.ds(i, 1), :, k * U:(k + 1) * U, :]
                                         .rearrange("g p c d -> (g p) c d")).then_inc(s_land[k].sem, 16)

                        for k in range(T):
                            load(0, k)
                        with sp.Fori(1, G) as i:
                            for k in range(T):
                                sp.wait_ge(s_v.sem, ready(i - 1, k))
                                load(i, k)
                else:
                    @block.gpsimd
                    def _(pool):
                        pool.wait_ge(s_v.sem, 2)
                        pool.sem_inc(s_gate.sem, 1)
                        for k in range(T):
                            gather(pool, IDX3[:, k, :], table[:, :], VIN[:, k, :, :], s_land[k])
                        with pool.Fori(1, G) as i:
                            for k in range(T):
                                pool.wait_ge(s_v.sem, ready(i - 1, k))
                                pool.sem_inc(s_gate.sem, 1)
                                gather(pool, IDX3[:, k, :], table[:, :], VIN[:, k, :, :], s_land[k])

            for k in range(T):
                s_land[k].n += landed * G

        def layer0_tables():
            W1 = over(FW, 0, [3, D])
            W1T = over(XT, 0, [3, D])
            w2 = over(FW, 400, [1])
            REL = over(FW, 512, [4, D], F32, ROWS)
            RELT = over(FW, 1024, [4, ROWS])
            WREL = over(FW, 2048, [W0])
            BX = over(FW, 2304, [4, W0], F32, ROWS)
            sem = Phase()
            s_l, s_v, s_pe = sem("l0w_l"), sem("l0w_v"), sem("l0w_pe")
            with sem.block(1) as block:
                @block.sync
                def _(sp):
                    s_l.inc(sp.dma_start(W1, A["L0_gnn_W_e1"].rearrange("d (a f) -> d a f", a=3)), 16)
                    s_l.inc(sp.dma_start(w2, A["L0_gnn_W_e2"].rearrange("a d -> d a")), 16)
                    s_l.inc(sp.dma_start(REL, A["L0_gnn_rel_embedding"].rearrange("(t p) d -> p t d", p=ROWS)), 16)
                    sp.wait_ge(s_v.sem, 8)
                    s_l.inc(sp.dma_start(d_rel[0:RELS, :].rearrange("(t p) d -> p t d", p=ROWS), BX), 16)
                    s_l.wait(sp)

                @block.tensor
                def _(pe):
                    pe.wait_ge(s_l.sem, 48)
                    for a in range(3):
                        pe.transpose(PS[:, 0, a * P:(a + 1) * P], W1[:, a, :], ident[:, :])
                        pe.matmul(PS[:, 1, a:a + 1], W1[:, a, :], w2, start=True, stop=True)
                    for r in range(4):
                        m = pe.transpose(PS[:, 2, r * P:r * P + ROWS], REL[:, r, :], ident[0:ROWS, 0:ROWS])
                    m.then_inc(s_pe.sem, 1)
                    pe.wait_ge(s_v.sem, 7)
                    for r in range(4):
                        m = pe.matmul(PS[0:ROWS, 3 + r, 0:D + 1], RELT[:, r, :], WREL[:, 0:D + 1], start=True, stop=True)
                    m.then_inc(s_pe.sem, 1)

                @block.vector
                def _(dve):
                    s_v.inc(dve.memset(BIAS, 0.0))
                    s_v.inc(dve.memset(WCAT, 0.0))
                    s_v.inc(dve.memset(BX, 0.0))
                    s_v.wait(dve)
                    dve.wait_ge(s_pe.sem, 1)
                    dve.tensor_copy(WCAT[:, 0:D], PS[:, 0, 0:D])
                    dve.tensor_copy(WCAT[:, D:D + 1], PS[:, 1, 0:1])
                    dve.tensor_copy(WCAT[:, D + 1:2 * D + 1], PS[:, 0, 2 * D:3 * D])
                    s_v.inc(dve.tensor_copy(WCAT[:, 2 * D + 1:2 * D + 2], PS[:, 1, 2:3]))
                    s_v.inc(dve.memset(BIAS[:, 2 * D + 2:2 * D + 3], 1.0))
                    dve.tensor_copy(WREL[:, 0:D], PS[:, 0, D:2 * D])
                    s_v.inc(dve.tensor_copy(WREL[:, D:D + 1], PS[:, 1, 1:2]))
                    s_v.inc(dve.tensor_copy(RELT, PS[:, 2, :].rearrange("p (r n) -> p r n", r=4)[:, :, 0:ROWS]))
                    dve.wait_ge(s_pe.sem, 2)
                    s_v.inc(dve.tensor_copy(BX[:, :, 0:D + 1], PS[0:ROWS, 3:7, 0:D + 1]))

            project("l0p", X, 2 * D + 3, D + 1, None, [(D + 1, 2 * D + 3, d_dst)], 2)

        QT0 = QT[:, 0:NT * (D + 1)].rearrange("p (t q) -> p t q", q=D + 1)

        def layer0_edges(tag, g0, g1, ranked, each):

            RA = over(XT, 0, [T, U, W0])
            RB = over(XT, 2304, [T, U, W0])
            I1, I2 = over(XT, 4608, [T, U], U32), over(XT, 4624, [T, U], U32)
            SC = over(XT, 4640, [T, 3, U])
            ONE = over(FW, 0, [T, U, P])
            ONET = over(FW, 2048, [T, U, P])
            sem = Phase()
            s_done, s_v, s_oh, s_t, s_sc, s_w, s_sum = (sem(tag + x) for x in
                                                        ("_done", "_v", "_oh", "_t", "_sc", "_w", "_sum"))
            s_tc, s_gate = sem(tag + "_tc"), sem(tag + "_gate")
            s_place, s_gate2 = sem(tag + "_place"), sem(tag + "_gate2")
            s_land = sem.rows_moved(T)
            landed = 32 * U
            turns, finding = g1 - g0, ranked.pairs // each
            assert finding * each == ranked.pairs and finding < turns
            order = [("rows", 0), ("messages", 0)]
            for k in range(1, T):
                order += [("rows", k), ("add", k - 1), ("messages", k)]
            order += [("add", T - 1)]
            after, n = {}, 0
            for part, k in order:
                n += {"rows": 3, "messages": 1, "add": U}[part]
                after[part, k] = n
            per = n
            sums = lambda b: PS[:, 2 * b:2 * b + 2, :].rearrange("p b (a d) -> p (b a) d", d=256)
            with sem.block() as block:
                @block.gpsimd
                def _(pool):
                    with pool.Fori(0, turns) as i:
                        for k in range(T):
                            pool.wait_ge(s_done.sem, i * T + k + 1)
                            pool.sem_inc(s_gate.sem, 1)
                            gather(pool, I1[:, k, :], d_dst[:, :], RA[:, k, :, :], s_land[k])
                            gather(pool, I2[:, k, :], d_rel[:, :], RB[:, k, :, :], s_land[k])

                @block.vector
                def _(dve):
                    def ask_step(k, at):
                        ask(dve, I1[:, k, :], SDST, at)
                        ask(dve, I2[:, k, :], SREL, at).then_inc(s_done.sem, 1)

                    for k in range(T):
                        ask_step(k, g0 * C + k * U)
                    for k in range(2):
                        one_hot(dve, ONE[:, k, :, :], sdl, g0 * C + k * U).then_inc(s_oh.sem, 1)
                    if g0 == 0:
                        s_v.link(dve, dve.memset(ACC[:, :, :], 0.0))
                    else:
                        dve.sem_inc(s_v.sem, 1)
                        s_v.n += 1
                    for n in range(2):
                        s_place.inc(dve.memset(SC[:, 0, n, :], 0.0))

                    def turn_of(i, finds):
                        tiles = tiles_of(dve, ENG.DVE, sbt, i * C + g0 * C)
                        t = Step(s_v, i, per)
                        t2 = Step(s_place, i, 6 * each)
                        for part, k in order:
                            total, leaky, weight = (SC[:, k, n, :] for n in range(3))
                            if part == "rows":
                                dve.wait_ge(s_land[k].sem, i * landed + (s_land[k].n + landed))
                                t.link(dve, dve.tensor_tensor(RA[:, k, :, :], RA[:, k, :, :], RB[:, k, :, :], ALU.add))
                                dve.wait_ge(s_sc.sem, i * T + k + 1)
                                t.link(dve, dve.tensor_tensor(total, RA[:, k, :, D], PS[:, 6 + k % 2, k * U:(k + 1) * U], ALU.add))
                                t.inc(dve.scalar_tensor_tensor(leaky, total, 0.2, total, ALU.mult, ALU.max))
                            elif part == "messages":
                                dve.wait_ge(s_w.sem, i * T + k + 1)
                                t.inc(dve.tensor_tensor(RA[:, k, :, :], RA[:, k, :, :], bc(weight, 2, W0), ALU.mult))
                                one_hot(dve, ONE[:, (k + 2) % T, :, :], sdl, i * C + (g0 * C + (k + 2) * U)).then_inc(s_oh.sem, 1)
                                for what, q in shares[k] if finds else ():
                                    what(dve, t2, i * each + q, 6 * q)
                            else:
                                dve.wait_ge(s_sum.sem, i * T + k + 1)
                                for j in range(U):
                                    acc = ACC[:, bass.ds(tiles[k * U + j], 1), :]
                                    t.link(dve, dve.tensor_tensor(acc, acc, sums(k % 2)[:, j:j + 1, 0:W0], ALU.add))
                                ask_step(k, i * C + (g0 * C + C + k * U))
                        return t2

                    places = ranked.places(s_place, s_gate2)
                    m, c, p = places.masks, places.counts, places.positions
                    shares = [[(m, 0)], [(c, 0)], [(p, 0)], []] if each == 1 else \
                        [[(m, 0), (c, 0)], [(p, 0)], [(m, 1), (c, 1)], [(p, 1)]]
                    with dve.Fori(0, finding) as i:
                        t2 = turn_of(i, True)
                    t2.end(finding)
                    with dve.Fori(finding, turns) as i:
                        turn_of(i, False)
                    s_v.n += turns * per
                    s_place.wait(dve)
                    s_place.inc(ranked.settle(dve))

                @block.tensor
                def _(pe):
                    def turn_one_hots(k):
                        for j in range(U):
                            m = pe.transpose(PS[:, 4, j * P:(j + 1) * P], ONE[:, k, j, :], ident[:, :])
                        m.then_inc(s_t.sem, 1)

                    def source_scores(k, tiles):
                        for j in range(U):
                            m = pe.matmul(PS[:, 6 + k % 2, k * U + j:k * U + j + 1], ONET[:, k, j, :],
                                          QT0[:, bass.ds(tiles[j], 1), D:D + 1].rearrange("p a q -> p (a q)"),
                                          start=True, stop=True)
                        m.then_inc(s_sc.sem, 1)

                    base = 1
                    pe.wait_ge(s_oh.sem, 1)
                    turn_one_hots(0)
                    pe.wait_ge(s_tc.sem, 1)
                    source_scores(0, tiles_of(pe, ENG.PE, sbt, g0 * C))
                    with pe.Fori(0, turns) as i:
                        tiles = tiles_of(pe, ENG.PE, sbt, i * C + (g0 * C + U))
                        for k in range(T):
                            nxt = (k + 1) % T
                            pe.wait_ge(s_oh.sem, i * T + k + 2)
                            turn_one_hots(nxt)
                            pe.wait_ge(s_tc.sem, i * T + k + 2)
                            source_scores(nxt, tiles[k * U:(k + 1) * U])
                            pe.wait_ge(s_v.sem, i * per + (base + after["messages", k]))
                            for j in range(U):
                                m = pe.matmul(sums(k % 2)[:, j, 0:W0], ONE[:, k, j, :], RA[:, k, j, :], start=True, stop=True)
                            m.then_inc(s_sum.sem, 1)

                @block.scalar
                def _(act):
                    def copy_one_hots(k):
                        act.activation(ONET[:, k, :, :].rearrange("p a d -> p (a d)"), PS[:, 4, :], ACT.Copy)\
                           .then_inc(s_tc.sem, 1)

                    act.wait_ge(s_t.sem, 1)
                    copy_one_hots(0)
                    with act.Fori(0, turns) as i:
                        for k in range(T):
                            act.wait_ge(s_t.sem, i * T + k + 2)
                            copy_one_hots((k + 1) % T)
                            act.wait_ge(s_v.sem, i * per + (1 + after["rows", k]))
                            act.activation(SC[:, k, 2, :], SC[:, k, 1, :], ACT.Exp, scale=-1.0).then_inc(s_w.sem, 1)

            for k in range(T):
                s_land[k].n += landed * turns

        def layer0_nodes():
            sem = Phase()
            s_v, s_a = sem("l0f_v"), sem("l0f_a")
            norms = Norms(s_v, s_a)
            S, Z = over(TT, 4200, [NT]), over(TT, 4232, [NT])
            own = over(FW, 0, [NT, D])
            with sem.block(2) as block:
                @block.vector
                def _(dve):
                    v = s_v
                    v.link(dve, dve.tensor_copy(S, ACC[:, :, D + 1]))
                    v.inc(dve.tensor_tensor(own, QT0[:, :, 0:D], bc(S, 2, D), ALU.mult))
                    v.inc(dve.tensor_scalar(Z, S, 0.0, 1e-12, ALU.is_equal, ALU.mult))
                    v.wait(dve)
                    v.link(dve, dve.tensor_tensor(Z, Z, S, ALU.add))
                    v.link(dve, dve.reciprocal(Z, Z))
                    v.link(dve, dve.tensor_tensor(own, own, ACC[:, :, 0:D], ALU.add))
                    v.link(dve, dve.tensor_tensor(own, own, bc(Z, 2, D), ALU.mult))
                    v.link(dve, dve.tensor_tensor(X[:, :, :], X[:, :, :], own, ALU.add))
                    norms.norm(dve, X[:, :, :], own)

                @block.scalar
                def _(act):
                    norms.roots(act)

        def layer1_tables():
            sem = Phase()
            s_l, s_v = sem("l1w_l"), sem("l1w_v")
            names = ("q", "k", "v", "skip")
            with sem.block(1) as block:
                @block.sync
                def _(sp):
                    for n, w in enumerate(names):
                        s_l.inc(sp.dma_start(WCAT[:, n * D:(n + 1) * D], A["L1_gnn_W" + w][:, :]), 16)
                        s_l.inc(sp.dma_start(BIAS[:, n * D:(n + 1) * D], row_of("L1_gnn_b" + w)), 16)
                    s_l.wait(sp)

                @block.vector
                def _(dve):
                    dve.wait_ge(s_l.sem, 128)
                    s_v.inc(dve.tensor_scalar(WCAT[:, 0:D], WCAT[:, 0:D], 0.25, None, ALU.mult))
                    s_v.inc(dve.tensor_scalar(BIAS[:, 0:D], BIAS[:, 0:D], 0.25, None, ALU.mult))

            project("l1p", X, 4 * D, D, (3 * D, 4 * D), [(D, 3 * D, d_kv)], 4)

        def layer1():
            sem = Phase()
            s_l = sem("l1e_l")
            with sem.block() as block:
                @block.sync
                def _(sp):
                    s_l.inc(sp.dma_start(WE, A["L1_gnn_We"][:, :]), 16)
                    s_l.wait(sp)

            scores("l1s", "mha", d_kv, 2 * D, D)

            sem = Phase()
            s_v = sem("l1m_v")
            off = over(FW, 0, [G, C])
            with sem.block() as block:
                @block.vector
                def _(dve):
                    s_v.link(dve, dve.tensor_scalar(off, dlm[:, 0:G * C].rearrange("p (g c) -> p g c", c=C),
                                                    NEG, -BIG, ALU.is_ge, ALU.mult))
                    s_v.inc(dve.tensor_tensor(LA[:, :, :, :], LA[:, :, :, :], bc(off, 3, HD), ALU.add))

            turn("l1ta", LAF, XT)
            softmax("l1x", cD, whole_d, False)
            turn("l1tb", XT, LAF)
            aggregate("l1g", dlm, HD, None, True)

            RWS = over(FW, 3200, [4, D])
            WF1 = over(FW, 3712, [4 * D])
            WF2 = over(FW, 4224, [4, D])
            BF1 = over(FW, 4736, [4])
            BF2 = over(TT, 4300, [D], F32, 1)
            H = ACC[:, :, 0:D]
            sem = Phase()
            s_l, s_v, s_a = sem("l1f_l"), sem("l1f_v"), sem("l1f_a")
            norms = Norms(s_v, s_a)
            with sem.block() as block:
                @block.sync
                def _(sp):
                    for n, w in enumerate(("g1", "b1", "g2", "b2")):
                        s_l.inc(sp.dma_start(RWS[:, n, :], rows_of("L1_gnn_" + w)), 16)
                    s_l.inc(sp.dma_start(WF1, A["L1_gnn_Wf1"][:, :]), 16)
                    s_l.inc(sp.dma_start(WF2, A["L1_gnn_Wf2"].rearrange("(c p) d -> p c d", p=P)), 16)
                    s_l.inc(sp.dma_start(BF1, A["L1_gnn_bf1"].rearrange("(c p) -> p c", p=P),
                                         allow_slow_non_contiguous=True), 16)
                    s_l.inc(sp.dma_start(BF2, row_of("L1_gnn_bf2")), 16)
                    s_l.wait(sp)

                @block.vector
                def _(dve):
                    dve.wait_ge(s_l.sem, 128)
                    norms.norm(dve, H, over(FW, 0, [NT, D]), RWS[:, 0, :], RWS[:, 1, :])

                @block.scalar
                def _(act):
                    norms.roots(act)

            hin, hT = over(TT, 0, [5, P]), over(TT, 640, [5, P])
            gT = over(TT, 1280, [5, 4, P])
            sem = Phase()
            s_t, s_tc, s_up, s_g, s_dn, s_add = (sem("ffn" + x) for x in ("_t", "_tc", "_up", "_g", "_dn", "_add"))
            s_here = sem("ffn_here")
            with sem.block() as block:
                @block.gpsimd
                def _(pool):
                    pool.sem_inc(s_t.sem, 1)
                    with pool.Fori(0, NT // 5) as i:
                        pool.wait_ge(s_t.sem, i * 5 + 1)
                        pool.tensor_copy(hin, H[:, bass.ds(i * 5, 5), :]).then_inc(s_here.sem, 1)

                @block.tensor
                def _(pe):
                    def up(i, j):
                        pe.transpose(PS[:, 0, 0:P], hin[:, j, :], ident[:, :]).then_inc(s_t.sem, 1)
                        pe.wait_ge(s_tc.sem, i * 5 + j + 1)
                        for c in range(4):
                            m = pe.matmul(PS[:, 1 + j, c * P:(c + 1) * P], WF1[:, c * P:(c + 1) * P], hT[:, j, :],
                                          start=True, stop=True)
                        m.then_inc(s_up.sem, 1)

                    pe.sem_inc(s_add.sem, 1)
                    with pe.Fori(0, NT // 5) as i:
                        pe.wait_ge(s_here.sem, i + 1)
                        up(i, 0)
                        for j in range(5):
                            if j < 4:
                                up(i, j + 1)
                            pe.wait_ge(s_g.sem, (i * 5 + j) * 4 + 4)
                            pe.wait_ge(s_add.sem, i * 5 + j + 1)
                            for c in range(4):
                                pe.matmul(PS[:, 6, 0:D], gT[:, j, c, :], WF2[:, c, :], start=c == 0, stop=False)
                            pe.matmul(PS[:, 6, 0:D], ones[0:1, :], BF2, start=False, stop=True).then_inc(s_dn.sem, 1)

                @block.scalar
                def _(act):
                    with act.Fori(0, NT // 5) as i:
                        for j in range(5):
                            act.wait_ge(s_up.sem, i * 5 + j + 1)
                            for c in range(4):
                                act.activation(gT[:, j, c, :], PS[:, 1 + j, c * P:(c + 1) * P], ACT.Gelu, bias=BF1[:, c:c + 1])\
                                   .then_inc(s_g.sem, 1)

                @block.vector
                def _(dve):
                    def turned(i, j):
                        dve.wait_ge(s_t.sem, i * 5 + j + 2)
                        dve.tensor_copy(hT[:, j, :], PS[:, 0, 0:P]).then_inc(s_tc.sem, 1)

                    with dve.Fori(0, NT // 5) as i:
                        turned(i, 0)
                        for j in range(5):
                            if j < 4:
                                turned(i, j + 1)
                            dve.wait_ge(s_dn.sem, i * 5 + j + 1)
                            at = bass.ds(i * 5 + j, 1)
                            dve.tensor_tensor(HID[:, at, :], H[:, at, :], PS[:, 6:7, 0:D], ALU.add).then_inc(s_add.sem, 1)

            sem = Phase()
            s_v, s_a = sem("l1n_v"), sem("l1n_a")
            norms = Norms(s_v, s_a)
            with sem.block() as block:
                @block.vector
                def _(dve):
                    norms.norm(dve, HID, over(FW, 0, [NT, D]), RWS[:, 2, :], RWS[:, 3, :])
                    s_v.link(dve, dve.tensor_tensor(X[:, :, :], X[:, :, :], HID, ALU.add))
                    norms.norm(dve, X[:, :, :], over(FW, 0, [NT, D]))

                @block.scalar
                def _(act):
                    norms.roots(act)

        def layer2():
            WR = over(XT, 0, [TYPES, D])
            WK2, WK3 = over(FW, 0, [D]), over(FW, 128, [D])
            WQ = over(FW, 256, [D])
            WQT = over(FW, 384, [D])
            KM = over(FW, 512, [TYPES + 4])
            HREL = over(FW, 576, [TYPES])
            HRUL = over(FW, 640, [4])
            BQ = over(FW, 656, [1])
            RID = over(FW, 660, [1], U32, 4)
            RULE = over(FW, 700, [D], F32, 4)
            M = TYPES + 4
            sem = Phase()
            s_l, s_v, s_pe, s_id = sem("l2w_l"), sem("l2w_v"), sem("l2w_pe"), sem("l2w_id")
            s_r, = sem.rows_moved(1)
            with sem.block() as block:
                @block.sync
                def _(sp):
                    s_id.inc(sp.dma_start(RID.bitcast(I32), A["L2_gnn_rule_ids"].rearrange("(p a) -> p a", a=1)), 16)
                    wk = A["L2_gnn_Wk_w"].rearrange("(a f) d -> a f d", a=3)
                    for t, src in ((WR, A["L2_gnn_W_r"].rearrange("r f o -> f r o")), (WQ, A["L2_gnn_Wq_w"][:, :]),
                                   (WCAT[:, 0:D], A["L2_gnn_Wq_w"][:, :]), (WCAT[:, LQ:LQ + D], wk[0]), (WK2, wk[1]), (WK3, wk[2]),
                                   (BIAS[:, 0:D], row_of("L2_gnn_Wq_b")), (BIAS[:, LQ:LQ + D], row_of("L2_gnn_Wk_b")),
                                   (BQ, A["L2_gnn_Wq_b"].rearrange("(p a) -> p a", a=1))):
                        s_l.inc(sp.dma_start(t, src), 16)
                    s_l.wait(sp)

                @block.gpsimd
                def _(pool):
                    pool.wait_ge(s_id.sem, 16)
                    pool.indirect_dma_start(out=RULE, out_offset=None, in_=A["L2_gnn_rule_emb"][:, :],
                                            in_offset=bass.IndirectOffsetOnAxis(ap=RID, axis=0)).then_inc(s_r.sem, 16)
                    s_r.n += 16
                    s_r.wait(pool)

                @block.vector
                def _(dve):
                    v = s_v
                    dve.wait_ge(s_l.sem, 9 * 16)
                    v.link(dve, dve.tensor_reduce(HREL, WR, AX.X, ALU.add))
                    v.link(dve, dve.tensor_scalar(HREL, HREL, 1.0 / D, None, ALU.mult))
                    dve.wait_ge(s_pe.sem, 1)
                    v.inc(dve.tensor_copy(HRUL, PS[:, 0, 0:4]))
                    v.inc(dve.tensor_copy(WQT, PS[:, 1, 0:D]))
                    dve.wait_ge(s_pe.sem, 2)
                    v.inc(dve.tensor_copy(KM[:, 0:TYPES], PS[:, 2, 0:TYPES]))
                    v.inc(dve.tensor_copy(KM[:, TYPES:M], PS[:, 2, TYPES:M]))
                    dve.wait_ge(s_pe.sem, 3)
                    v.inc(dve.tensor_copy(WCAT[:, D:LQ], PS[:, 3, 0:M]))
                    v.inc(dve.tensor_copy(BIAS[:, D:LQ], PS[0:1, 4, 0:M]))

                @block.tensor
                def _(pe):
                    pe.wait_ge(s_l.sem, 9 * 16)
                    s_r.wait(pe)
                    pe.transpose(PS[:, 0, 0:4], RULE, ident[0:4, 0:4])
                    pe.transpose(PS[:, 1, 0:D], WQ, ident[:, :]).then_inc(s_pe.sem, 1)
                    pe.wait_ge(s_v.sem, 4)
                    pe.matmul(PS[:, 2, 0:TYPES], WK2, HREL, start=True, stop=True)
                    pe.matmul(PS[:, 2, TYPES:M], WK3, HRUL, start=True, stop=True).then_inc(s_pe.sem, 1)
                    pe.wait_ge(s_v.sem, 6)
                    pe.matmul(PS[:, 3, 0:M], WQT, KM, start=True, stop=True)
                    pe.matmul(PS[0:1, 4, 0:M], BQ, KM, start=True, stop=True).then_inc(s_pe.sem, 1)

            stages = [over(FW, 1024, [4, 512]), over(FW, 1024 + 2048, [4, 512])]
            xT = over(FW, 5200, [P])
            sem = Phase()
            s_here, s_stored = sem("pr_here"), sem("pr_stored")
            xin = over(FW, 5330, [1, P])
            s_t, s_tc, s_pe, s_c = sem("pr_t"), sem("pr_tc"), sem("pr_pe"), [sem(f"pr_c{h}") for h in range(2)]
            s_st = [sem(f"pr_st{h}") for h in range(2)]
            WRF = WR.rearrange("p r o -> p (r o)")
            target = d_proj[:, :].rearrange("(t p r) o -> t p (r o)", p=P, r=TYPES)
            with sem.block() as block:
                @block.gpsimd
                def _(pool):
                    with pool.Fori(0, NT) as i:
                        pool.wait_ge(s_t.sem, i + 1)
                        pool.tensor_copy(xin, X[:, bass.ds(i, 1), :]).then_inc(s_here.sem, 1)

                @block.tensor
                def _(pe):
                    pe.sem_inc(s_t.sem, 1)
                    with pe.Fori(0, NT) as i:
                        pe.wait_ge(s_here.sem, i + 1)
                        pe.transpose(PS[:, 4, 0:P], xin.rearrange("p a d -> p (a d)"), ident[:, :]).then_inc(s_t.sem, 1)
                        pe.wait_ge(s_tc.sem, i + 1)
                        for n in range(8):
                            pe.wait_ge(s_c[n % 2].sem, i * 4 + n // 2 + 1)
                            pe.matmul(PS[:, n % 2 + 2 * (n // 2 % 2), :], xT, WRF[:, n * 512:(n + 1) * 512],
                                      start=True, stop=True).then_inc(s_pe.sem, 1)

                def copies(eng, copy, h):
                    eng.sem_inc(s_c[h].sem, 2)
                    with eng.Fori(0, NT) as i:
                        if h == 1:
                            eng.wait_ge(s_t.sem, i + 2)
                            copy(xT, PS[:, 4, 0:P]).then_inc(s_tc.sem, 1)
                        for n in range(h, 8, 2):
                            m = n // 4
                            eng.wait_ge(s_stored.sem, i * 2 + m + 1)
                            eng.wait_ge(s_pe.sem, i * 8 + n + 1)
                            copy(stages[m][:, n % 4, :], PS[:, n % 2 + 2 * (n // 2 % 2), :]).then_inc(s_c[h].sem, 1)

                @block.vector
                def _(dve):
                    copies(dve, dve.tensor_copy, 0)

                @block.scalar
                def _(act):
                    copies(act, lambda o, i: act.activation(o, i, ACT.Copy), 1)

                @block.sync
                def _(sp):
                    sp.sem_inc(s_stored.sem, 2)
                    with sp.Fori(0, NT) as i:
                        for m in range(2):
                            for h in range(2):
                                sp.wait_ge(s_c[h].sem, i * 4 + (2 * m + 4))
                            sp.dma_start(target[bass.ds(i, 1), :, m * 2048:(m + 1) * 2048].rearrange("t p o -> (t p) o"),
                                         stages[m].rearrange("p a o -> p (a o)")).then_inc(s_st[m].sem, 16)
                        for m in range(2):
                            sp.wait_ge(s_st[m].sem, i * 16 + 16)
                            sp.sem_inc(s_stored.sem, 1)

            project("l2p", X, LQ + D, LQ, None, [(LQ, LQ + D, d_kn)])
            scores("l2s", "rules", d_kn, D, LQ)
            turn("l2ta", LAF, XT)
            softmax("l2x", cK, whole_k, True, float(D) ** -0.5)
            turn("l2tb", XT, LAF)

            ROW2 = over(FW, 3200, [3, D])
            sem = Phase()
            s_l, s_v = sem("l2m_l"), sem("l2m_v")
            with sem.block() as block:
                @block.vector
                def _(dve):
                    al = ALPHA.rearrange("p (g c) -> p g c", c=C)
                    s_v.link(dve, dve.tensor_reduce(al, LA[:, :, :, 0:4], AX.X, ALU.add))
                    s_v.inc(dve.tensor_scalar(al, al, 0.25, None, ALU.mult))

            aggregate("l2g", dlm, 0, d_proj, False)

            sem = Phase()
            s_l, s_v, s_a = sem("l2f_l"), sem("l2f_v"), sem("l2f_a")
            norms = Norms(s_v, s_a)
            H = ACC[:, :, 0:D]
            with sem.block() as block:
                @block.sync
                def _(sp):
                    for n, w in enumerate(("bias", "ln_gamma", "ln_beta")):
                        s_l.inc(sp.dma_start(ROW2[:, n, :], rows_of("L2_gnn_" + w)), 16)

                @block.vector
                def _(dve):
                    dve.wait_ge(s_l.sem, 48)
                    s_v.link(dve, dve.tensor_tensor(H, H, bc(ROW2[:, 0, :], 1, NT), ALU.add))
                    norms.norm(dve, H, over(FW, 0, [NT, D]), ROW2[:, 1, :], ROW2[:, 2, :])
                    s_v.link(dve, dve.tensor_scalar(H, H, 0.0, None, ALU.max))
                    s_v.link(dve, dve.tensor_tensor(X[:, :, :], X[:, :, :], H, ALU.add))
                    norms.norm(dve, X[:, :, :], over(FW, 0, [NT, D]))

                @block.scalar
                def _(act):
                    norms.roots(act)

        def gatv2(n, src, final):
            tag = f"l3{n}"
            sem = Phase()
            s_l = sem(tag + "w_l")
            with sem.block() as block:
                @block.sync
                def _(sp):
                    s_l.inc(sp.dma_start(WCAT[:, 0:D], A[f"L3_gnn_W{n}_r"][:, :]), 16)
                    s_l.inc(sp.dma_start(WCAT[:, D:2 * D], A[f"L3_gnn_W{n}_l"][:, :]), 16)
                    s_l.inc(sp.dma_start(ATTW, A[f"L3_gnn_att{n}"].rearrange("h c -> (h c)").rearrange("(a m) -> a m", a=1)
                                         .to_broadcast([P, D])), 16)
                    s_l.wait(sp)

            project(tag + "p", src, 2 * D, D, None, [(D, 2 * D, d_xl)], bias=False)

            scores(tag + "s", "gatv2", d_xl, D, D)
            turn(tag + "ta", LAF, XT)
            softmax(tag + "x", cD, whole_d, False)
            turn(tag + "tb", XT, LAF)
            aggregate(tag + "g", dl, 4, None, False, 1e-16)

            ROW1 = over(FW, 3200, [D])
            sem = Phase()
            s_l, s_v, s_a = sem(tag + "f_l"), sem(tag + "f_v"), sem(tag + "f_a")
            norms = Norms(s_v, s_a)
            H = ACC[:, :, 0:D]
            with sem.block() as block:
                @block.sync
                def _(sp):
                    s_l.inc(sp.dma_start(ROW1, rows_of(f"L3_gnn_b{n}")), 16)
                    s_l.wait(sp)
                    if final:
                        sp.wait_ge(s_v.sem, at.final)
                        s_l.inc(sp.dma_start(out[0:(NT - 1) * P, :].rearrange("(t p) d -> p t d", p=P), X[:, 0:NT - 1, :]), 16)
                        s_l.inc(sp.dma_start(out[(NT - 1) * P:N, :], X[0:NLAST, NT - 1, :]), 16)
                        s_l.wait(sp)

                at.final = 11

                @block.vector
                def _(dve):
                    dve.wait_ge(s_l.sem, 16)
                    s_v.link(dve, dve.tensor_tensor(H, H, bc(ROW1, 1, NT), ALU.add))
                    if final:
                        s_v.link(dve, dve.tensor_scalar(H, H, 0.0, None, ALU.max))
                        s_v.link(dve, dve.tensor_tensor(X[:, :, :], X[:, :, :], H, ALU.add))
                        norms.norm(dve, X[:, :, :], over(FW, 0, [NT, D]))
                        assert s_v.n == at.final
                    else:
                        s_v.inc(dve.tensor_scalar(HID, H, 0.0, None, ALU.max))

                @block.scalar
                def _(act):
                    norms.roots(act)

        constants()
        records_by_src()
        by_source = rank("ss", KEPT, ECOL, 7, 5, NT, d_slist, sbt, 1)
        by_source.start()
        records_by_dst()
        by_type = rank("s0", EARLY, ACOL, 0, 6, TYPES + 1, d_pass[0], None, 0, beside=4)
        layer0_tables()
        by_source.rest("ssr")
        source_tables()
        by_type.start()
        by_type.rest("s0r")
        load_records("r0", d_pass[0], EARLY)
        by_low = rank("s1", EARLY, ACOL, 6, 6, 64, d_pass[1], None, 0, later=True)
        half = EG - NT - 1
        layer0_edges("l0a", 0, half, by_low, 2)
        by_low.start()
        by_low.rest("s1r")
        load_records("r1", d_pass[1], EARLY)
        by_high = rank("s2", EARLY, ACOL, 12, 6, 2 * NT, d_list, bt, 2, later=True)
        layer0_edges("l0b", half, EG, by_high, 1)
        by_high.start()
        layer0_nodes()
        layer1_tables()
        by_high.rest("s2r")
        LIST = over(XT, 0, [C, G, 4], I32)
        read_list("kl", d_list, over(XT, 0, [G * C, 4], I32))
        keys("kk", LIST, 0, True)
        turn("kt", TT, LAF)
        flags("kf", cK, whole_k)
        keys("dk", LIST, 6, False)
        turn("dt", TT, LAF)
        flags("df", cD, whole_d)
        layer1()
        layer2()
        gatv2(1, X, False)
        gatv2(2, HID, True)


_OUTS = [((N, D), "float32")]


def kernel(**inputs):
    import numpy as np
    import concourse.bacc as bacc
    from concourse.bass_utils import run_bass_kernel_spmd

    nc = bacc.Bacc("TRN2", target_bir_lowering=False, num_devices=1)
    arrays, aps = {}, {}
    for name, a in inputs.items():
        a = np.ascontiguousarray(a)
        arrays[f"in_{name}"] = a
        aps[name] = nc.dram_tensor(f"in_{name}", a.shape, mybir.dt.from_np(a.dtype), kind="ExternalInput").ap()
    out = nc.dram_tensor("out_x", (N, D), F32, kind="ExternalOutput").ap()
    gnn_kernel(nc, aps, out)
    r = run_bass_kernel_spmd(nc, [arrays], core_ids=[0])
    return r.results[0]["out_x"]
```
